# Optimizing a Trainium2 kernel written in Bass

```python
import numpy as np
import jax
import jax.numpy as jnp

def _softmax(x, axis=-1):
    return jax.nn.softmax(x, axis=axis)

def _gelu(x):
    return jax.nn.gelu(x, approximate=True)

def _silu(x):
    return jax.nn.silu(x)

def _sigmoid(x):
    return jax.nn.sigmoid(x)

def _layernorm(x, axis=-1, eps=1e-05):
    m = jnp.mean(x, axis=axis, keepdims=True)
    v = jnp.var(x, axis=axis, keepdims=True)
    return (x - m) / jnp.sqrt(v + eps)

def _scatter_add(tgt, idx, src, axis=0):
    return tgt.at[idx].add(src)

def _segment_sum(src, seg, n):
    return jax.ops.segment_sum(src, seg, n)
kernel_name = 'mk_decoder_preln_d4_seqx_r8_c680db'

def setup_inputs(seed: int=0):
    np.random.seed(seed)
    _w = jnp.asarray

    def _rec_inputs():
        import jax
        import jax.numpy as jnp
        _rk = jax.random.key(seed)
        x = -0.0003929 + 0.9999 * jax.random.normal(jax.random.fold_in(_rk, 1), (4, 256, 128), jnp.float32)
        _lenS = 256 - jax.random.randint(jax.random.fold_in(_rk, 7), (4,), 0, max(1, 256 // 4) + 1, jnp.int32)
        _lenS2 = 512 - jax.random.randint(jax.random.fold_in(_rk, 8), (4,), 0, max(1, 512 // 4) + 1, jnp.int32)
        _ctx_1024P = jax.random.normal(jax.random.fold_in(_rk, 11), (4, 16, 128), jnp.float32)
        _ctx_1024c = jax.random.dirichlet(jax.random.fold_in(_rk, 511), 0.3 * jnp.ones((16,), jnp.float32), (4, 512))
        _ctx_1024t = jnp.einsum('bsk,bkd->bsd', _ctx_1024c, _ctx_1024P)
        _ctx_1024t = _ctx_1024t * jax.lax.rsqrt(jnp.mean(jnp.square(_ctx_1024t)) + 1e-12) * 0.953939
        ctx_1024 = -0.000514642 + 1.00011 * (_ctx_1024t + 0.3 * jax.random.normal(jax.random.fold_in(_rk, 611), (4, 512, 128), jnp.float32))
        _validS = jnp.arange(256)[None, :] < _lenS[:, None]
        _validS2 = jnp.arange(512)[None, :] < _lenS2[:, None]
        _causal = jnp.tril(jnp.ones((256, 256), dtype=bool))
        mask_BxS2_bk0 = jnp.logical_not(jnp.broadcast_to(_validS2[:, :], (4, 512)))
        mask_BxS2_bf1 = jnp.ones((4, 512), dtype=bool)
        mask_1x1xSxS2_if1 = jnp.where(jnp.ones((1, 1, 256, 512), dtype=bool), 1, 0).astype(jnp.int32)
        return (x, ctx_1024, mask_BxS2_bk0, mask_BxS2_bf1, mask_1x1xSxS2_if1)
    x, ctx_1024, mask_BxS2_bk0, mask_BxS2_bf1, mask_1x1xSxS2_if1 = _rec_inputs()

    def _L0_attn_setup():
        import jax, jax.numpy as jnp
        import numpy as np
        DIM = 128
        HEADS = 16
        HEAD_DIM = DIM // HEADS
        key = jax.random.key(seed)
        ks = jax.random.split(key, 5)
        x = jax.random.normal(ks[0], (4, 256, DIM), dtype=jnp.float32)
        s = DIM ** (-0.5)
        W_qkv = jax.random.normal(ks[1], (DIM, 3 * DIM), dtype=jnp.float32) * s
        b_qkv = jnp.zeros((3 * DIM,), dtype=jnp.float32)
        W_proj = jax.random.normal(ks[2], (DIM, DIM), dtype=jnp.float32) * s
        b_proj = jnp.zeros((DIM,), dtype=jnp.float32)
        return {'x': x, 'W_qkv': W_qkv, 'b_qkv': b_qkv, 'W_proj': W_proj, 'b_proj': b_proj}
    _L0_attn_all = _L0_attn_setup()
    _L0_attn_in = {k: v for k, v in _L0_attn_all.items() if k in ('W_qkv', 'b_qkv', 'W_proj', 'b_proj')}
    del _L0_attn_all

    def _L0_xattn_setup():
        import jax, jax.numpy as jnp
        import numpy as np
        DIM = 128
        HEADS = 16
        HEAD_DIM = DIM // HEADS
        B, N, S = (4, 512, 64)
        key = jax.random.key(seed)
        ks = jax.random.split(key, 9)
        scale = DIM ** (-0.5)
        return {'x': jax.random.normal(ks[0], (B, N, DIM), dtype=jnp.float32), 'context': jax.random.normal(ks[1], (B, S, DIM), dtype=jnp.float32), 'context_mask': jax.random.uniform(ks[2], (B, S)) < 0.2, 'q_w': jax.random.normal(ks[3], (DIM, DIM), dtype=jnp.float32) * scale, 'q_b': jnp.zeros((DIM,), dtype=jnp.float32), 'kv_w': jax.random.normal(ks[4], (DIM, 2 * DIM), dtype=jnp.float32) * scale, 'kv_b': jnp.zeros((2 * DIM,), dtype=jnp.float32), 'proj_w': jax.random.normal(ks[5], (DIM, DIM), dtype=jnp.float32) * scale, 'proj_b': jnp.zeros((DIM,), dtype=jnp.float32)}
    _L0_xattn_all = _L0_xattn_setup()
    _L0_xattn_in = {k: v for k, v in _L0_xattn_all.items() if k in ('q_w', 'q_b', 'kv_w', 'kv_b', 'proj_w', 'proj_b')}
    del _L0_xattn_all

    def _L0_ffn_setup():
        import jax, jax.numpy as jnp
        import numpy as np
        H = 128
        I = 256
        E = 32
        B, S = (4, 256)

        def _grouped_mm(a, w, group_sizes):
            return jax.lax.ragged_dot(a, w, group_sizes)

        def _swiglu(x, gw, uw, dw):
            return jax.nn.silu(x @ gw) * (x @ uw) @ dw
        key = jax.random.key(seed)
        ks = jax.random.split(key, 8)
        scale = 0.02
        inp = {'hidden_states': jax.random.normal(ks[0], (B, S, H), dtype=jnp.float32), 'gate_w': jax.random.normal(ks[1], (H, E), dtype=jnp.float32) * scale, 'shared_gate_w': jax.random.normal(ks[2], (H, I), dtype=jnp.float32) * scale, 'shared_up_w': jax.random.normal(ks[3], (H, I), dtype=jnp.float32) * scale, 'shared_down_w': jax.random.normal(ks[4], (I, H), dtype=jnp.float32) * scale, 'routed_gate_w': jax.random.normal(ks[5], (E, H, I), dtype=jnp.float32) * scale, 'routed_up_w': jax.random.normal(ks[6], (E, H, I), dtype=jnp.float32) * scale, 'routed_down_w': jax.random.normal(ks[7], (E, I, H), dtype=jnp.float32) * scale}
        return inp
    _L0_ffn_all = _L0_ffn_setup()
    _L0_ffn_in = {k: v for k, v in _L0_ffn_all.items() if k in ('gate_w', 'shared_gate_w', 'shared_up_w', 'shared_down_w', 'routed_gate_w', 'routed_up_w', 'routed_down_w')}
    del _L0_ffn_all

    def _L1_attn_setup():
        import jax, jax.numpy as jnp
        import numpy as np
        B, T, D, H = (1, 512, 128, 16)
        DK = D // H
        SCALE = 1.0 / float(np.sqrt(DK))
        NEG = -1000000000.0
        key = jax.random.key(seed)
        k1, k2, k3 = jax.random.split(key, 3)
        x = jax.random.normal(k1, (B, T, D), dtype=jnp.float32)
        Wqkv = jax.random.normal(k2, (3 * D, D), dtype=jnp.float32) * 0.02
        Wout = jax.random.normal(k3, (D, D), dtype=jnp.float32) * 0.02
        return {'x': x, 'Wqkv': Wqkv, 'Wout': Wout}
    _L1_attn_all = _L1_attn_setup()
    _L1_attn_in = {k: v for k, v in _L1_attn_all.items() if k in ('Wqkv', 'Wout')}
    del _L1_attn_all

    def _L1_xattn_setup():
        import jax, jax.numpy as jnp
        import numpy as np
        E = 128
        H = 16
        D = E // H
        key = jax.random.key(seed)
        ks = jax.random.split(key, 12)
        B, Tq, Tk = (2, 128, 1024)
        s = 0.02
        return {'hidden_states': jax.random.normal(ks[0], (B, Tq, E), jnp.float32), 'key_value_states': jax.random.normal(ks[1], (B, Tk, E), jnp.float32), 'Wq': jax.random.normal(ks[2], (E, E), jnp.float32) * s, 'bq': jnp.zeros((E,), jnp.float32), 'Wk': jax.random.normal(ks[3], (E, E), jnp.float32) * s, 'bk': jnp.zeros((E,), jnp.float32), 'Wv': jax.random.normal(ks[4], (E, E), jnp.float32) * s, 'bv': jnp.zeros((E,), jnp.float32), 'Wo': jax.random.normal(ks[5], (E, E), jnp.float32) * s, 'bo': jnp.zeros((E,), jnp.float32), 'stride': 16}
    _L1_xattn_all = _L1_xattn_setup()
    _L1_xattn_in = {k: v for k, v in _L1_xattn_all.items() if k in ('Wq', 'bq', 'Wk', 'bk', 'Wv', 'bv', 'Wo', 'bo')}
    del _L1_xattn_all

    def _L1_ffn_setup():
        import jax, jax.numpy as jnp
        import numpy as np
        NUM_EXPERTS = 8
        TOP_K = 2
        DIM = 128
        HIDDEN = 512
        B, S = (2, 128)
        key = jax.random.key(seed)
        k_x, k_g, k_1, k_2, k_3 = jax.random.split(key, 5)
        s_d = 1.0 / np.sqrt(DIM)
        s_h = 1.0 / np.sqrt(HIDDEN)
        return {'x': jax.random.normal(k_x, (B, S, DIM), dtype=jnp.float32), 'gate_w': jax.random.normal(k_g, (NUM_EXPERTS, DIM), dtype=jnp.float32) * s_d, 'w1': jax.random.normal(k_1, (NUM_EXPERTS, HIDDEN, DIM), dtype=jnp.float32) * s_d, 'w2': jax.random.normal(k_2, (NUM_EXPERTS, DIM, HIDDEN), dtype=jnp.float32) * s_h, 'w3': jax.random.normal(k_3, (NUM_EXPERTS, HIDDEN, DIM), dtype=jnp.float32) * s_d}
    _L1_ffn_all = _L1_ffn_setup()
    _L1_ffn_in = {k: v for k, v in _L1_ffn_all.items() if k in ('gate_w', 'w1', 'w2', 'w3')}
    del _L1_ffn_all

    def _L2_attn_setup():
        import jax, jax.numpy as jnp
        import numpy as np
        B, L, E, H = (8, 256, 128, 16)
        D = E // H
        EPS = 1e-06
        key = jax.random.key(seed)
        ks = jax.random.split(key, 9)
        s = 1.0 / np.sqrt(E)

        def lin_w(k):
            return jax.random.uniform(k, (E, E), jnp.float32, -s, s)

        def lin_b(k):
            return jax.random.uniform(k, (E,), jnp.float32, -s, s)
        return {'query': jax.random.normal(ks[0], (B, L, E), jnp.float32), 'Wq': lin_w(ks[1]), 'bq': lin_b(ks[2]), 'Wk': lin_w(ks[3]), 'bk': lin_b(ks[4]), 'Wv': lin_w(ks[5]), 'bv': lin_b(ks[6]), 'Wo': lin_w(ks[7]), 'bo': lin_b(ks[8])}
    _L2_attn_all = _L2_attn_setup()
    _L2_attn_in = {k: v for k, v in _L2_attn_all.items() if k in ('Wq', 'bq', 'Wk', 'bk', 'Wv', 'bv', 'Wo', 'bo')}
    del _L2_attn_all

    def _L2_xattn_setup():
        import jax, jax.numpy as jnp
        import numpy as np
        DIM = 128
        HEADS = 16
        DIM_HEAD = 64
        INNER = HEADS * DIM_HEAD
        B, F, Q = (16, 512, 64)
        EPS = 1e-05
        SCALE = DIM_HEAD ** (-0.5)

        def _layernorm(x, gamma, beta):
            mu = jnp.mean(x, axis=-1, keepdims=True)
            var = jnp.var(x, axis=-1, keepdims=True)
            return (x - mu) * jax.lax.rsqrt(var + EPS) * gamma + beta
        key = jax.random.key(seed)
        ks = jax.random.split(key, 8)
        features = jax.random.normal(ks[0], (B, F, DIM), dtype=jnp.float32)
        masks = jnp.ones((B, F), dtype=bool)
        latents = jax.random.normal(ks[1], (B, Q, DIM), dtype=jnp.float32)
        Wq = jax.random.normal(ks[2], (DIM, INNER), dtype=jnp.float32) / np.sqrt(DIM)
        Wk = jax.random.normal(ks[3], (DIM, INNER), dtype=jnp.float32) / np.sqrt(DIM)
        Wv = jax.random.normal(ks[4], (DIM, INNER), dtype=jnp.float32) / np.sqrt(DIM)
        Wo = jax.random.normal(ks[5], (INNER, DIM), dtype=jnp.float32) / np.sqrt(INNER)
        gm = jnp.ones((DIM,), jnp.float32)
        bm = jnp.zeros((DIM,), jnp.float32)
        gl = jnp.ones((DIM,), jnp.float32)
        bl = jnp.zeros((DIM,), jnp.float32)
        return {'features': features, 'masks': masks, 'latents': latents, 'gm': gm, 'bm': bm, 'gl': gl, 'bl': bl, 'Wq': Wq, 'Wk': Wk, 'Wv': Wv, 'Wo': Wo}
    _L2_xattn_all = _L2_xattn_setup()
    _L2_xattn_in = {k: v for k, v in _L2_xattn_all.items() if k in ('gm', 'bm', 'gl', 'bl', 'Wq', 'Wk', 'Wv', 'Wo')}
    del _L2_xattn_all

    def _L2_ffn_setup():
        import jax, jax.numpy as jnp
        import numpy as np
        TEMPERATURE = 1.0
        TOPK = 2
        key = jax.random.key(seed)
        ks = jax.random.split(key, 6)
        S, B, H, F, E = (256, 4, 128, 512, 8)
        x = jax.random.normal(ks[0], (S, B, H), dtype=jnp.float32)
        gate_w = jax.random.normal(ks[1], (E, H), dtype=jnp.float32) * (1.0 / np.sqrt(H))
        w1 = jax.random.normal(ks[2], (E, H, F), dtype=jnp.float32) * (1.0 / np.sqrt(H))
        b1 = jnp.zeros((E, F), dtype=jnp.float32)
        w2 = jax.random.normal(ks[3], (E, F, H), dtype=jnp.float32) * (1.0 / np.sqrt(F))
        b2 = jnp.zeros((E, H), dtype=jnp.float32)
        return {'x': x, 'gate_w': gate_w, 'w1': w1, 'b1': b1, 'w2': w2, 'b2': b2}
    _L2_ffn_all = _L2_ffn_setup()
    _L2_ffn_in = {k: v for k, v in _L2_ffn_all.items() if k in ('gate_w', 'w1', 'b1', 'w2', 'b2')}
    del _L2_ffn_all

    def _L3_attn_setup():
        import jax, jax.numpy as jnp
        import numpy as np
        D_MODEL = 128
        NUM_HEADS = 16
        HEAD_DIM = D_MODEL // NUM_HEADS
        D_LATENT = 32
        B, T = (4, 256)
        key = jax.random.key(seed)
        ks = jax.random.split(key, 8)
        s_in = 1.0 / np.sqrt(D_MODEL)
        s_lat = 1.0 / np.sqrt(D_LATENT)
        x = jax.random.normal(ks[0], (B, T, D_MODEL), dtype=jnp.float32)
        mask = jnp.tril(jnp.ones((T, T), dtype=bool))[None, None, :, :]
        Wq_down = jax.random.uniform(ks[1], (D_LATENT, D_MODEL), jnp.float32, -s_in, s_in)
        Wkv_down = jax.random.uniform(ks[2], (D_LATENT, D_MODEL), jnp.float32, -s_in, s_in)
        Wq_up = jax.random.uniform(ks[3], (D_MODEL, D_LATENT), jnp.float32, -s_lat, s_lat)
        Wk_up = jax.random.uniform(ks[4], (D_MODEL, D_LATENT), jnp.float32, -s_lat, s_lat)
        Wv_up = jax.random.uniform(ks[5], (D_MODEL, D_LATENT), jnp.float32, -s_lat, s_lat)
        Wout = jax.random.uniform(ks[6], (D_MODEL, D_MODEL), jnp.float32, -s_in, s_in)
        return {'x': x, 'mask': mask, 'Wq_down': Wq_down, 'Wkv_down': Wkv_down, 'Wq_up': Wq_up, 'Wk_up': Wk_up, 'Wv_up': Wv_up, 'Wout': Wout}
    _L3_attn_all = _L3_attn_setup()
    _L3_attn_in = {k: v for k, v in _L3_attn_all.items() if k in ('mask', 'Wq_down', 'Wkv_down', 'Wq_up', 'Wk_up', 'Wv_up', 'Wout')}
    del _L3_attn_all

    def _L3_xattn_setup():
        import jax, jax.numpy as jnp
        import numpy as np
        D_MODEL = 128
        H = 16
        D_K = D_MODEL // H
        B, S = (2, 256)
        NEG = -1000000000.0

        def _split_heads(x):
            b, s, _ = x.shape
            return x.reshape(b, s, H, D_K).transpose(0, 2, 1, 3)
        key = jax.random.key(seed)
        ks = jax.random.split(key, 8)
        scale = 1.0 / np.sqrt(D_MODEL)
        return {'q': jax.random.normal(ks[0], (B, S, D_MODEL), jnp.float32), 'k': jax.random.normal(ks[1], (B, S, D_MODEL), jnp.float32), 'v': jax.random.normal(ks[2], (B, S, D_MODEL), jnp.float32), 'mask': jnp.ones((1, 1, S, S), jnp.int32), 'Wq': jax.random.normal(ks[3], (D_MODEL, D_MODEL), jnp.float32) * scale, 'bq': jnp.zeros((D_MODEL,), jnp.float32), 'Wk': jax.random.normal(ks[4], (D_MODEL, D_MODEL), jnp.float32) * scale, 'bk': jnp.zeros((D_MODEL,), jnp.float32), 'Wv': jax.random.normal(ks[5], (D_MODEL, D_MODEL), jnp.float32) * scale, 'bv': jnp.zeros((D_MODEL,), jnp.float32), 'Wo': jax.random.normal(ks[6], (D_MODEL, D_MODEL), jnp.float32) * scale, 'bo': jnp.zeros((D_MODEL,), jnp.float32)}
    _L3_xattn_all = _L3_xattn_setup()
    _L3_xattn_in = {k: v for k, v in _L3_xattn_all.items() if k in ('Wq', 'bq', 'Wk', 'bk', 'Wv', 'bv', 'Wo', 'bo')}
    del _L3_xattn_all

    def _L3_ffn_setup():
        import jax, jax.numpy as jnp
        import numpy as np
        EMBED_DIM = 128
        HIDDEN = 4 * EMBED_DIM
        BATCH, SEQ = (4, 512)
        EPS = 1e-05

        def _quant_weight(w):
            s = jnp.clip(jnp.mean(jnp.abs(w)), EPS, None)
            wq = jnp.clip(jnp.round(w / s), -1.0, 1.0) * s
            return w + jax.lax.stop_gradient(wq - w)

        def _quant_act(x):
            scale = 127.0 / jnp.clip(jnp.max(jnp.abs(x), axis=-1, keepdims=True), EPS, None)
            xq = jnp.clip(jnp.round(x * scale), -128.0, 127.0) / scale
            return x + jax.lax.stop_gradient(xq - x)

        def _bitlinear(x, w):
            return jnp.einsum('bsi,oi->bso', _quant_act(x), _quant_weight(w))
        key = jax.random.key(seed)
        k1, k2, k3 = jax.random.split(key, 3)
        x = jax.random.normal(k1, (BATCH, SEQ, EMBED_DIM), dtype=jnp.float32)
        w1 = jax.random.normal(k2, (HIDDEN, EMBED_DIM), dtype=jnp.float32) * (1.0 / np.sqrt(EMBED_DIM))
        w2 = jax.random.normal(k3, (EMBED_DIM, HIDDEN), dtype=jnp.float32) * (1.0 / np.sqrt(HIDDEN))
        return {'x': x, 'w1': w1, 'w2': w2}
    _L3_ffn_all = _L3_ffn_setup()
    _L3_ffn_in = {k: v for k, v in _L3_ffn_all.items() if k in ('w1', 'w2')}
    del _L3_ffn_all
    return {'x': x, 'ctx_1024': ctx_1024, 'mask_BxS2_bk0': mask_BxS2_bk0, 'mask_BxS2_bf1': mask_BxS2_bf1, 'mask_1x1xSxS2_if1': mask_1x1xSxS2_if1, 'L0_attn_W_qkv': _L0_attn_in['W_qkv'], 'L0_attn_b_qkv': _L0_attn_in['b_qkv'], 'L0_attn_W_proj': _L0_attn_in['W_proj'], 'L0_attn_b_proj': _L0_attn_in['b_proj'], 'L0_xattn_q_w': _L0_xattn_in['q_w'], 'L0_xattn_q_b': _L0_xattn_in['q_b'], 'L0_xattn_kv_w': _L0_xattn_in['kv_w'], 'L0_xattn_kv_b': _L0_xattn_in['kv_b'], 'L0_xattn_proj_w': _L0_xattn_in['proj_w'], 'L0_xattn_proj_b': _L0_xattn_in['proj_b'], 'L0_ffn_gate_w': _L0_ffn_in['gate_w'], 'L0_ffn_shared_gate_w': _L0_ffn_in['shared_gate_w'], 'L0_ffn_shared_up_w': _L0_ffn_in['shared_up_w'], 'L0_ffn_shared_down_w': _L0_ffn_in['shared_down_w'], 'L0_ffn_routed_gate_w': _L0_ffn_in['routed_gate_w'], 'L0_ffn_routed_up_w': _L0_ffn_in['routed_up_w'], 'L0_ffn_routed_down_w': _L0_ffn_in['routed_down_w'], 'L1_attn_Wqkv': _L1_attn_in['Wqkv'], 'L1_attn_Wout': _L1_attn_in['Wout'], 'L1_xattn_Wq': _L1_xattn_in['Wq'], 'L1_xattn_bq': _L1_xattn_in['bq'], 'L1_xattn_Wk': _L1_xattn_in['Wk'], 'L1_xattn_bk': _L1_xattn_in['bk'], 'L1_xattn_Wv': _L1_xattn_in['Wv'], 'L1_xattn_bv': _L1_xattn_in['bv'], 'L1_xattn_Wo': _L1_xattn_in['Wo'], 'L1_xattn_bo': _L1_xattn_in['bo'], 'L1_ffn_gate_w': _L1_ffn_in['gate_w'], 'L1_ffn_w1': _L1_ffn_in['w1'], 'L1_ffn_w2': _L1_ffn_in['w2'], 'L1_ffn_w3': _L1_ffn_in['w3'], 'L2_attn_Wq': _L2_attn_in['Wq'], 'L2_attn_bq': _L2_attn_in['bq'], 'L2_attn_Wk': _L2_attn_in['Wk'], 'L2_attn_bk': _L2_attn_in['bk'], 'L2_attn_Wv': _L2_attn_in['Wv'], 'L2_attn_bv': _L2_attn_in['bv'], 'L2_attn_Wo': _L2_attn_in['Wo'], 'L2_attn_bo': _L2_attn_in['bo'], 'L2_xattn_gm': _L2_xattn_in['gm'], 'L2_xattn_bm': _L2_xattn_in['bm'], 'L2_xattn_gl': _L2_xattn_in['gl'], 'L2_xattn_bl': _L2_xattn_in['bl'], 'L2_xattn_Wq': _L2_xattn_in['Wq'], 'L2_xattn_Wk': _L2_xattn_in['Wk'], 'L2_xattn_Wv': _L2_xattn_in['Wv'], 'L2_xattn_Wo': _L2_xattn_in['Wo'], 'L2_ffn_gate_w': _L2_ffn_in['gate_w'], 'L2_ffn_w1': _L2_ffn_in['w1'], 'L2_ffn_b1': _L2_ffn_in['b1'], 'L2_ffn_w2': _L2_ffn_in['w2'], 'L2_ffn_b2': _L2_ffn_in['b2'], 'L3_attn_mask': _L3_attn_in['mask'], 'L3_attn_Wq_down': _L3_attn_in['Wq_down'], 'L3_attn_Wkv_down': _L3_attn_in['Wkv_down'], 'L3_attn_Wq_up': _L3_attn_in['Wq_up'], 'L3_attn_Wk_up': _L3_attn_in['Wk_up'], 'L3_attn_Wv_up': _L3_attn_in['Wv_up'], 'L3_attn_Wout': _L3_attn_in['Wout'], 'L3_xattn_Wq': _L3_xattn_in['Wq'], 'L3_xattn_bq': _L3_xattn_in['bq'], 'L3_xattn_Wk': _L3_xattn_in['Wk'], 'L3_xattn_bk': _L3_xattn_in['bk'], 'L3_xattn_Wv': _L3_xattn_in['Wv'], 'L3_xattn_bv': _L3_xattn_in['bv'], 'L3_xattn_Wo': _L3_xattn_in['Wo'], 'L3_xattn_bo': _L3_xattn_in['bo'], 'L3_ffn_w1': _L3_ffn_in['w1'], 'L3_ffn_w2': _L3_ffn_in['w2']}

def reference(x, ctx_1024, mask_BxS2_bk0, mask_BxS2_bf1, mask_1x1xSxS2_if1, L0_attn_W_qkv, L0_attn_b_qkv, L0_attn_W_proj, L0_attn_b_proj, L0_xattn_q_w, L0_xattn_q_b, L0_xattn_kv_w, L0_xattn_kv_b, L0_xattn_proj_w, L0_xattn_proj_b, L0_ffn_gate_w, L0_ffn_shared_gate_w, L0_ffn_shared_up_w, L0_ffn_shared_down_w, L0_ffn_routed_gate_w, L0_ffn_routed_up_w, L0_ffn_routed_down_w, L1_attn_Wqkv, L1_attn_Wout, L1_xattn_Wq, L1_xattn_bq, L1_xattn_Wk, L1_xattn_bk, L1_xattn_Wv, L1_xattn_bv, L1_xattn_Wo, L1_xattn_bo, L1_ffn_gate_w, L1_ffn_w1, L1_ffn_w2, L1_ffn_w3, L2_attn_Wq, L2_attn_bq, L2_attn_Wk, L2_attn_bk, L2_attn_Wv, L2_attn_bv, L2_attn_Wo, L2_attn_bo, L2_xattn_gm, L2_xattn_bm, L2_xattn_gl, L2_xattn_bl, L2_xattn_Wq, L2_xattn_Wk, L2_xattn_Wv, L2_xattn_Wo, L2_ffn_gate_w, L2_ffn_w1, L2_ffn_b1, L2_ffn_w2, L2_ffn_b2, L3_attn_mask, L3_attn_Wq_down, L3_attn_Wkv_down, L3_attn_Wq_up, L3_attn_Wk_up, L3_attn_Wv_up, L3_attn_Wout, L3_xattn_Wq, L3_xattn_bq, L3_xattn_Wk, L3_xattn_bk, L3_xattn_Wv, L3_xattn_bv, L3_xattn_Wo, L3_xattn_bo, L3_ffn_w1, L3_ffn_w2):
    import jax
    import jax.numpy as jnp

    def _L0_attn_ref(x, W_qkv, b_qkv, W_proj, b_proj):
        import jax, jax.numpy as jnp
        import numpy as np
        DIM = 128
        HEADS = 16
        HEAD_DIM = DIM // HEADS
        B, S, D = x.shape
        scale = HEAD_DIM ** (-0.5)
        qkv = x @ W_qkv + b_qkv
        q, k, v = jnp.split(qkv, 3, axis=-1)

        def heads(t):
            return t.reshape(B, S, HEADS, HEAD_DIM).transpose(0, 2, 1, 3)
        q, k, v = (heads(q), heads(k), heads(v))
        attn = jnp.einsum('bhqd,bhkd->bhqk', q, k) * scale
        attn = jax.nn.softmax(attn, axis=-1)
        out = jnp.einsum('bhqk,bhkd->bhqd', attn, v)
        out = out.transpose(0, 2, 1, 3).reshape(B, S, D)
        return out @ W_proj + b_proj

    def _L0_xattn_ref(x, context, context_mask, q_w, q_b, kv_w, kv_b, proj_w, proj_b):
        import jax, jax.numpy as jnp
        import numpy as np
        DIM = 128
        HEADS = 16
        HEAD_DIM = DIM // HEADS
        B, N, S = (4, 512, 64)
        b, n, c = x.shape
        s = context.shape[1]
        h, d = (HEADS, HEAD_DIM)
        scale = d ** (-0.5)
        q = (x @ q_w + q_b).reshape(b, n, h, d)
        kv = (context @ kv_w + kv_b).reshape(b, s, 2, h, d)
        k = kv[:, :, 0]
        v = kv[:, :, 1]
        attn = jnp.einsum('bnhd,bshd->bhns', q, k) * scale
        attn = jnp.where(context_mask[:, None, None, :], -jnp.inf, attn)
        attn = jax.nn.softmax(attn, axis=-1)
        out = jnp.einsum('bhns,bshd->bnhd', attn, v).reshape(b, n, c)
        return out @ proj_w + proj_b

    def _L0_ffn_ref(hidden_states, gate_w, shared_gate_w, shared_up_w, shared_down_w, routed_gate_w, routed_up_w, routed_down_w):
        import jax, jax.numpy as jnp
        import numpy as np
        H = 128
        I = 256
        E = 32
        B, S = (4, 256)

        def _grouped_mm(a, w, group_sizes):
            return jax.lax.ragged_dot(a, w, group_sizes)

        def _swiglu(x, gw, uw, dw):
            return jax.nn.silu(x @ gw) * (x @ uw) @ dw
        b, s, h = hidden_states.shape
        x = hidden_states.reshape(-1, h)
        shared_out = _swiglu(x, shared_gate_w, shared_up_w, shared_down_w)
        logits = x @ gate_w
        topk_ids = jnp.argmax(logits, axis=-1)
        topk_val = jnp.max(logits, axis=-1)
        scores = jax.nn.sigmoid(topk_val)[:, None]
        xs = x * scores
        tokens_per_expert = jnp.zeros((E,), jnp.int32).at[topk_ids].add(1)
        order = jnp.argsort(topk_ids)
        sorted_x = xs[order]
        g = _grouped_mm(sorted_x, routed_gate_w, tokens_per_expert)
        u = _grouped_mm(sorted_x, routed_up_w, tokens_per_expert)
        d = _grouped_mm(jax.nn.silu(g) * u, routed_down_w, tokens_per_expert)
        inv = jnp.argsort(order)
        routed_out = d[inv]
        return (shared_out + routed_out).reshape(b, s, h)

    def _L1_attn_ref(x, Wqkv, Wout):
        import jax, jax.numpy as jnp
        import numpy as np
        B, T, D, H = (1, 512, 128, 16)
        DK = D // H
        SCALE = 1.0 / float(np.sqrt(DK))
        NEG = -1000000000.0
        b, t, d = x.shape
        qkv = jnp.einsum('btd,ed->bte', x, Wqkv)
        qkv = qkv.reshape(b, t, 3, H, DK).transpose(2, 0, 3, 1, 4)
        q, k, v = (qkv[0], qkv[1], qkv[2])
        scores = jnp.einsum('bhtd,bhsd->bhts', q, k) * SCALE
        scores = jnp.clip(scores, -10.0, 10.0)
        mask = jnp.triu(jnp.full((t, t), NEG, dtype=scores.dtype), k=1)
        scores = scores + mask[None, None, :, :]
        attn = jax.nn.softmax(scores, axis=-1)
        out = jnp.einsum('bhts,bhsd->bhtd', attn, v)
        out = out.transpose(0, 2, 1, 3).reshape(b, t, d)
        return jnp.einsum('btd,ed->bte', out, Wout)

    def _L1_xattn_ref(hidden_states, key_value_states, Wq, bq, Wk, bk, Wv, bv, Wo, bo, stride):
        import jax, jax.numpy as jnp
        import numpy as np
        E = 128
        H = 16
        D = E // H
        B, Tq, _ = hidden_states.shape
        Tk = key_value_states.shape[1]
        scaling = D ** (-0.5)
        Q = (hidden_states @ Wq.T + bq).reshape(B, Tq, H, D).transpose(0, 2, 1, 3)
        K = (key_value_states @ Wk.T + bk).reshape(B, Tk, H, D).transpose(0, 2, 1, 3)
        V = (key_value_states @ Wv.T + bv).reshape(B, Tk, H, D).transpose(0, 2, 1, 3)
        m = Tk // stride
        idx = jnp.arange(H)[:, None] + stride * jnp.arange(m)[None, :]
        gather = idx[None, :, :, None]
        Kg = jnp.take_along_axis(K, gather, axis=2)
        Vg = jnp.take_along_axis(V, gather, axis=2)
        scores = jnp.einsum('bhqd,bhkd->bhqk', Q, Kg) * scaling
        attn = jax.nn.softmax(scores, axis=-1)
        out = jnp.einsum('bhqk,bhkd->bhqd', attn, Vg)
        out = out.transpose(0, 2, 1, 3).reshape(B, Tq, E)
        return out @ Wo.T + bo

    def _L1_ffn_ref(x, gate_w, w1, w2, w3):
        import jax, jax.numpy as jnp
        import numpy as np
        NUM_EXPERTS = 8
        TOP_K = 2
        DIM = 128
        HIDDEN = 512
        B, S = (2, 128)
        orig_shape = x.shape
        xt = x.reshape(-1, orig_shape[-1])
        scores = xt @ gate_w.T
        top_vals, top_idx = jax.lax.top_k(scores, TOP_K)
        top_w = jax.nn.softmax(top_vals, axis=-1)
        combine = jnp.einsum('tke,tk->te', jax.nn.one_hot(top_idx, NUM_EXPERTS, dtype=xt.dtype), top_w)
        h = jax.nn.silu(jnp.einsum('td,ehd->eth', xt, w1)) * jnp.einsum('td,ehd->eth', xt, w3)
        ye = jnp.einsum('eth,edh->etd', h, w2)
        y = jnp.einsum('te,etd->td', combine, ye)
        return y.reshape(orig_shape)

    def _L2_attn_ref(query, Wq, bq, Wk, bk, Wv, bv, Wo, bo):
        import jax, jax.numpy as jnp
        import numpy as np
        B, L, E, H = (8, 256, 128, 16)
        D = E // H
        EPS = 1e-06
        bsz, tgt_len, embed_dim = query.shape
        n_head = H
        head_dim = embed_dim // n_head
        m = tgt_len
        q = query @ Wq + bq
        k = query @ Wk + bk
        v = query @ Wv + bv

        def to_heads(x):
            return x.reshape(bsz, tgt_len, n_head, head_dim).transpose(0, 2, 1, 3)
        q = jax.nn.softmax(to_heads(q), axis=-1)
        k = jax.nn.softmax(to_heads(k), axis=-1)
        v = to_heads(v)
        comp_q = 1.0 - q
        comp_k = 1.0 - k
        idx = np.pi / 2 * jnp.arange(1, m + 1, dtype=jnp.float32) / m
        sin = jnp.sin(idx)[None, None, :, None]
        cos = jnp.cos(idx)[None, None, :, None]

        def feat(x):
            return jnp.concatenate([x * sin, x * cos], axis=-1)
        qf, comp_qf = (feat(q), feat(comp_q))
        kf, comp_kf = (feat(k), feat(comp_k))

        def branch(qf_, kf_):
            kv = jnp.einsum('bhld,bhlm->bhdm', kf_, v)
            z = 1.0 / jnp.maximum(jnp.einsum('bhld,bhd->bhl', qf_, kf_.sum(axis=2)), EPS)
            return jnp.einsum('bhld,bhdm,bhl->bhlm', qf_, kv, z)
        attn = branch(qf, kf) + branch(comp_qf, comp_kf)
        out = attn.transpose(2, 0, 1, 3).reshape(tgt_len, bsz, embed_dim)
        out = out @ Wo + bo
        return out.reshape(bsz, tgt_len, embed_dim)

    def _L2_xattn_ref(features, masks, latents, gm, bm, gl, bl, Wq, Wk, Wv, Wo):
        import jax, jax.numpy as jnp
        import numpy as np
        DIM = 128
        HEADS = 16
        DIM_HEAD = 64
        INNER = HEADS * DIM_HEAD
        B, F, Q = (16, 512, 64)
        EPS = 1e-05
        SCALE = DIM_HEAD ** (-0.5)

        def _layernorm(x, gamma, beta):
            mu = jnp.mean(x, axis=-1, keepdims=True)
            var = jnp.var(x, axis=-1, keepdims=True)
            return (x - mu) * jax.lax.rsqrt(var + EPS) * gamma + beta
        b, f, d = features.shape
        q_len = latents.shape[1]
        x = _layernorm(features, gm, bm)
        lat = _layernorm(latents, gl, bl)
        q = (lat @ Wq).reshape(b, q_len, HEADS, DIM_HEAD).transpose(0, 2, 1, 3)
        kv_input = jnp.concatenate([x, lat], axis=1)
        kv_mask = jnp.concatenate([masks, jnp.ones((b, q_len), dtype=bool)], axis=1)
        kv_mask = kv_mask[:, None, None, :]
        k = (kv_input @ Wk).reshape(b, f + q_len, HEADS, DIM_HEAD).transpose(0, 2, 1, 3)
        v = (kv_input @ Wv).reshape(b, f + q_len, HEADS, DIM_HEAD).transpose(0, 2, 1, 3)
        q = q * SCALE
        sim = jnp.einsum('bhqd,bhfd->bhqf', q, k)
        sim = sim - jax.lax.stop_gradient(jnp.max(sim, axis=-1, keepdims=True))
        sim = jnp.where(kv_mask, sim, -jnp.inf)
        alphas = jax.nn.softmax(sim, axis=-1)
        out = jnp.einsum('bhqf,bhfd->bhqd', alphas, v)
        out = out.transpose(0, 2, 1, 3).reshape(b, q_len, INNER)
        return out @ Wo

    def _L2_ffn_ref(x, gate_w, w1, b1, w2, b2):
        import jax, jax.numpy as jnp
        import numpy as np
        TEMPERATURE = 1.0
        TOPK = 2
        s, b, h = x.shape
        x_flat = x.reshape(s * b, h)
        logits = x_flat @ gate_w.T
        probs = jax.nn.softmax(logits / TEMPERATURE, axis=-1)
        topk_probs, topk_idx = jax.lax.top_k(probs, TOPK)
        hidden = jax.nn.relu(jnp.einsum('th,ehf->tef', x_flat, w1) + b1[None])
        all_out = jnp.einsum('tef,efh->teh', hidden, w2) + b2[None]
        gathered = jnp.take_along_axis(all_out, topk_idx[:, :, None], axis=1)
        y_flat = jnp.sum(gathered * topk_probs[:, :, None], axis=1)
        return y_flat.reshape(s, b, h)

    def _L3_attn_ref(x, mask, Wq_down, Wkv_down, Wq_up, Wk_up, Wv_up, Wout):
        import jax, jax.numpy as jnp
        import numpy as np
        D_MODEL = 128
        NUM_HEADS = 16
        HEAD_DIM = D_MODEL // NUM_HEADS
        D_LATENT = 32
        B, T = (4, 256)
        Bz, Tz, C = x.shape
        scale = HEAD_DIM ** (-0.5)
        latent_q = x @ Wq_down.T
        latent_kv = x @ Wkv_down.T
        q = (latent_q @ Wq_up.T).reshape(Bz, Tz, NUM_HEADS, HEAD_DIM).transpose(0, 2, 1, 3)
        k = (latent_kv @ Wk_up.T).reshape(Bz, Tz, NUM_HEADS, HEAD_DIM).transpose(0, 2, 1, 3)
        v = (latent_kv @ Wv_up.T).reshape(Bz, Tz, NUM_HEADS, HEAD_DIM).transpose(0, 2, 1, 3)
        attn = jnp.einsum('bhqd,bhkd->bhqk', q, k) * scale
        attn = jnp.where(mask, attn, jnp.float32(-jnp.inf))
        attn = jax.nn.softmax(attn, axis=-1)
        out = jnp.einsum('bhqk,bhkd->bhqd', attn, v)
        out = out.transpose(0, 2, 1, 3).reshape(Bz, Tz, C)
        return out @ Wout.T

    def _L3_xattn_ref(q, k, v, mask, Wq, bq, Wk, bk, Wv, bv, Wo, bo):
        import jax, jax.numpy as jnp
        import numpy as np
        D_MODEL = 128
        H = 16
        D_K = D_MODEL // H
        B, S = (2, 256)
        NEG = -1000000000.0

        def _split_heads(x):
            b, s, _ = x.shape
            return x.reshape(b, s, H, D_K).transpose(0, 2, 1, 3)
        query = _split_heads(q @ Wq.T + bq)
        key_ = _split_heads(k @ Wk.T + bk)
        value = _split_heads(v @ Wv.T + bv)
        scores = jnp.einsum('bhqd,bhkd->bhqk', query, key_) / jnp.sqrt(jnp.asarray(D_K, query.dtype))
        scores = jnp.where(mask == 0, jnp.asarray(NEG, scores.dtype), scores)
        attn = jax.nn.softmax(scores, axis=-1)
        ctx = jnp.einsum('bhqk,bhkd->bhqd', attn, value)
        ctx = ctx.transpose(0, 2, 1, 3).reshape(q.shape[0], -1, D_MODEL)
        return ctx @ Wo.T + bo

    def _L3_ffn_ref(x, w1, w2):
        import jax, jax.numpy as jnp
        import numpy as np
        EMBED_DIM = 128
        HIDDEN = 4 * EMBED_DIM
        BATCH, SEQ = (4, 512)
        EPS = 1e-05

        def _quant_weight(w):
            s = jnp.clip(jnp.mean(jnp.abs(w)), EPS, None)
            wq = jnp.clip(jnp.round(w / s), -1.0, 1.0) * s
            return w + jax.lax.stop_gradient(wq - w)

        def _quant_act(x):
            scale = 127.0 / jnp.clip(jnp.max(jnp.abs(x), axis=-1, keepdims=True), EPS, None)
            xq = jnp.clip(jnp.round(x * scale), -128.0, 127.0) / scale
            return x + jax.lax.stop_gradient(xq - x)

        def _bitlinear(x, w):
            return jnp.einsum('bsi,oi->bso', _quant_act(x), _quant_weight(w))
        h = jax.nn.gelu(_bitlinear(x, w1), approximate=False)
        return _bitlinear(h, w2)
    x = x + _L0_attn_ref(_layernorm(x, axis=-1), L0_attn_W_qkv, L0_attn_b_qkv, L0_attn_W_proj, L0_attn_b_proj)
    x = x + _L0_xattn_ref(_layernorm(x, axis=-1), ctx_1024, mask_BxS2_bk0, L0_xattn_q_w, L0_xattn_q_b, L0_xattn_kv_w, L0_xattn_kv_b, L0_xattn_proj_w, L0_xattn_proj_b)
    x = x + _L0_ffn_ref(_layernorm(x, axis=-1), L0_ffn_gate_w, L0_ffn_shared_gate_w, L0_ffn_shared_up_w, L0_ffn_shared_down_w, L0_ffn_routed_gate_w, L0_ffn_routed_up_w, L0_ffn_routed_down_w)
    x = x + _L1_attn_ref(_layernorm(x, axis=-1), L1_attn_Wqkv, L1_attn_Wout)
    x = x + _L1_xattn_ref(_layernorm(x, axis=-1), ctx_1024, L1_xattn_Wq, L1_xattn_bq, L1_xattn_Wk, L1_xattn_bk, L1_xattn_Wv, L1_xattn_bv, L1_xattn_Wo, L1_xattn_bo, 16)
    x = x + _L1_ffn_ref(_layernorm(x, axis=-1), L1_ffn_gate_w, L1_ffn_w1, L1_ffn_w2, L1_ffn_w3)
    x = x + _L2_attn_ref(_layernorm(x, axis=-1), L2_attn_Wq, L2_attn_bq, L2_attn_Wk, L2_attn_bk, L2_attn_Wv, L2_attn_bv, L2_attn_Wo, L2_attn_bo)
    x = x + _L2_xattn_ref(ctx_1024, mask_BxS2_bf1, _layernorm(x, axis=-1), L2_xattn_gm, L2_xattn_bm, L2_xattn_gl, L2_xattn_bl, L2_xattn_Wq, L2_xattn_Wk, L2_xattn_Wv, L2_xattn_Wo)
    x = x + _L2_ffn_ref(_layernorm(x, axis=-1), L2_ffn_gate_w, L2_ffn_w1, L2_ffn_b1, L2_ffn_w2, L2_ffn_b2)
    x = x + _L3_attn_ref(_layernorm(x, axis=-1), L3_attn_mask, L3_attn_Wq_down, L3_attn_Wkv_down, L3_attn_Wq_up, L3_attn_Wk_up, L3_attn_Wv_up, L3_attn_Wout)
    x = x + _L3_xattn_ref(_layernorm(x, axis=-1), ctx_1024, ctx_1024, mask_1x1xSxS2_if1, L3_xattn_Wq, L3_xattn_bq, L3_xattn_Wk, L3_xattn_bk, L3_xattn_Wv, L3_xattn_bv, L3_xattn_Wo, L3_xattn_bo)
    x = x + _L3_ffn_ref(_layernorm(x, axis=-1), L3_ffn_w1, L3_ffn_w2)
    return x

_drawn_inputs = setup_inputs


def setup_inputs(seed=0):
    import zlib

    import numpy as np

    out = dict(_drawn_inputs(seed))
    spreads = {'L0_attn_b_qkv': (0.0, 0.1),
     'L0_attn_b_proj': (0.0, 0.1),
     'L0_xattn_q_b': (0.0, 0.1),
     'L0_xattn_kv_b': (0.0, 0.1),
     'L0_xattn_proj_b': (0.0, 0.1),
     'L1_xattn_bq': (0.0, 0.8),
     'L1_xattn_bk': (0.0, 2.0),
     'L1_xattn_bv': (0.0, 0.1),
     'L1_xattn_bo': (0.0, 0.1),
     'L2_xattn_gm': (1.0, 0.2),
     'L2_xattn_bm': (0.0, 0.1),
     'L2_xattn_gl': (1.0, 0.2),
     'L2_xattn_bl': (0.0, 0.1),
     'L2_ffn_b1': (0.0, 0.38),
     'L2_ffn_b2': (0.0, 0.1),
     'L3_xattn_bq': (0.0, 0.47),
     'L3_xattn_bk': (0.0, 2.0),
     'L3_xattn_bv': (0.0, 0.1),
     'L3_xattn_bo': (0.0, 0.1)}
    factors = {'L0_ffn_gate_w': 4.741,
     'L0_ffn_shared_gate_w': 2.686,
     'L0_ffn_routed_gate_w': 4.101,
     'L0_ffn_routed_up_w': 3.774,
     'L0_ffn_routed_down_w': 4.111,
     'L1_xattn_Wq': 8.0,
     'L1_xattn_Wk': 8.0,
     'L2_attn_Wq': 8.0,
     'L2_attn_bq': 39.694,
     'L2_attn_Wk': 8.0,
     'L2_attn_bk': 42.6,
     'L3_attn_Wq_down': 8.0,
     'L3_attn_Wq_up': 8.0,
     'L3_attn_Wk_up': 8.0}
    for name, (base, spread) in spreads.items():
        noise = np.random.default_rng([zlib.crc32(name.encode()), seed]).standard_normal(out[name].shape)
        drawn = base * np.exp(spread * noise) if base else spread * noise
        out[name] = jnp.asarray(drawn.astype(out[name].dtype))
    for name, factor in factors.items():
        out[name] = (out[name] * factor).astype(out[name].dtype)
    return out
```

```python
from contextlib import ExitStack

import numpy as np

import concourse.bass as bass
from concourse import mybir

P = 128
B, S, D = 4, 256, 128
T = B * S
NT = T // P
S2 = 512
TC = B * S2
H, HD = 16, 8
NQ = H // 4
G = B * NQ
SCALE = float(HD) ** -0.5
BIG = float(2.0 ** 100)
EPS = 1e-5

F32 = mybir.dt.float32
BF16 = mybir.dt.bfloat16
ALU = mybir.AluOpType
ACT = mybir.ActivationFunctionType
AX = mybir.AxisListType

TERMS = 6
Q_PART = [0, 0, 1, 0, 2, 1]
K_PART = [0, 1, 0, 2, 0, 1]
STACK = HD * TERMS
MAXROW = 64
MASKROW = 96

N_SUB = 12

ATTN = [
    dict(name="L0_attn", sub=0, cross=False, maximum=True, mask=None),
    dict(name="L0_xattn", sub=1, cross=True, maximum=True, mask="row"),
    dict(name="L1_attn", sub=3, cross=False, maximum=False, mask="causal"),
    dict(name="L3_attn", sub=9, cross=False, maximum=True, mask="full"),
    dict(name="L3_xattn", sub=10, cross=True, maximum=True, mask="full"),
]


W_OF = {}
W_COLS = 0
for _name, _n in ([(f"{a}_{w}", n) for a in ("L0_attn", "L0_xattn", "L1_attn", "L3_attn", "L3_xattn")
                   for w, n in (("q", 1), ("k", 1), ("v", 1), ("o", NQ))]
                  + [("L3_down", 1)]
                  + [(f"{a}_{w}", 1) for a in ("L1_xattn", "L2_attn") for w in "qkvo"]):
    W_OF[_name] = W_COLS
    W_COLS += _n
C_OF = {n: i for i, n in enumerate([
    "L0_attn_q", "L0_attn_k", "L0_xattn_q", "L0_xattn_k", "L3_xattn_q", "L3_xattn_k",
    "L1_xattn_q", "L1_xattn_k", "zero"])}
R_OF = {n: i for i, n in enumerate([
    "L0_attn_v", "L0_attn_o", "L0_xattn_v", "L0_xattn_o", "L3_xattn_v", "L3_xattn_o",
    "L1_xattn_v", "L1_xattn_o", "L2_attn_q", "L2_attn_k", "L2_attn_v", "L2_attn_o",
    "L2_xattn_gm", "L2_xattn_bm", "L2_xattn_gl", "L2_xattn_bl"])}


class Count:

    def __init__(self, sem, totals, step=1):
        self.sem, self.totals, self.step = sem, list(totals), step

    def at(self, use, n):
        return self.step * (sum(self.totals[:use]) + n)


def program(nc, a, ctx):
    sb = lambda name, shape, dt=F32: ctx.enter_context(nc.sbuf_tensor(name, shape, dt))
    new = lambda name: ctx.enter_context(nc.semaphore(name))
    counter = lambda name, totals, step=1: Count(new(name), totals, step)

    x = sb("x", [P, NT, D])
    h = sb("h", [P, NT, D])
    hT = sb("hT", [P, T])
    ctxT = sb("ctxT", [P, TC])
    w = sb("w", [P, W_COLS * D])
    bcol = sb("bcol", [P, len(C_OF)])
    brow = sb("brow", [P, len(R_OF), D])
    ident = sb("ident", [P, P])
    identb = sb("identb", [P, P], BF16)
    sumsel = sb("sumsel", [P, P])
    qs = sb("qs", [P, G * 4 * S], BF16)
    ks = sb("ks", [P, G * 4 * S], BF16)
    probs = sb("probs", [P, 2, 4, 2 * S2])
    v = sb("v", [P, TC // P, D])
    vaug = sb("vaug", [P, 2, 4, 4, 32])
    osb = sb("osb", [P, 2, S])
    rsum = sb("rsum", [P, 2, S])
    oT = sb("oT", [P, 2, NQ, S])
    mx = sb("mx", [P, 2, 8])
    mres = sb("mres", [P, 2, 8])
    mpart = sb("mpart", [P, 2, 2, 4, 3], BF16)
    mT = sb("mT", [P, 2, S], BF16)
    stats = sb("stats", [P, NT, 6])
    mv = sb("mv", [P, NT, 2])
    rstd = sb("rstd", [P, NT])
    veps = sb("veps", [P, NT])
    mhalf = sb("mhalf", [P, NT])
    tmp = probs[:, :, :, :].rearrange("p s j n -> p (s j n)")
    parts_at = tmp[:, 6 * 512:].bitcast(BF16)
    qpart = parts_at[:, 0:3 * T].rearrange("p (k n) -> p k n", k=3)
    kpart = parts_at[:, 3 * T:3 * (T + TC)].rearrange("p (k n) -> p k n", k=3)
    ps = ctx.enter_context(nc.psum_tensor("ps", [P, 8, 512], F32))
    scr_q = nc.dram_tensor("scr_q", [H * STACK, T], BF16, kind="Internal").ap()
    scr_k = nc.dram_tensor("scr_k", [H * STACK, TC], BF16, kind="Internal").ap()
    mrow_raw = sb("mrow_raw", [B, S2], mybir.dt.uint8)
    mrow = sb("mrow", [B, S2], BF16)
    m3a_raw = sb("m3a_raw", [P, 2, 2, S], mybir.dt.uint8)
    m3a = sb("m3a", [P, 2, 2 * S], BF16)
    m3x_raw = tmp[:, 0:4 * S2].bitcast(mybir.dt.int32)
    m3x = sb("m3x", [P, 2, 2 * S2], BF16)

    def wt(name, n=1):
        c = W_OF[name] * D
        return w[:, c:c + n * D]

    def bank(i, lo=0, hi=512):
        return ps[:, i, lo:hi]

    A = range(len(ATTN))
    kt_n = [4 if c["cross"] else 2 for c in ATTN]
    units = [8 if c["cross"] else 4 for c in ATTN]
    chunks = [6 if c["cross"] else 4 for c in ATTN]
    vgroups = [4 if c["cross"] else 2 for c in ATTN]
    maxed = [int(c["maximum"]) for c in ATTN]
    loaded = new("loaded")
    consts = new("consts")
    dchain, achain, pchain = new("dve_chain"), new("act_chain"), new("pool_chain")
    norms = 15
    ln_var = counter("ln_var", [1] * norms)
    ln_rstd = counter("ln_rstd", [1] * norms)
    ln_h = counter("ln_h", [1] * norms)
    ln_tp = counter("ln_tp", [0 if n in (9, 14) else 2 for n in range(norms)])
    ln_hT = counter("ln_hT", [0 if n in (7, 8, 9, 10, 14) else 2 for n in range(norms)])
    x_done = counter("x_done", [1] * N_SUB)
    biased = [0, 1, 4, 6, 10]
    x_biased = counter("x_biased", [1] * len(biased))
    lat_mm = counter("lat_mm", [2])
    lat_sb = counter("lat_sb", [2])
    proj_mm = counter("proj_mm", chunks)
    proj_f = counter("proj_f", chunks)
    proj_p1 = counter("proj_p1", chunks)
    proj_r = counter("proj_r", chunks)
    proj_p2 = counter("proj_p2", chunks)
    proj_p3 = counter("proj_p3", chunks)
    v_mm = counter("v_mm", vgroups)
    v_sb = counter("v_sb", vgroups)
    spilled = [counter(f"spilled{i}", [int(i < chunks[n]) for n in A], 96) for i in range(6)]
    stacked = [counter(f"stacked{b}", [1 for n in A], 32) for b in range(B)]
    mask_in = [counter(f"mask_in{b}", [1], 16) for b in range(B)]
    q_rows_clear = counter("q_rows_clear", [1] * len(ATTN))
    a_mm = counter("a_mm", [G * u * m for u, m in zip(units, maxed)])
    a_max = counter("a_max", [G * u * m for u, m in zip(units, maxed)])
    m_split = counter("m_split", [G * m for m in maxed])
    m_tp = counter("m_tp", [G * m for m in maxed])
    m_sb = counter("m_sb", [G * m for m in maxed])
    m_in = [counter(f"m_in{i}", [G // 4 * m for m in maxed], 64) for i in range(4)]
    b_mm = counter("b_mm", [G * u for u in units])
    clipped = counter("clipped", [G * u * (1 - m) for u, m in zip(units, maxed)])
    p_exp = counter("p_exp", [G * u for u in units])
    p_cut = counter("p_cut", [G * 4 * (1 - m) for u, m in zip(units, maxed)])
    va_set = counter("va_set", [G] * len(ATTN))
    av_mm = counter("av_mm", [G] * len(ATTN))
    o_sb = counter("o_sb", [G] * len(ATTN))
    sel_mm = counter("sel_mm", [G] * len(ATTN))
    o_recip = counter("o_recip", [G] * len(ATTN))
    o_div = counter("o_div", [G] * len(ATTN))
    y_mm = counter("y_mm", [B] * len(ATTN))
    out_sem = new("out_sem")

    chained = {}

    def link(eng, sem, ins):
        ins.then_inc(sem, 1)
        chained[sem.name] = chained.get(sem.name, 0) + 1
        eng.wait_ge(sem, chained[sem.name])

    def norm_vector(dve, n, src=x, dst=h, affine=None):
        for j in range(NT):
            dve.bn_stats(stats[:, j, :], src[:, j, :]).then_inc(dchain, 1)
            chained[dchain.name] = chained.get(dchain.name, 0) + 1
        dve.wait_ge(dchain, chained[dchain.name])
        for j in range(NT):
            ins = dve.bn_aggr(mv[:, j, :], stats[:, j, :])
        link(dve, dchain, ins)
        dve.tensor_scalar(veps[:, :], mv[:, :, 1], EPS, None, ALU.add).then_inc(ln_var.sem, 1)
        dve.wait_ge(ln_rstd.sem, ln_rstd.at(n, 1))
        for j in range(NT):
            ins = dve.tensor_scalar(dst[:, j, :], src[:, j, :], mv[:, j, 0:1], rstd[:, j:j + 1],
                                    ALU.subtract, ALU.mult)
        if affine:
            for name, op in zip(affine, (ALU.mult, ALU.add)):
                link(dve, dchain, ins)
                ins = dve.tensor_tensor(dst[:, :, :], dst[:, :, :], brow[:, R_OF[name], :].unsqueeze(1).to_broadcast([P, NT, D]), op)
        ins.then_inc(ln_h.sem, 1)

    def norm_gpsimd(pool, n):
        pool.wait_ge(ln_var.sem, ln_var.at(n, 1))
        pool.tensor_tensor(rstd[:, :], veps[:, :], mhalf[:, :], ALU.pow).then_inc(ln_rstd.sem, 1)
        pool.wait_ge(ln_rstd.sem, ln_rstd.at(n, 1))

    def norm_tensor(pe, n, src=h, after=None):
        pe.wait_ge(ln_h.sem, ln_h.at(n, 1))
        if after:
            pe.wait_ge(*after)
        for j in range(NT):
            ins = pe.transpose(bank(6 + j // 4, j % 4 * P, j % 4 * P + P), src[:, j, :], ident[:, :])
            if j % 4 == 3:
                ins.then_inc(ln_tp.sem, 1)

    def norm_scalar(act, n):
        for c in range(2):
            act.wait_ge(ln_tp.sem, ln_tp.at(n, c + 1))
            act.copy(hT[:, c * 512:c * 512 + 512], bank(6 + c)).then_inc(ln_hT.sem, 1)

    def bias_gpsimd(pool, sub, n, name):
        pool.wait_ge(ln_h.sem, ln_h.at(n, 1))
        pool.tensor_tensor(x[:, :, :], x[:, :, :],
                           brow[:, R_OF[name], :].unsqueeze(1).to_broadcast([P, NT, D]),
                           ALU.add).then_inc(x_biased.sem, 1)
        pool.wait_ge(x_biased.sem, x_biased.at(biased.index(sub), 1))

    class Attention:
        def __init__(self, n, norm):
            c = ATTN[n]
            self.n, self.norm, self.name, self.sub = n, norm, c["name"], c["sub"]
            self.cross, self.maximum, self.mask = c["cross"], c["maximum"], c["mask"]
            self.kt, self.u, self.nch, self.nv = kt_n[n], units[n], chunks[n], vgroups[n]
            self.keys = self.kt * P
            self.low_rank = self.name == "L3_attn"
            self.kin = ctxT if self.cross else hT
            self.lag = 2 if self.maximum else 0
            self.bias = f"{self.name}_q" in C_OF

        def qv(self, g, j):
            return qs[:, (4 * g + j) * S:(4 * g + j + 1) * S]

        def kv(self, g, j, lo=0, hi=None):
            at = (4 * g + j) % (G * 4 * S // self.keys) * self.keys
            return ks[:, at + lo:at + (hi or self.keys)]

        def chunk(self, i):
            return (True, i) if i < 2 else (False, i - 2)

        def project_tensor(self, pe):
            n = self.n
            if self.low_rank:
                for c in range(2):
                    pe.wait_ge(ln_hT.sem, ln_hT.at(self.norm, c + 1))
                    pe.matmul(bank(c)[0:64, :], wt("L3_down")[:, 0:64], hT[:, c * 512:c * 512 + 512],
                              start=True, stop=True).then_inc(lat_mm.sem, 1)
                for c in range(2):
                    pe.wait_ge(lat_sb.sem, lat_sb.at(0, c + 1))
            for i in range(self.nch):
                query, c = self.chunk(i)
                if query or not self.cross:
                    pe.wait_ge(ln_hT.sem, ln_hT.at(self.norm, c + 1))
                cols = slice(c * 512, c * 512 + 512)
                if self.low_rank:
                    r = slice(0, 32) if query else slice(32, 64)
                    lhs, rhs = wt(f"{self.name}_{'q' if query else 'k'}")[r, :], lat[r, cols]
                else:
                    lhs = wt(f"{self.name}_{'q' if query else 'k'}")
                    rhs = (hT if query else self.kin)[:, cols]
                pe.matmul(bank(i), lhs, rhs, start=True, stop=True).then_inc(proj_mm.sem, 1)
            for c in range(self.nv):
                if c >= 2:
                    pe.wait_ge(v_sb.sem, v_sb.at(n, c - 1))
                else:
                    pe.wait_ge(ln_hT.sem, ln_hT.at(self.norm, 2))
                for t in range(4):
                    cols = slice((4 * c + t) * P, (4 * c + t + 1) * P)
                    if self.low_rank:
                        lhs, rhs = lat[32:64, cols], wt(f"{self.name}_v")[32:64, :]
                    else:
                        lhs, rhs = self.kin[:, cols], wt(f"{self.name}_v")
                    ins = pe.matmul(bank(6 + c % 2, t * P, t * P + P), lhs, rhs, start=True, stop=True)
                ins.then_inc(v_mm.sem, 1)

        def project_vector(self, dve):
            n = self.n
            if self.low_rank:
                for c in range(2):
                    dve.wait_ge(lat_mm.sem, lat_mm.at(0, c + 1))
                    dve.tensor_copy(lat[0:64, c * 512:c * 512 + 512], bank(c)[0:64, :]).then_inc(lat_sb.sem, 1)
            for i in range(self.nch + 2):
                if i < self.nch:
                    query, c = self.chunk(i)
                    f = tmp[:, i * 512:i * 512 + 512]
                    col = C_OF[f"{self.name}_{'q' if query else 'k'}" if self.bias else "zero"]
                    dve.wait_ge(proj_mm.sem, proj_mm.at(n, i + 1))
                    dve.tensor_scalar(f, bank(i), bcol[:, col:col + 1], SCALE if query else 1.0,
                                      ALU.add, ALU.mult).then_inc(proj_f.sem, 1)
                if 0 <= i - 1 < self.nch:
                    f, (p1, _, _) = tmp[:, (i - 1) * 512:i * 512], self.parts(i - 1)
                    dve.wait_ge(proj_f.sem, proj_f.at(n, i))
                    dve.wait_ge(proj_p1.sem, proj_p1.at(n, i))
                    dve.tensor_tensor(f, f, p1, ALU.subtract).then_inc(proj_r.sem, 1)
                if 0 <= i - 2:
                    f, (_, p2, p3) = tmp[:, (i - 2) * 512:(i - 1) * 512], self.parts(i - 2)
                    dve.wait_ge(proj_r.sem, proj_r.at(n, i - 1))
                    dve.wait_ge(proj_p2.sem, proj_p2.at(n, i - 1))
                    dve.tensor_tensor(p3, f, p2, ALU.subtract).then_inc(proj_p3.sem, 1)
            for c in range(self.nv):
                out = v[:, 4 * c:4 * c + 4, :]
                src = bank(6 + c % 2).rearrange("p (t d) -> p t d", d=D)
                dve.wait_ge(v_mm.sem, v_mm.at(n, c + 1))
                if self.bias:
                    b_v = brow[:, R_OF[f"{self.name}_v"], :].unsqueeze(1).to_broadcast([P, 4, D])
                    dve.tensor_tensor(out, src, b_v, ALU.add).then_inc(v_sb.sem, 1)
                else:
                    dve.tensor_copy(out, src).then_inc(v_sb.sem, 1)

        def parts(self, i):
            query, c = self.chunk(i)
            return [(qpart if query else kpart)[:, k, c * 512:c * 512 + 512] for k in range(3)]

        def project_scalar(self, act):
            n = self.n
            for i in range(self.nch + 1):
                if i < self.nch:
                    act.wait_ge(proj_f.sem, proj_f.at(n, i + 1))
                    act.copy(self.parts(i)[0], tmp[:, i * 512:i * 512 + 512]).then_inc(proj_p1.sem, 1)
                if i >= 1:
                    act.wait_ge(proj_r.sem, proj_r.at(n, i))
                    act.copy(self.parts(i - 1)[1], tmp[:, (i - 1) * 512:i * 512]).then_inc(proj_p2.sem, 1)

        def stack_sync(self, sp):
            n = self.n
            for i in range(self.nch):
                query, c = self.chunk(i)
                scr = (scr_q if query else scr_k).rearrange("(r t) n -> r t n", t=TERMS)
                sp.wait_ge(proj_p3.sem, proj_p3.at(n, i + 1))
                sp.wait_ge(proj_p2.sem, proj_p2.at(n, i + 1))
                for t in range(TERMS):
                    part = self.parts(i)[(Q_PART if query else K_PART)[t]]
                    sp.dma_start(scr[:, t, c * 512:c * 512 + 512], part).then_inc(spilled[i].sem, 16)
            for b in range(2 if self.cross else B):
                self.load_sync(sp, b)

        def load_sync(self, sp, b):
            n = self.n
            if n == 3 and b == 0:
                sp.wait_ge(rows_again.sem, rows_again.at(0, 1))
            if self.cross and b >= 2:
                sp.wait_ge(b_mm.sem, b_mm.at(n, (b - 1) * NQ * self.u))
            for query in (True, False):
                cols = S if query else self.keys
                i = b * cols // 512 + (0 if query else 2)
                sp.wait_ge(spilled[i].sem, spilled[i].at(n, 1))
                src = (scr_q if query else scr_k).rearrange("(h r) n -> r h n", r=STACK)
                slot = b if query or not self.cross else b % 2
                at = slice(slot * H * cols, (slot + 1) * H * cols)
                dst = (qs if query else ks)[0:STACK, at]
                sp.dma_start(dst.rearrange("p (h k) -> p h k", h=H),
                             src[:, :, b * cols:(b + 1) * cols]).then_inc(stacked[b].sem, 16)
            if self.mask == "row":
                sp.dma_start(ks[MASKROW:MASKROW + 1, at].rearrange("p (h k) -> p h k", h=H),
                             mrow[b:b + 1, :].unsqueeze(1).to_broadcast([1, H, S2])).then_inc(mask_in[b].sem, 16)

        def maxima_sync(self, sp):
            if not self.maximum:
                return
            for g in range(G):
                sp.wait_ge(m_sb.sem, m_sb.at(self.n, g + 1))
                for j in range(4):
                    sp.dma_start(self.qv(g, j)[MAXROW:MAXROW + 3, :],
                                 mT[3 * j:3 * j + 3, g % 2, :]).then_inc(m_in[g % 4].sem, 16)
                if self.cross and g in (5, 9):
                    self.load_sync(sp, (g + 3) // 4)

        def a_tensor(self, pe, s, u):
            n, k = self.n, s * self.u + u
            if u == 0 and s % NQ == 0:
                pe.wait_ge(stacked[s // NQ].sem, stacked[s // NQ].at(n, 1))
                if self.mask == "row":
                    pe.wait_ge(mask_in[s // NQ].sem, 16)
            if k == 0:
                pe.wait_ge(q_rows_clear.sem, q_rows_clear.at(n, 1))
            if k >= 2:
                pe.wait_ge(a_max.sem, a_max.at(n, k - 1))
            full = self.mask == "full"
            if self.cross:
                j, qt = u // 2, u % 2
                if full:
                    pe.matmul(bank(k % 2), identb[:, :], m3x[:, 0, qt * S2:(qt + 1) * S2], start=True, stop=False)
                ins = pe.matmul(bank(k % 2), self.qv(s, j)[:, qt * P:(qt + 1) * P], self.kv(s, j),
                                start=not full, stop=True)
            else:
                for qt in range(2):
                    if full:
                        pe.matmul(bank(k % 2, qt * S, (qt + 1) * S), identb[:, :], m3a[:, 0, qt * S:(qt + 1) * S],
                                  start=True, stop=False)
                    ins = pe.matmul(bank(k % 2, qt * S, (qt + 1) * S), self.qv(s, u)[:, qt * P:(qt + 1) * P],
                                    self.kv(s, u), start=not full, stop=True)
            ins.then_inc(a_mm.sem, 1)

        def a_vector(self, dve, s, u):
            n, k = self.n, s * self.u + u
            if u == 0 and s >= 2:
                dve.wait_ge(m_split.sem, m_split.at(n, s - 1))
            dve.wait_ge(a_mm.sem, a_mm.at(n, k + 1))
            if self.cross:
                j, qt = u // 2, u % 2
                out, src = mx[:, s % 2, 4 * qt + j:4 * qt + j + 1], bank(k % 2)
            else:
                out = mx[:, s % 2, :].rearrange("p (t j) -> p j t", t=2)[:, u, :]
                src = bank(k % 2).rearrange("p (t k) -> p t k", t=2)
            dve.tensor_reduce(out, src, AX.X, ALU.max).then_inc(a_max.sem, 1)

        def split_vector(self, dve, s):
            n = self.n
            m, r = mx[:, s % 2, :], mres[:, s % 2, :]
            part = lambda k: mpart[:, s % 2, :, :, k].rearrange("p t j -> p (t j)")
            if s >= 2:
                dve.wait_ge(m_tp.sem, m_tp.at(n, s - 1))
            dve.wait_ge(a_max.sem, a_max.at(n, (s + 1) * self.u))
            link(dve, dchain, dve.tensor_scalar(part(0), m, -1.0, None, ALU.mult))
            link(dve, dchain, dve.scalar_tensor_tensor(out=r, in0=m, scalar=-1.0, in1=part(0),
                                                       op0=ALU.mult, op1=ALU.subtract))
            link(dve, dchain, dve.tensor_copy(part(1), r))
            dve.tensor_tensor(part(2), r, part(1), ALU.subtract).then_inc(m_split.sem, 1)

        def turn_tensor(self, pe, s):
            n = self.n
            pe.wait_ge(m_split.sem, m_split.at(n, s + 1))
            if s >= 1:
                pe.wait_ge(m_sb.sem, m_sb.at(n, s))
            for qt in range(2):
                ins = pe.transpose(bank(7).bitcast(BF16)[0:12, qt * P:(qt + 1) * P],
                                   mpart[:, s % 2, qt, :, :].rearrange("p j k -> p (j k)"), identb[:, :])
            ins.then_inc(m_tp.sem, 1)

        def turn_scalar(self, act, s):
            n = self.n
            act.wait_ge(m_tp.sem, m_tp.at(n, s + 1))
            if s >= 2:
                act.wait_ge(m_in[s % 4 - 2].sem, m_in[s % 4 - 2].at(n, (s - 2) // 4 + 1))
            act.copy(mT[0:12, s % 2, :], bank(7).bitcast(BF16)[0:12, 0:S]).then_inc(m_sb.sem, 1)

        def unit(self, u):
            return (u // 2, 2 * (u % 2)) if self.cross else (u, 0)

        def b_tensor(self, pe, s, u):
            n, k = self.n, s * self.u + u
            j, kt0 = self.unit(u)
            if u == 0:
                if self.maximum:
                    pe.wait_ge(m_in[s % 4].sem, m_in[s % 4].at(n, s // 4 + 1))
                elif s % NQ == 0:
                    pe.wait_ge(stacked[s // NQ].sem, stacked[s // NQ].at(n, 1))
            if k == 0 and not self.maximum:
                pe.wait_ge(q_rows_clear.sem, q_rows_clear.at(n, 1))
            if k >= 2:
                done = p_exp if self.maximum else clipped
                pe.wait_ge(done.sem, done.at(n, k - 1))
            full = self.mask == "full"
            mask = m3x[:, 1, kt0 * S:(kt0 + 2) * S] if self.cross else m3a[:, 1, :]
            for t in range(2):
                q0 = P if self.mask == "causal" and t else 0
                out = bank(2 + k % 2, t * S, (t + 1) * S - q0)
                if full:
                    pe.matmul(out, identb[:, :], mask[:, t * S:(t + 1) * S], start=True, stop=False)
                ins = pe.matmul(out, self.kv(s, j, (kt0 + t) * P, (kt0 + t + 1) * P), self.qv(s, j)[:, q0:S],
                                start=not full, stop=True)
            ins.then_inc(b_mm.sem, 1)

        def clip_vector(self, dve, s, u):
            n, k = self.n, s * self.u + u
            dve.wait_ge(b_mm.sem, b_mm.at(n, k + 1))
            if k >= 4:
                dve.wait_ge(p_exp.sem, p_exp.at(n, k - 3))
            dve.tensor_scalar(clip_sb[:, k % 4, :], bank(2 + k % 2, 0, 3 * P), 10.0, -10.0,
                              ALU.min, ALU.max).then_inc(clipped.sem, 1)

        def b_scalar(self, act, s, u):
            n, k = self.n, s * self.u + u
            j, kt0 = self.unit(u)
            if k == 0:
                for i in range(self.nch):
                    act.wait_ge(spilled[i].sem, spilled[i].at(n, 1))
            if u == 0 and s >= 2:
                act.wait_ge(av_mm.sem, av_mm.at(n, s - 1))
            if self.maximum:
                act.wait_ge(b_mm.sem, b_mm.at(n, k + 1))
                act.activation(probs[:, s % 2, j, kt0 * S:(kt0 + 2) * S], bank(2 + k % 2),
                               ACT.Exp).then_inc(p_exp.sem, 1)
            else:
                act.wait_ge(clipped.sem, clipped.at(n, k + 1))
                act.activation(probs[:, s % 2, j, 0:3 * P], clip_sb[:, k % 4, :], ACT.Exp).then_inc(p_exp.sem, 1)

        def cut_gpsimd(self, pool, s):
            n = self.n
            for j in range(4):
                pool.wait_ge(p_exp.sem, p_exp.at(n, s * self.u + j + 1))
                part = probs[:, s % 2, j, 0:4 * P].rearrange("p (t q) -> p t q", t=2)[:, :, 0:P]
                pool.tensor_tensor(part, part, tri[:, :].unsqueeze(1).to_broadcast([P, 2, P]),
                                   ALU.mult).then_inc(p_cut.sem, 1)
                pool.wait_ge(p_cut.sem, p_cut.at(n, 4 * s + j + 1))

        def values_gpsimd(self, pool, s):
            n, b, quad = self.n, s // NQ, s % NQ
            if s == 0:
                pool.wait_ge(v_sb.sem, v_sb.at(n, self.nv))
            if s >= 2:
                pool.wait_ge(av_mm.sem, av_mm.at(n, s - 1))
            src = v[:, b * self.kt:(b + 1) * self.kt, quad * 4 * HD:(quad + 1) * 4 * HD]
            pool.tensor_copy(vaug[:, s % 2, 0:self.kt, :, 0:HD],
                             src.rearrange("p t (j d) -> p t j d", j=4)).then_inc(va_set.sem, 1)
            pool.wait_ge(va_set.sem, va_set.at(n, s + 1))

        def av_tensor(self, pe, s, kt):
            n = self.n
            if kt == 0:
                pe.wait_ge(va_set.sem, va_set.at(n, s + 1))
                if s >= 2:
                    pe.wait_ge(o_sb.sem, o_sb.at(n, s - 1))
                done = p_exp if self.maximum else p_cut
                pe.wait_ge(done.sem, done.at(n, (s + 1) * (self.u if self.maximum else 4)))
            q0 = P if self.mask == "causal" and kt else 0
            for j in range(4):
                ins = pe.matmul(ps[32 * j:32 * j + 32, 4 + s % 2, q0:S], vaug[:, s % 2, kt, j, :],
                                probs[:, s % 2, j, kt * S:(kt + 1) * S - q0],
                                start=(kt == 0), stop=(kt == self.kt - 1), skip_group_check=True)
            if kt == self.kt - 1:
                ins.then_inc(av_mm.sem, 1)

        def o_scalar(self, act, s):
            n = self.n
            act.wait_ge(av_mm.sem, av_mm.at(n, s + 1))
            if s >= 2:
                act.wait_ge(o_div.sem, o_div.at(n, s - 1))
                act.wait_ge(sel_mm.sem, sel_mm.at(n, s - 1))
            act.copy(osb[:, s % 2, :], bank(4 + s % 2, 0, S)).then_inc(o_sb.sem, 1)

        def sum_tensor(self, pe, s):
            n = self.n
            pe.wait_ge(o_sb.sem, o_sb.at(n, s + 1))
            if s >= 1:
                pe.wait_ge(o_recip.sem, o_recip.at(n, s))
            if s and s % NQ == 0:
                pe.wait_ge(y_out.sem, y_out.at(n, s // NQ))
            pe.matmul(bank(6, 0, S), sumsel[:, :], osb[:, s % 2, :], start=True, stop=True).then_inc(sel_mm.sem, 1)

        def recip_vector(self, dve, s):
            n = self.n
            dve.wait_ge(sel_mm.sem, sel_mm.at(n, s + 1))
            if s >= 2:
                dve.wait_ge(o_div.sem, o_div.at(n, s - 1))
            dve.reciprocal(rsum[:, s % 2, :], bank(6, 0, S)).then_inc(o_recip.sem, 1)

        def div_gpsimd(self, pool, s):
            n, b, quad = self.n, s // NQ, s % NQ
            pool.wait_ge(o_recip.sem, o_recip.at(n, s + 1))
            pool.wait_ge(o_sb.sem, o_sb.at(n, s + 1))
            if quad == 0 and b >= 2:
                pool.wait_ge(y_mm.sem, y_mm.at(n, b - 1))
            pool.tensor_tensor(oT[:, b % 2, quad, :], osb[:, s % 2, :], rsum[:, s % 2, :],
                               ALU.mult).then_inc(o_div.sem, 1)
            pool.wait_ge(o_div.sem, o_div.at(n, s + 1))

        def y_tensor(self, pe, b):
            n = self.n
            pe.wait_ge(o_div.sem, o_div.at(n, NQ * (b + 1)))
            wo = wt(f"{self.name}_o", NQ)
            for qt in range(2):
                for quad in range(NQ):
                    ins = pe.matmul(bank(6, S + qt * P, S + (qt + 1) * P), oT[:, b % 2, quad, qt * P:(qt + 1) * P],
                                    wo[:, quad * D:(quad + 1) * D], start=(quad == 0), stop=(quad == NQ - 1),
                                    skip_group_check=True)
            ins.then_inc(y_mm.sem, 1)

        def y_vector(self, dve, b):
            n = self.n
            dve.wait_ge(y_mm.sem, y_mm.at(n, b + 1))
            if b == 0 and self.bias:
                dve.wait_ge(x_biased.sem, x_biased.at(biased.index(self.sub), 1))
            xb = x[:, 2 * b:2 * b + 2, :]
            dve.tensor_tensor(xb, xb, bank(6, S, 2 * S).rearrange("p (t d) -> p t d", d=D),
                              ALU.add).then_inc(y_out.sem, 1)

        def order(self):
            for s in range(G + self.lag + 5):
                e, o, d = s - self.lag, s - self.lag - 1, s - self.lag - 2
                for u in range(self.u):
                    if self.maximum and s < G:
                        yield "a", s, u
                    if 0 <= e < G:
                        yield "b", e, u
                    if 0 <= o < G and u % 2 == 0 if self.cross else 0 <= o < G and u < 2:
                        yield "av", o, u // 2 if self.cross else u
                    if u == 0 and 0 <= d < G:
                        yield "sum", d, 0
                    if u == self.u // 2 and self.maximum and 0 <= s - 1 < G:
                        yield "turn", s - 1, 0
                if self.maximum and s < G:
                    yield "split", s, 0
                if 0 <= o < G:
                    yield "o", o, 0
                if d >= 0 and d % NQ == NQ - 1 and d < G:
                    yield "y", d // NQ, 0

        def tensor(self, pe):
            for what, s, u in self.order():
                if what == "a":
                    self.a_tensor(pe, s, u)
                elif what == "b":
                    self.b_tensor(pe, s, u)
                elif what == "av":
                    self.av_tensor(pe, s, u)
                elif what == "sum":
                    self.sum_tensor(pe, s)
                elif what == "turn":
                    self.turn_tensor(pe, s)
                elif what == "y":
                    self.y_tensor(pe, s)

        def vector(self, dve):
            for what, s, u in self.order():
                if what == "a":
                    self.a_vector(dve, s, u)
                elif what == "b" and not self.maximum:
                    self.clip_vector(dve, s, u)
                elif what == "sum":
                    self.recip_vector(dve, s)
                elif what == "split":
                    self.split_vector(dve, s)
                elif what == "y":
                    self.y_vector(dve, s)

        def scalar(self, act):
            for what, s, u in self.order():
                if what == "b":
                    self.b_scalar(act, s, u)
                elif what == "o":
                    self.o_scalar(act, s)
                elif what == "turn":
                    self.turn_scalar(act, s)

        def gpsimd(self, pool):
            for what, s, u in self.order():
                if what == "b" and u == 0:
                    self.values_gpsimd(pool, s)
                if what == "b" and u == self.u - 1 and self.mask == "causal":
                    self.cut_gpsimd(pool, s)
                elif what == "sum":
                    self.div_gpsimd(pool, s)

    wring = sb("wring", [P, 2, 1536])
    gatew = sb("gatew", [P, 48])
    down = sb("expert_order", [P, 32])
    b1c = sb("b1c", [P, 8 * 4])
    b2r = sb("b2r", [8, D])
    gated = sb("gated", [P, 2, 512])
    comb = sb("comb", [P, NT, 32])
    lg = sb("lg", [P, NT, 32])
    r1 = sb("r1", [P, NT, 32])
    r2 = sb("r2", [P, NT, 32])
    rcol = sb("rcol", [P, 6, NT])
    combT = sb("combT", [8, T])
    MOES = [dict(name="L0_ffn", sub=2, experts=32, chunks=2, shared=True, gate_at=0),
            dict(name="L1_ffn", sub=5, experts=8, chunks=4, shared=False, gate_at=32),
            dict(name="L2_ffn", sub=8, experts=8, chunks=4, shared=False, gate_at=40)]
    runs = [m["experts"] + m["shared"] for m in MOES]
    munits = [r * m["chunks"] * 2 for r, m in zip(runs, MOES)]
    routed_mm = counter("routed_mm", [1] * 3)
    r_exp_in = counter("r_exp_in", [1] * 3)
    r_exp = counter("r_exp", [1] * 3)
    xs_ready = counter("xs_ready", [1, 0, 0])
    xs_tp = counter("xs_tp", [2, 0, 0])
    xs_T = counter("xs_T", [2, 0, 0])
    w_in = [counter(f"w_in{i}", [(r + 1 - i) // 2 for r in runs], 48) for i in range(2)]
    up_mm = counter("up_mm", munits)
    act_sb = counter("act_sb", munits)
    hid_sb = counter("hid_sb", munits)
    down_mm = counter("down_mm", [2 * r for r in runs])
    mixed = counter("mixed", [2 * r for r in runs])
    combT_mm = counter("combT_mm", [0, 0, 1])
    combT_sb = counter("combT_sb", [0, 0, 1])
    yb_mm = counter("yb_mm", [0, 0, 1])

    class Mixture:
        def __init__(self, m, norm):
            c = MOES[m]
            self.m, self.norm, self.name, self.sub = m, norm, c["name"], c["sub"]
            self.e, self.c, self.shared, self.gate_at = c["experts"], c["chunks"], c["shared"], c["gate_at"]
            self.runs = runs[m]
            self.relu = self.name == "L2_ffn"
            self.width = self.c * P
            self.xsT = tmp[:, 4096:4096 + T]

        def hid(self, r):
            at = r % 2 * (2048 if self.c == 2 else 4096)
            return tmp[:, at:at + self.c * T].rearrange("p (c n) -> p c n", c=self.c)

        def weights(self, r):
            s, n = r % 2, self.width
            if self.relu:
                return wring[:, s, 0:n], None, wring[:, s, 1024:1024 + self.c * D]
            return wring[:, s, 0:n], wring[:, s, 512:512 + n], wring[:, s, 1024:1024 + self.c * D]

        def sync(self, sp):
            m = self.m
            if self.sub:
                sp.wait_ge(x_done.sem, x_done.at(self.sub - 1, 1))
            for r in range(self.runs):
                if r >= 2:
                    sp.wait_ge(down_mm.sem, down_mm.at(m, 2 * (r - 1)))
                first, second, last = self.weights(r)
                e = r - self.shared
                src = a[f"{self.name}_up"], a[f"{self.name}_down"]
                i = r
                sp.dma_start(first, src[0][i, :, 0:self.width]).then_inc(w_in[r % 2].sem, 16)
                if self.relu:
                    sp.dma_start(last[:, 0:D], src[1][i, :, 0:D]).then_inc(w_in[r % 2].sem, 16)
                    sp.dma_start(last[:, D:], src[1][i, :, D:]).then_inc(w_in[r % 2].sem, 16)
                else:
                    sp.dma_start(second, src[0][i, :, self.width:]).then_inc(w_in[r % 2].sem, 16)
                    sp.dma_start(last, src[1][i]).then_inc(w_in[r % 2].sem, 16)

        def tensor(self, pe):
            m, e = self.m, self.e
            pe.wait_ge(ln_hT.sem, ln_hT.at(self.norm, 2))
            for t in range(NT):
                ins = pe.matmul(bank(7, t * 32, t * 32 + e), hT[:, t * P:(t + 1) * P],
                                gatew[:, self.gate_at:self.gate_at + e], start=True, stop=True)
            ins.then_inc(routed_mm.sem, 1)
            for r in range(self.runs + 1):
                if r == 1 and self.shared:
                    pe.wait_ge(xs_ready.sem, xs_ready.at(m, 1))
                    for j in range(NT):
                        ins = pe.transpose(bank(6 + j // 4, j % 4 * P, j % 4 * P + P), h[:, j, :], ident[:, :])
                        if j % 4 == 3:
                            ins.then_inc(xs_tp.sem, 1)
                    pe.wait_ge(xs_T.sem, xs_T.at(m, 2))
                if r < self.runs:
                    self.up_tensor(pe, r)
                if r >= 1:
                    self.down_tensor(pe, r - 1)
            if self.relu:
                for t in range(NT):
                    ins = pe.transpose(bank(0 + t // 4, t % 4 * P, t % 4 * P + P)[0:8, :], comb[:, t, 0:8], ident[:, :])
                ins.then_inc(combT_mm.sem, 1)
                pe.wait_ge(combT_sb.sem, combT_sb.at(m, 1))
                for t in range(NT):
                    ins = pe.matmul(bank(2 + t // 4, t % 4 * P, t % 4 * P + P), combT[:, t * P:(t + 1) * P],
                                    b2r[:, :], start=True, stop=True)
                ins.then_inc(yb_mm.sem, 1)

        def up_tensor(self, pe, r):
            m = self.m
            first, second, _ = self.weights(r)
            src = self.xsT if self.shared and r else hT
            pe.wait_ge(w_in[r % 2].sem, w_in[r % 2].at(m, r // 2 + 1))
            for c in range(self.c):
                for half in range(2):
                    k = r * self.c * 2 + c * 2 + half
                    if k >= 2:
                        pe.wait_ge(hid_sb.sem, hid_sb.at(m, k - 1))
                    cols = src[:, half * 512:half * 512 + 512]
                    ins = pe.matmul(bank(k % 2), first[:, c * P:(c + 1) * P], cols, start=True, stop=True)
                    if second is not None:
                        ins = pe.matmul(bank(2 + k % 2), second[:, c * P:(c + 1) * P], cols, start=True, stop=True)
                    ins.then_inc(up_mm.sem, 1)

        def down_tensor(self, pe, r):
            m = self.m
            hid, last = self.hid(r), self.weights(r)[2]
            pe.wait_ge(hid_sb.sem, hid_sb.at(m, (r + 1) * self.c * 2))
            for half in range(2):
                if r >= 2:
                    pe.wait_ge(mixed.sem, mixed.at(m, 2 * (r - 2) + half + 1))
                for q in range(4):
                    t = half * 4 + q
                    for c in range(self.c):
                        ins = pe.matmul(bank(4 + r % 2 * 2 + half, q * P, q * P + P), hid[:, c, t * P:(t + 1) * P],
                                        last[:, c * D:(c + 1) * D], start=(c == 0), stop=(c == self.c - 1))
                ins.then_inc(down_mm.sem, 1)

        def scalar(self, act):
            m = self.m
            act.wait_ge(r_exp_in.sem, r_exp_in.at(m, 1))
            if self.name == "L0_ffn":
                act.activation(rcol[:, 1, :], rcol[:, 0, :], ACT.Exp, scale=-1.0).then_inc(r_exp.sem, 1)
            elif self.name == "L1_ffn":
                act.activation(rcol[:, 3, :], rcol[:, 2, :], ACT.Exp).then_inc(r_exp.sem, 1)
            else:
                act.activation(r2[:, :, 0:8], r1[:, :, 0:8], ACT.Exp).then_inc(r_exp.sem, 1)
            for r in range(self.runs):
                if r == 1 and self.shared:
                    for c in range(2):
                        act.wait_ge(xs_tp.sem, xs_tp.at(m, c + 1))
                        act.copy(self.xsT[:, c * 512:c * 512 + 512], bank(6 + c)).then_inc(xs_T.sem, 1)
                for i in range(self.c * 2):
                    k = r * self.c * 2 + i
                    act.wait_ge(up_mm.sem, up_mm.at(m, k + 1))
                    if k >= 2:
                        act.wait_ge(hid_sb.sem, hid_sb.at(m, k - 1))
                    act.activation(gated[:, k % 2, :], bank(k % 2), ACT.Silu).then_inc(act_sb.sem, 1) \
                        if not self.relu else act.activation(
                            gated[:, k % 2, :], bank(k % 2), ACT.Relu,
                            bias=b1c[:, r * 4 + i // 2:r * 4 + i // 2 + 1]).then_inc(act_sb.sem, 1)
            if self.relu:
                act.wait_ge(combT_mm.sem, combT_mm.at(m, 1))
                act.copy(combT[:, :].rearrange("p (b n) -> p b n", b=2), ps[0:8, 0:2, :]).then_inc(combT_sb.sem, 1)

        def route_vector(self, dve):
            m, e = self.m, self.e
            L, R1, R2, C = lg[:, :, 0:e], r1[:, :, 0:e], r2[:, :, 0:e], comb[:, :, 0:e]
            col = lambda i: rcol[:, i, :]
            wide = lambda ap: ap.unsqueeze(2).to_broadcast([P, NT, e])
            do = lambda ins: link(dve, dchain, ins)
            order = down[:, 32 - e:32].unsqueeze(1).to_broadcast([P, NT, e])

            def first_of(out, src, top, scratch, topcol):
                do(dve.tensor_tensor(out, src, wide(top), ALU.is_equal))
                do(dve.tensor_tensor(scratch, out, order, ALU.mult))
                do(dve.tensor_reduce(topcol, scratch, AX.X, ALU.max))
                do(dve.tensor_tensor(out, scratch, wide(topcol), ALU.is_equal))

            dve.wait_ge(routed_mm.sem, routed_mm.at(m, 1))
            do(dve.tensor_copy(L, bank(7, 0, NT * 32).rearrange("p (t e) -> p t e", e=32)[:, :, 0:e]))
            do(dve.tensor_reduce(col(0), L, AX.X, ALU.max))
            first_of(C, L, col(0), R2, col(4))
            if self.name == "L0_ffn":
                dve.engine_nop().then_inc(r_exp_in.sem, 1)
                dve.wait_ge(r_exp.sem, r_exp.at(m, 1))
                do(dve.tensor_scalar(col(2), col(1), 1.0, None, ALU.add))
                do(dve.reciprocal(col(3), col(2)))
                for j in range(NT):
                    ins = dve.tensor_scalar(h[:, j, :], h[:, j, :], rcol[:, 3, j:j + 1], None, ALU.mult)
                ins.then_inc(xs_ready.sem, 1)
                return
            do(dve.scalar_tensor_tensor(out=R1, in0=C, scalar=-BIG, in1=L, op0=ALU.mult, op1=ALU.add))
            do(dve.tensor_reduce(col(1), R1, AX.X, ALU.max))
            first_of(R2, R1, col(1), R1, col(4))
            if self.name == "L1_ffn":
                dve.tensor_tensor(col(2), col(1), col(0), ALU.subtract).then_inc(r_exp_in.sem, 1)
                dve.wait_ge(r_exp.sem, r_exp.at(m, 1))
                do(dve.tensor_scalar(col(4), col(3), 1.0, None, ALU.add))
                do(dve.reciprocal(col(5), col(4)))
                do(dve.tensor_tensor(R2, R2, wide(col(3)), ALU.mult))
                do(dve.tensor_tensor(C, C, R2, ALU.add))
                do(dve.tensor_tensor(C, C, wide(col(5)), ALU.mult))
            else:
                do(dve.tensor_tensor(C, C, R2, ALU.add))
                dve.tensor_tensor(R1, L, wide(col(0)), ALU.subtract).then_inc(r_exp_in.sem, 1)
                dve.wait_ge(r_exp.sem, r_exp.at(m, 1))
                do(dve.tensor_reduce(col(2), R2, AX.X, ALU.add))
                do(dve.reciprocal(col(3), col(2)))
                do(dve.tensor_tensor(C, C, R2, ALU.mult))
                do(dve.tensor_tensor(C, C, wide(col(3)), ALU.mult))

        def vector(self, dve):
            m = self.m
            self.route_vector(dve)
            for r in range(self.runs + 1):
                if r < self.runs:
                    hid = self.hid(r)
                    if r >= 2:
                        dve.wait_ge(down_mm.sem, down_mm.at(m, 2 * (r - 1)))
                    for c in range(self.c):
                        for half in range(2):
                            k = r * self.c * 2 + c * 2 + half
                            out = hid[:, c, half * 512:half * 512 + 512]
                            dve.wait_ge(act_sb.sem, act_sb.at(m, k + 1))
                            if self.relu:
                                dve.tensor_copy(out, gated[:, k % 2, :]).then_inc(hid_sb.sem, 1)
                            else:
                                dve.tensor_tensor(out, gated[:, k % 2, :], bank(2 + k % 2),
                                                  ALU.mult).then_inc(hid_sb.sem, 1)
                if r >= 1:
                    self.mix_vector(dve, r - 1)
            if self.relu:
                dve.wait_ge(yb_mm.sem, yb_mm.at(m, 1))
                dve.wait_ge(mixed.sem, mixed.at(m, 2 * self.runs))
                link(dve, dchain, dve.tensor_tensor(x[:, :, :].rearrange("p t d -> p (t d)"),
                                                    x[:, :, :].rearrange("p t d -> p (t d)"),
                                                    ps[:, 2:4, :].rearrange("p b n -> p (b n)"), ALU.add))

        def mix_vector(self, dve, r):
            m = self.m
            if r >= 1:
                dve.wait_ge(mixed.sem, mixed.at(m, 2 * r))
            for half in range(2):
                dve.wait_ge(down_mm.sem, down_mm.at(m, 2 * r + half + 1))
                for q in range(4):
                    t, e = half * 4 + q, r - self.shared
                    out = bank(4 + r % 2 * 2 + half, q * P, q * P + P)
                    if e < 0:
                        ins = dve.tensor_tensor(x[:, t, :], out, x[:, t, :], ALU.add)
                    else:
                        ins = dve.scalar_tensor_tensor(out=x[:, t, :], in0=out, scalar=comb[:, t, e:e + 1],
                                                       in1=x[:, t, :], op0=ALU.mult, op1=ALU.add)
                ins.then_inc(mixed.sem, 1)

    bmask = sb("bmask", [P, H])
    vmask = sb("vmask", [P, 32])
    NK = S2 // H
    g_ctx = counter("g_ctx", [1], 16)
    g_k_mm = counter("g_k_mm", [B])
    g_k_sb = counter("g_k_sb", [B])
    g_v_mm = counter("g_v_mm", [1])
    g_v_sb = counter("g_v_sb", [1])
    g_q_mm = counter("g_q_mm", [2])
    g_q_sb = counter("g_q_sb", [2])
    g_s_mm = counter("g_s_mm", [NT])
    g_s_sub = counter("g_s_sub", [NT])
    g_exp = counter("g_exp", [NT])
    g_p = counter("g_p", [NT])
    g_tp = counter("g_tp", [NT])
    g_pT = counter("g_pT", [NT])
    g_av = counter("g_av", [B])
    g_oT = counter("g_oT", [B])
    g_y = counter("g_y", [2])

    class Gathered:
        sub, norm, name = 4, 4, "L1_xattn"
        ctxg = tmp[:, 0:TC]
        kbd = tmp[:, TC:2 * TC]
        vbd = tmp[:, 2 * TC:2 * TC + 512].rearrange("p (t n) -> p t n", n=32)
        qT = tmp[:, 2 * TC + 512:2 * TC + 512 + T]
        pr = tmp[:, 2 * TC + 512 + T:2 * TC + 512 + 2 * T].rearrange("p (s n) -> p s n", s=2)
        pT = tmp[:, 2 * TC + 512 + 2 * T:2 * TC + 512 + 3 * T].rearrange("p (c n) -> p c n", c=NQ)
        oT = hT

        def sync(self, sp):
            sp.wait_ge(x_done.sem, x_done.at(self.sub - 1, 1))
            sp.dma_start(self.ctxg, a["ctxT_by_head"]).then_inc(g_ctx.sem, 16)

        def order(self):
            for t in range(NT + 2):
                if t < NT:
                    yield "score", t
                if 0 <= t - 1 < NT:
                    yield "turn", t - 1
                    if (t - 1) % 2:
                        yield "sum", (t - 1) // 2

        def tensor(self, pe):
            pe.wait_ge(g_ctx.sem, 16)
            for b in range(B):
                pe.matmul(bank(b), wt("L1_xattn_k"), self.ctxg[:, b * S2:(b + 1) * S2],
                          start=True, stop=True).then_inc(g_k_mm.sem, 1)
            for t in range(B * NQ):
                c = t % NQ
                ins = pe.matmul(bank(4, t * 32, t * 32 + 32), self.ctxg[:, t * P:(t + 1) * P],
                                wt("L1_xattn_v")[:, c * 32:c * 32 + 32], start=True, stop=True)
            ins.then_inc(g_v_mm.sem, 1)
            for c in range(2):
                pe.wait_ge(ln_hT.sem, ln_hT.at(self.norm, c + 1))
                pe.matmul(bank(5 + c), wt("L1_xattn_q"), hT[:, c * 512:c * 512 + 512],
                          start=True, stop=True).then_inc(g_q_mm.sem, 1)
            pe.wait_ge(g_k_sb.sem, g_k_sb.at(0, B))
            pe.wait_ge(g_q_sb.sem, g_q_sb.at(0, 2))
            pe.wait_ge(g_v_sb.sem, g_v_sb.at(0, 1))
            for what, t in self.order():
                if what == "score":
                    if t >= 2:
                        pe.wait_ge(g_s_sub.sem, g_s_sub.at(0, t - 1))
                    pe.matmul(bank(t % 2), self.qT[:, t * P:(t + 1) * P], self.kbd[:, t // 2 * S2:(t // 2 + 1) * S2],
                              start=True, stop=True).then_inc(g_s_mm.sem, 1)
                elif what == "turn":
                    pe.wait_ge(g_p.sem, g_p.at(0, t + 1))
                    if t >= 2:
                        pe.wait_ge(g_pT.sem, g_pT.at(0, t - 1))
                    for c in range(NQ):
                        ins = pe.transpose(bank(2 + t % 2, c * P, c * P + P), self.pr[:, t % 2, c * P:(c + 1) * P],
                                           ident[:, :])
                    ins.then_inc(g_tp.sem, 1)
                else:
                    b = t
                    pe.wait_ge(g_pT.sem, g_pT.at(0, 2 * b + 2))
                    if b >= 2:
                        pe.wait_ge(g_oT.sem, g_oT.at(0, b - 1))
                    for c in range(NQ):
                        ins = pe.matmul(ps[32 * c:32 * c + 32, 4 + b % 2, 0:S], self.vbd[:, b * NQ + c, :],
                                        self.pT[:, c, :], start=True, stop=True)
                    ins.then_inc(g_av.sem, 1)
            pe.wait_ge(g_oT.sem, g_oT.at(0, B))
            for t in range(NT):
                ins = pe.matmul(bank(6 + t // 4, t % 4 * P, t % 4 * P + P), self.oT[:, t * P:(t + 1) * P],
                                wt("L1_xattn_o"), start=True, stop=True)
                if t % 4 == 3:
                    ins.then_inc(g_y.sem, 1)

        def scalar(self, act):
            for what, t in self.order():
                if what == "score":
                    act.wait_ge(g_s_sub.sem, g_s_sub.at(0, t + 1))
                    act.activation(self.pr[:, t % 2, :], self.pr[:, t % 2, :], ACT.Exp).then_inc(g_exp.sem, 1)
                elif what == "turn":
                    act.wait_ge(g_tp.sem, g_tp.at(0, t + 1))
                    if t >= 2 and t % 2 == 0:
                        act.wait_ge(g_av.sem, g_av.at(0, t // 2))
                    act.copy(self.pT[:, :, t % 2 * P:t % 2 * P + P],
                             bank(2 + t % 2).rearrange("p (c n) -> p c n", c=NQ)).then_inc(g_pT.sem, 1)
                else:
                    act.wait_ge(g_av.sem, g_av.at(0, t + 1))
                    act.wait_ge(g_q_mm.sem, g_q_mm.at(0, 2))
                    act.copy(self.oT[:, t * S:(t + 1) * S], bank(4 + t % 2, 0, S)).then_inc(g_oT.sem, 1)

        def vector(self, dve):
            do = lambda ins: link(dve, dchain, ins)
            for b in range(B):
                dve.wait_ge(g_k_mm.sem, g_k_mm.at(0, b + 1))
                dve.scalar_tensor_tensor(
                    out=self.kbd[:, b * S2:(b + 1) * S2].rearrange("p (h k) -> p h k", h=H),
                    in0=bank(b).rearrange("p (h k) -> p h k", h=H), scalar=bcol[:, C_OF["L1_xattn_k"]:C_OF["L1_xattn_k"] + 1],
                    in1=bmask[:, :].unsqueeze(2).to_broadcast([P, H, NK]), op0=ALU.add, op1=ALU.mult).then_inc(g_k_sb.sem, 1)
            dve.wait_ge(g_v_mm.sem, g_v_mm.at(0, 1))
            b_v = brow[:, R_OF["L1_xattn_v"], :].unsqueeze(1).to_broadcast([P, B, D])
            do(dve.tensor_tensor(self.vbd[:, :, :].rearrange("p (b c) n -> p b (c n)", b=B),
                                 bank(4).rearrange("p (b n) -> p b n", b=B), b_v, ALU.add))
            dve.tensor_tensor(self.vbd[:, :, :], self.vbd[:, :, :],
                              vmask[:, :].unsqueeze(1).to_broadcast([P, B * NQ, 32]), ALU.mult).then_inc(g_v_sb.sem, 1)
            for c in range(2):
                dve.wait_ge(g_q_mm.sem, g_q_mm.at(0, c + 1))
                dve.tensor_scalar(self.qT[:, c * 512:c * 512 + 512], bank(5 + c),
                                  bcol[:, C_OF["L1_xattn_q"]:C_OF["L1_xattn_q"] + 1], SCALE,
                                  ALU.add, ALU.mult).then_inc(g_q_sb.sem, 1)
            for what, t in self.order():
                top, tot = r1[:, t % 2, 0:H], r1[:, 2 + t % 2, 0:H]
                pr = self.pr[:, t % 2, :].rearrange("p (h k) -> p h k", h=H)
                wide = lambda ap: ap.unsqueeze(2).to_broadcast([P, H, NK])
                if what == "score":
                    src = bank(t % 2).rearrange("p (h k) -> p h k", h=H)
                    dve.wait_ge(g_s_mm.sem, g_s_mm.at(0, t + 1))
                    do(dve.tensor_reduce(top, src, AX.X, ALU.max))
                    if t >= 2:
                        dve.wait_ge(g_tp.sem, g_tp.at(0, t - 1))
                    dve.tensor_tensor(pr, src, wide(top), ALU.subtract).then_inc(g_s_sub.sem, 1)
                elif what == "turn":
                    dve.wait_ge(g_exp.sem, g_exp.at(0, t + 1))
                    do(dve.tensor_reduce(tot, pr, AX.X, ALU.add))
                    do(dve.reciprocal(tot, tot))
                    dve.tensor_tensor(pr, pr, wide(tot), ALU.mult).then_inc(g_p.sem, 1)
            for c in range(2):
                dve.wait_ge(g_y.sem, g_y.at(0, c + 1))
                dve.wait_ge(x_biased.sem, x_biased.at(biased.index(self.sub), 1))
                xc = x[:, 4 * c:4 * c + 4, :]
                do(dve.tensor_tensor(xc, xc, bank(6 + c).rearrange("p (t d) -> p t d", d=D), ALU.add))

        def gpsimd(self, pool):
            bias_gpsimd(pool, self.sub, self.norm, "L1_xattn_o")

    l_in = counter("l_in", [2], 16)
    l_ones = counter("l_ones", [1])
    l_qkv = counter("l_qkv", [NT])
    l_sub = counter("l_sub", [NT])
    l_exp = counter("l_exp", [NT])
    l_z = counter("l_z", [NT])
    l_sm = counter("l_sm", [NT])
    l_kf = counter("l_kf", [NT])
    l_v = counter("l_v", [NT])
    l_tp = counter("l_tp", [NT])
    l_qTb = counter("l_qTb", [B])
    l_cT = counter("l_cT", [B])
    l_kv = counter("l_kv", [B])
    l_kvm = counter("l_kvm", [B])
    l_num = counter("l_num", [NT])
    l_read = counter("l_read", [NT])
    l_o = counter("l_o", [NT])
    l_otp = counter("l_otp", [NT])
    l_oT = counter("l_oT", [NT])
    l_y = counter("l_y", [2])

    class Linear:
        sub, norm, name = 6, 6, "L2_attn"
        AW = D + H
        at = np.cumsum([0, 768, 4 * 4 * D, NT * (D + H), 2 * 4 * (D + H), T, T, D + H, 8, 4 * (D + H), 2 * D])
        part = lambda at, i: tmp[:, int(at[i]):int(at[i + 1])]
        z = part(at, 0).rearrange("p (s n) -> p s n", s=2)
        kf = part(at, 1).rearrange("p (t f n) -> p t f n", t=4, f=4)
        vx = part(at, 2).rearrange("p (t n) -> p t n", t=NT)
        kvm = part(at, 3).rearrange("p (s f n) -> p s f n", s=2, f=4)
        qT, cT = part(at, 4), part(at, 5)
        kvmask = part(at, 6)
        trig = part(at, 7).rearrange("p (t k) -> p t k", t=2)
        nd = part(at, 8).rearrange("p (f n) -> p f n", f=4)
        o = part(at, 9).rearrange("p (s n) -> p s n", s=2)
        oT = hT

        def sync(self, sp):
            sp.wait_ge(x_done.sem, x_done.at(self.sub - 1, 1))
            sp.dma_start(self.kvmask, a["kv_mask"]).then_inc(l_in.sem, 16)
            sp.dma_start(self.trig, a["trig"]).then_inc(l_in.sem, 16)

        def order(self):
            for t in range(NT + 1):
                if t < NT:
                    yield "qkv", t
                if t:
                    yield "turn", t - 1
                    if (t - 1) % 2:
                        yield "kv", (t - 1) // 2
                        for q in (t - 2, t - 1):
                            yield "num", q
            for t in range(NT):
                yield "out", t

        def tensor(self, pe):
            for what, t in self.order():
                if what == "qkv":
                    pe.wait_ge(ln_hT.sem, ln_hT.at(self.norm, t // 4 + 1))
                    if t >= 2:
                        pe.wait_ge(l_z.sem, l_z.at(0, t - 1))
                    pe.matmul(bank(t % 2, 0, 3 * D), hT[:, t * P:(t + 1) * P], wt("L2_attn_q", 3),
                              start=True, stop=True).then_inc(l_qkv.sem, 1)
                elif what == "turn":
                    pe.wait_ge(l_sm.sem, l_sm.at(0, t + 1))
                    if t >= 2 and t % 2 == 0:
                        pe.wait_ge(l_cT.sem, l_cT.at(0, t // 2))
                    pe.transpose(bank(4, t % 2 * P, t % 2 * P + P), self.z[:, t % 2, 0:D],
                                 ident[:, :]).then_inc(l_tp.sem, 1)
                elif what == "kv":
                    b = t
                    pe.wait_ge(l_v.sem, l_v.at(0, 2 * b + 2))
                    pe.wait_ge(l_kf.sem, l_kf.at(0, 2 * b + 2))
                    if b:
                        pe.wait_ge(l_kvm.sem, l_kvm.at(0, b))
                    for f in range(4):
                        for k in range(2):
                            ins = pe.matmul(bank(2 + f // 2, f % 2 * self.AW, (f % 2 + 1) * self.AW),
                                            self.kf[:, (2 * b + k) % 4, f, :], self.vx[:, 2 * b + k, :],
                                            start=(k == 0), stop=(k == 1))
                    ins.then_inc(l_kv.sem, 1)
                elif what == "num":
                    b = t // 2
                    pe.wait_ge(l_kvm.sem, l_kvm.at(0, b + 1))
                    pe.wait_ge(l_cT.sem, l_cT.at(0, b + 1))
                    if t:
                        pe.wait_ge(l_read.sem, l_read.at(0, t))
                    for f in range(4):
                        lhs = (self.qT if f < 2 else self.cT)[:, t * P:(t + 1) * P]
                        ins = pe.matmul(bank(6 + f // 2, f % 2 * self.AW, (f % 2 + 1) * self.AW), lhs,
                                        self.kvm[:, b % 2, f, :], start=True, stop=True)
                    ins.then_inc(l_num.sem, 1)
                else:
                    pe.wait_ge(l_o.sem, l_o.at(0, t + 1))
                    pe.transpose(bank(5, t % 4 * P, t % 4 * P + P), self.o8(t), ident[:, :]).then_inc(l_otp.sem, 1)
                    pe.wait_ge(l_oT.sem, l_oT.at(0, t + 1))
            for t in range(NT):
                ins = pe.matmul(bank(2 + t // 4, t % 4 * P, t % 4 * P + P), self.oT[:, t * P:(t + 1) * P],
                                wt("L2_attn_o"), start=True, stop=True)
                if t % 4 == 3:
                    ins.then_inc(l_y.sem, 1)

        def o8(self, t):
            return h[:, t, :]

        def scalar(self, act):
            for what, t in self.order():
                if what == "qkv":
                    act.wait_ge(l_sub.sem, l_sub.at(0, t + 1))
                    act.activation(self.z[:, t % 2, 0:2 * D], self.z[:, t % 2, 0:2 * D], ACT.Exp).then_inc(l_exp.sem, 1)
                elif what == "turn" and t % 2:
                    b = t // 2
                    act.wait_ge(l_tp.sem, l_tp.at(0, t + 1))
                    act.copy(self.qT[:, b * S:(b + 1) * S], bank(4, 0, S)).then_inc(l_qTb.sem, 1)
                elif what == "out":
                    act.wait_ge(l_otp.sem, l_otp.at(0, t + 1))
                    b, k = t // 2, t % 2
                    act.copy(self.oT[:, :].rearrange("p (l b) -> p b l", b=B)[:, b, k * P:(k + 1) * P],
                             bank(5, t % 4 * P, t % 4 * P + P)).then_inc(l_oT.sem, 1)

        def vector(self, dve):
            do = lambda ins: link(dve, dchain, ins)
            dve.wait_ge(l_in.sem, l_in.at(0, 2))
            dve.memset(self.vx[:, :, D:], 1.0).then_inc(l_ones.sem, 1)
            for what, t in self.order():
                z = self.z[:, t % 2, :]
                if what == "qkv":
                    top = r1[:, 0, 0:32]
                    qk = z[:, 0:2 * D].rearrange("p (h d) -> p h d", d=HD)
                    dve.wait_ge(l_qkv.sem, l_qkv.at(0, t + 1))
                    if t >= 2:
                        dve.wait_ge(l_tp.sem, l_tp.at(0, t - 1))
                        dve.wait_ge(l_v.sem, l_v.at(0, t - 1))
                        dve.wait_ge(l_kf.sem, l_kf.at(0, t - 1))
                    dve.tensor_tensor(z, bank(t % 2, 0, 3 * D), brow[:, R_OF["L2_attn_q"]:R_OF["L2_attn_q"] + 3, :]
                                      .rearrange("p r d -> p (r d)"), ALU.add).then_inc(l_z.sem, 1)
                    dve.wait_ge(l_z.sem, l_z.at(0, t + 1))
                    do(dve.tensor_reduce(top, qk, AX.X, ALU.max))
                    dve.tensor_tensor(qk, qk, top.unsqueeze(2).to_broadcast([P, 32, HD]),
                                      ALU.subtract).then_inc(l_sub.sem, 1)
                elif what == "turn":
                    qk = z[:, 0:2 * D].rearrange("p (h d) -> p h d", d=HD)
                    tot, inv = r1[:, 1, 0:32], r1[:, 2, 0:32]
                    dve.wait_ge(l_exp.sem, l_exp.at(0, t + 1))
                    do(dve.tensor_reduce(tot, qk, AX.X, ALU.add))
                    do(dve.reciprocal(inv, tot))
                    dve.tensor_tensor(qk, qk, inv.unsqueeze(2).to_broadcast([P, 32, HD]),
                                      ALU.mult).then_inc(l_sm.sem, 1)
                    dve.wait_ge(l_sm.sem, l_sm.at(0, t + 1))
                    if t >= 4 and t % 2 == 0:
                        dve.wait_ge(l_kv.sem, l_kv.at(0, t // 2 - 1))
                    for f in range(4):
                        tr = self.trig[:, t % 2, :]
                        out = self.kf[:, t % 4, f, :]
                        if f < 2:
                            ins = dve.tensor_scalar(out, z[:, D:2 * D], tr[:, f:f + 1], None, ALU.mult)
                        else:
                            ins = dve.tensor_scalar(out, z[:, D:2 * D], 1.0, tr[:, f:f + 1], ALU.subtract, ALU.mult)
                    ins.then_inc(l_kf.sem, 1)
                    if t % 2:
                        b = t // 2
                        dve.wait_ge(l_qTb.sem, l_qTb.at(0, b + 1))
                        dve.tensor_scalar(self.cT[:, b * S:(b + 1) * S], self.qT[:, b * S:(b + 1) * S], -1.0, 1.0,
                                          ALU.mult, ALU.add).then_inc(l_cT.sem, 1)
                elif what == "kv":
                    b = t
                    dve.wait_ge(l_kv.sem, l_kv.at(0, b + 1))
                    if b >= 2:
                        dve.wait_ge(l_num.sem, l_num.at(0, 2 * b - 2))
                    for k in range(2):
                        ins = dve.tensor_tensor(self.kvm[:, b % 2, 2 * k:2 * k + 2, :],
                                                bank(2 + k, 0, 2 * self.AW).rearrange("p (f n) -> p f n", f=2),
                                                self.kvmask.unsqueeze(1).to_broadcast([P, 2, self.AW]), ALU.mult)
                    ins.then_inc(l_kvm.sem, 1)
                elif what == "num":
                    tr = self.trig[:, t % 2, :]
                    nd, both = self.nd, ps[:, 6:8, :]
                    even = both[:, :, 0:self.AW]
                    odd = both[:, :, self.AW:2 * self.AW]
                    dve.wait_ge(l_num.sem, l_num.at(0, t + 1))
                    do(dve.tensor_scalar(nd[:, 0:2, :], even, tr[:, 0:1], None, ALU.mult))
                    dve.scalar_tensor_tensor(out=nd[:, 2:4, :], in0=odd, scalar=tr[:, 1:2], in1=nd[:, 0:2, :],
                                             op0=ALU.mult, op1=ALU.add).then_inc(l_read.sem, 1)
                    dve.wait_ge(l_read.sem, l_read.at(0, t + 1))
                    den = r1[:, 3, 0:32].rearrange("p (f h) -> p f h", f=2)
                    inv = r1[:, 4, 0:32].rearrange("p (f h) -> p f h", f=2)
                    do(dve.tensor_scalar(den, nd[:, 2:4, D:], 1e-6, None, ALU.max))
                    do(dve.reciprocal(inv, den))
                    for k in range(2):
                        ins = dve.tensor_tensor(nd[:, k, 0:D].rearrange("p (h d) -> p h d", d=HD),
                                                nd[:, 2 + k, 0:D].rearrange("p (h d) -> p h d", d=HD),
                                                inv[:, k, :].unsqueeze(2).to_broadcast([P, H, HD]), ALU.mult)
                    do(ins)
                    dve.tensor_tensor(self.o8(t), nd[:, 0, 0:D], nd[:, 1, 0:D], ALU.add).then_inc(l_o.sem, 1)
                    dve.wait_ge(l_o.sem, l_o.at(0, t + 1))
            for c in range(2):
                dve.wait_ge(l_y.sem, l_y.at(0, c + 1))
                dve.wait_ge(x_biased.sem, x_biased.at(biased.index(self.sub), 1))
                xc = x[:, 4 * c:4 * c + 4, :]
                do(dve.tensor_tensor(xc, xc, bank(2 + c).rearrange("p (t d) -> p t d", d=D), ALU.add))

        def gpsimd(self, pool):
            bias_gpsimd(pool, self.sub, self.norm, "L2_attn_o")
            pool.wait_ge(l_ones.sem, l_ones.at(0, 1))
            for t in range(NT):
                pool.wait_ge(l_z.sem, l_z.at(0, t + 1))
                pool.tensor_copy(self.vx[:, t, 0:D], self.z[:, t % 2, 2 * D:3 * D]).then_inc(l_v.sem, 1)
                pool.wait_ge(l_v.sem, l_v.at(0, t + 1))

    HW = 64
    PR = H // 2
    KV = S2 + S
    KT = KV // P
    UN = B * H * 2
    c_in = counter("c_in", [6], 16)
    c_mask = counter("c_mask", [1])
    c_m_mm = counter("c_m_mm", [4])
    c_m_sb = counter("c_m_sb", [4])
    c_kvT = counter("c_kvT", [6])
    c_q_mm = counter("c_q_mm", [B * PR])
    c_q_sb = counter("c_q_sb", [B * PR])
    c_v_mm = counter("c_v_mm", [B * KT * 2])
    c_v_sb = counter("c_v_sb", [B * KT * 2])
    c_s_mm = counter("c_s_mm", [UN])
    c_max = counter("c_max", [UN])
    c_neg = counter("c_neg", [UN])
    c_exp = counter("c_exp", [UN])
    c_inv = counter("c_inv", [UN])
    c_div = counter("c_div", [UN])
    c_tp = counter("c_tp", [UN])
    c_pT = counter("c_pT", [UN])
    c_av = counter("c_av", [B * PR])
    c_o = counter("c_o", [B * PR])
    c_y = counter("c_y", [B])
    c_y_out = counter("c_y_out", [B])

    class Latents:
        sub, name = 7, "L2_xattn"
        LAG = 3
        ksf, qsf = ks[:, :].bitcast(F32), qs[:, :].bitcast(F32)
        kvT = tmp[:, 0:B * KV].rearrange("p (b n) -> p b n", b=B)
        mqk = tmp[:, 3072:3072 + H * D].rearrange("p (h n) -> p h n", h=H)
        qT = tmp[:, 5120:6144].rearrange("p (s j q) -> p s j q", s=2, j=2)
        maskb = tmp[:, 6144:6144 + B * KV // 2].bitcast(BF16).rearrange("p (b n) -> p b n", b=B)
        v = ksf[:, 0:KT * H * HW].rearrange("p (t n) -> p t n", t=KT)
        oT = ksf[:, 6144:8192].rearrange("p (r q) -> p r q", r=PR)
        mask_raw = ksf[:, 0:TC // 4].bitcast(mybir.dt.uint8)
        pT = qsf[:, 0:6144].rearrange("p (s j t q) -> p s j t q", s=2, j=2, t=KT)
        wo = qsf[:, 6144:7168]
        wv = qsf[:, 7168:8192]
        ctx_tm = qsf[:, 0:TC].rearrange("p (t d) -> p t d", d=D)
        wqT = qsf[0:HW, 2048:4096]
        wkT = qsf[0:HW, 4096:6144]
        sc = wring[:, :, :].rearrange("p s n -> p (s n)").rearrange("p (s n) -> p s n", s=4)
        cols = r1[:, :, :].rearrange("p t e -> p (t e)")
        top, neg, tot, inv = cols[:, 0:4], cols[:, 4:8], cols[:, 8:12], cols[:, 12:16]

        def sync(self, sp):
            sp.wait_ge(x_done.sem, x_done.at(self.sub - 1, 1))
            for dst, src in ((self.ctx_tm, a["ctx"].rearrange("(t p) d -> p t d", p=P)), (self.wqT, a["L2_xattn_qT"]),
                             (self.wkT, a["L2_xattn_kT"]), (self.wo, a["L2_xattn_o"]), (self.wv, a["L2_xattn_v"]),
                             (self.mask_raw, a["mask_L2x"].unsqueeze(0).to_broadcast([P, TC]))):
                sp.dma_start(dst, src).then_inc(c_in.sem, 16)

        def order(self):
            for i in range(KT * 2):
                yield "v", i
            yield "q", 0
            for u in range(UN + self.LAG + 5):
                if u < UN:
                    if u % 4 == 2 and u // 4 + 1 < B * PR:
                        yield "q", u // 4 + 1
                    yield "score", u
                t = u - self.LAG
                if 0 <= t < UN:
                    yield "turn", t
                if t % 4 == 0 and 4 <= t <= UN:
                    g = t // 4 - 1
                    yield "sum", g
                    if g % PR == PR - 1:
                        if g // PR + 1 < B:
                            for i in range(KT * 2):
                                yield "v", (g // PR + 1) * KT * 2 + i
                        yield "y", g // PR

        def tensor(self, pe):
            for half in range(2):
                norm_tensor(pe, 7 + half, src=self.ctx_tm[:, 8 * half:8 * half + 8, :],
                            after=(c_kvT.sem, c_kvT.at(0, 2)) if half else None)
            pe.wait_ge(c_in.sem, c_in.at(0, 6))
            for i in range(4):
                for j in range(4):
                    cols = slice((4 * i + j) * D, (4 * i + j + 1) * D)
                    ins = pe.matmul(bank(i, j * D, j * D + D), self.wqT[:, cols], self.wkT[:, cols], start=True, stop=True)
                ins.then_inc(c_m_mm.sem, 1)
            norm_tensor(pe, 10, after=(c_kvT.sem, c_kvT.at(0, 4)))
            pe.wait_ge(c_kvT.sem, c_kvT.at(0, 6))
            pe.wait_ge(c_m_sb.sem, c_m_sb.at(0, 4))
            for what, i in self.order():
                if what == "v":
                    b, kt, half = i // (2 * KT), i // 2 % KT, i % 2
                    if i % (2 * KT) < 2 and b:
                        pe.wait_ge(c_pT.sem, c_pT.at(0, 4 * PR * b + 1))
                    if i % (2 * KT) >= 2:
                        pe.wait_ge(c_v_sb.sem, c_v_sb.at(0, i - 1))
                    pe.matmul(bank(4 + i % 2), self.kvT[:, b, kt * P:(kt + 1) * P],
                              self.wv[:, half * 512:half * 512 + 512], start=True, stop=True).then_inc(c_v_mm.sem, 1)
                elif what == "q":
                    b = i // PR
                    if i >= 1:
                        pe.wait_ge(c_q_sb.sem, c_q_sb.at(0, i))
                    for j in range(2):
                        ins = pe.matmul(bank(7, j * S, j * S + S), self.mqk[:, 2 * (i % PR) + j, :],
                                        self.kvT[:, b, S2:KV], start=True, stop=True)
                    ins.then_inc(c_q_mm.sem, 1)
                elif what == "score":
                    g, b, j, k = i // 4, i // (4 * PR), i // 2 % 2, i % 2
                    pe.wait_ge(c_q_sb.sem, c_q_sb.at(0, g + 1))
                    if i >= 2:
                        pe.wait_ge(c_max.sem, c_max.at(0, i - 1))
                    lhs = self.qT[:, g % 2, j, k * P:(k + 1) * P]
                    at = i % 2 * 2
                    pe.matmul(bank(at), lhs, self.kvT[:, b, 0:512], start=True, stop=True)
                    pe.matmul(bank(at + 1, 0, S), lhs, self.kvT[:, b, 512:KV],
                              start=True, stop=True).then_inc(c_s_mm.sem, 1)
                elif what == "turn":
                    pe.wait_ge(c_div.sem, c_div.at(0, i + 1))
                    if i:
                        pe.wait_ge(c_pT.sem, c_pT.at(0, i))
                    if i % (4 * PR) == 0:
                        pe.wait_ge(c_v_sb.sem, c_v_sb.at(0, (i // (4 * PR) + 1) * 2 * KT)) if i == 0 else None
                    if i % (4 * PR) == 1 and i > 1:
                        pe.wait_ge(c_v_sb.sem, c_v_sb.at(0, (i // (4 * PR) + 1) * 2 * KT))
                    for t in range(KT):
                        ins = pe.transpose(bank(4 + t // 4, t % 4 * P, t % 4 * P + P), self.sc[:, i % 4, t * P:(t + 1) * P],
                                           ident[:, :])
                    ins.then_inc(c_tp.sem, 1)
                elif what == "sum":
                    pe.wait_ge(c_pT.sem, c_pT.at(0, 4 * i + 4))
                    if i:
                        pe.wait_ge(c_o.sem, c_o.at(0, i))
                    r = i % PR
                    for t in range(KT):
                        for j in range(2):
                            ins = pe.matmul(ps[HW * j:HW * j + HW, 6, 0:S], self.v[:, t, (2 * r + j) * HW:(2 * r + j + 1) * HW],
                                            self.pT[:, i % 2, j, t, :], start=(t == 0), stop=(t == KT - 1),
                                            skip_group_check=True)
                    ins.then_inc(c_av.sem, 1)
                else:
                    b = i
                    pe.wait_ge(c_o.sem, c_o.at(0, PR * (b + 1)))
                    for k in range(2):
                        for r in range(PR):
                            ins = pe.matmul(bank(6, k * D, k * D + D), self.oT[:, r, k * P:(k + 1) * P],
                                            self.wo[:, r * D:(r + 1) * D], start=(r == 0), stop=(r == PR - 1))
                    ins.then_inc(c_y.sem, 1)
                    pe.wait_ge(c_y_out.sem, c_y_out.at(0, b + 1))

        def scalar(self, act):
            for half in range(2):
                for c in range(2):
                    act.wait_ge(ln_tp.sem, ln_tp.at(7 + half, c + 1))
                    act.copy(self.kvT[:, 2 * half + c, 0:S2], bank(6 + c)).then_inc(c_kvT.sem, 1)
            for i in range(4):
                act.wait_ge(c_m_mm.sem, c_m_mm.at(0, i + 1))
                act.mul(self.mqk[:, 4 * i:4 * i + 4, :].rearrange("p h n -> p (h n)"), bank(i),
                        float(HW) ** -0.5).then_inc(c_m_sb.sem, 1)
            for c in range(2):
                act.wait_ge(ln_tp.sem, ln_tp.at(10, c + 1))
                act.copy(self.kvT[:, 2 * c:2 * c + 2, S2:KV],
                         bank(6 + c).rearrange("p (b n) -> p b n", b=2)).then_inc(c_kvT.sem, 1)
            for what, i in self.order():
                if what == "v":
                    b, kt, half = i // (2 * KT), i // 2 % KT, i % 2
                    act.wait_ge(c_v_mm.sem, c_v_mm.at(0, i + 1))
                    if i % (2 * KT) == 0 and b:
                        act.wait_ge(c_av.sem, c_av.at(0, PR * b))
                    act.copy(self.v[:, kt, half * 512:half * 512 + 512], bank(4 + i % 2)).then_inc(c_v_sb.sem, 1)
                elif what == "q":
                    act.wait_ge(c_q_mm.sem, c_q_mm.at(0, i + 1))
                    if i >= 2:
                        act.wait_ge(c_s_mm.sem, c_s_mm.at(0, 4 * (i - 1)))
                    act.copy(self.qT[:, i % 2, :, :], bank(7).rearrange("p (j q) -> p j q", j=2)).then_inc(c_q_sb.sem, 1)
                elif what == "score":
                    act.wait_ge(c_neg.sem, c_neg.at(0, i + 1))
                    act.activation(self.sc[:, i % 4, :], self.sc[:, i % 4, :], ACT.Exp, bias=self.neg[:, i % 4:i % 4 + 1],
                                   accum_out=self.tot[:, i % 4:i % 4 + 1]).then_inc(c_exp.sem, 1)
                elif what == "turn":
                    g, j, k = i // 4, i // 2 % 2, i % 2
                    act.wait_ge(c_tp.sem, c_tp.at(0, i + 1))
                    if i % 4 == 0 and g >= 2:
                        act.wait_ge(c_av.sem, c_av.at(0, g - 1))
                    act.copy(self.pT[:, g % 2, j, :, k * P:(k + 1) * P],
                             ps[:, 4:6, :].rearrange("p b n -> p (b n)")[:, 0:KV].rearrange("p (t n) -> p t n", n=P)
                             ).then_inc(c_pT.sem, 1)
                elif what == "sum":
                    act.wait_ge(c_av.sem, c_av.at(0, i + 1))
                    if i % PR == 0 and i:
                        act.wait_ge(c_y.sem, c_y.at(0, i // PR))
                    act.copy(self.oT[:, i % PR, :], bank(6, 0, S)).then_inc(c_o.sem, 1)

        def vector(self, dve):
            dve.wait_ge(c_in.sem, c_in.at(0, 6))
            do = lambda ins: link(dve, dchain, ins)
            do(dve.memset(self.maskb[:, :, S2:KV], 0.0))
            dve.tensor_scalar(self.maskb[:, :, 0:S2], self.mask_raw.rearrange("p (b n) -> p b n", b=B), 0.0, -BIG,
                              ALU.is_equal, ALU.mult).then_inc(c_mask.sem, 1)
            for half in range(2):
                c = self.ctx_tm[:, 8 * half:8 * half + 8, :]
                norm_vector(dve, 7 + half, src=c, dst=c, affine=("L2_xattn_gm", "L2_xattn_bm"))
            norm_vector(dve, 9)
            dve.wait_ge(ln_h.sem, ln_h.at(9, 1))
            norm_vector(dve, 10, src=h, affine=("L2_xattn_gl", "L2_xattn_bl"))
            dve.wait_ge(c_mask.sem, c_mask.at(0, 1))
            for what, i in self.order():
                if what == "score":
                    b, s = i // (4 * PR), i % 4
                    dve.wait_ge(c_s_mm.sem, c_s_mm.at(0, i + 1))
                    if i >= 4:
                        dve.wait_ge(c_tp.sem, c_tp.at(0, i - 3))
                        dve.wait_ge(c_neg.sem, c_neg.at(0, i - 3))
                    src = ps[:, i % 2 * 2:i % 2 * 2 + 2, :].rearrange("p b n -> p (b n)")[:, 0:KV]
                    dve.tensor_tensor_reduce(self.sc[:, s, :], src, self.maskb[:, b, :], 1.0, -3.0e38,
                                             ALU.add, ALU.max, self.top[:, s:s + 1]).then_inc(c_max.sem, 1)
                    dve.wait_ge(c_max.sem, c_max.at(0, i + 1))
                    dve.tensor_scalar(self.neg[:, s:s + 1], self.top[:, s:s + 1], -1.0, None,
                                      ALU.mult).then_inc(c_neg.sem, 1)
                    if i:
                        self.inv_vector(dve, i - 1)
                    if i == UN - 1:
                        self.inv_vector(dve, i)
                elif what == "y":
                    b = i
                    dve.wait_ge(c_y.sem, c_y.at(0, b + 1))
                    xb = x[:, 2 * b:2 * b + 2, :]
                    dve.tensor_tensor(xb, xb, bank(6, 0, S).rearrange("p (t d) -> p t d", d=D),
                                      ALU.add).then_inc(c_y_out.sem, 1)
            dve.wait_ge(c_y_out.sem, c_y_out.at(0, B))

        def inv_vector(self, dve, i):
            dve.wait_ge(c_exp.sem, c_exp.at(0, i + 1))
            if i >= 4:
                dve.wait_ge(c_div.sem, c_div.at(0, i - 3))
            dve.reciprocal(self.inv[:, i % 4:i % 4 + 1], self.tot[:, i % 4:i % 4 + 1]).then_inc(c_inv.sem, 1)

        def gpsimd(self, pool):
            for n in (7, 8, 9, 10):
                norm_gpsimd(pool, n)
            for i in range(UN):
                pool.wait_ge(c_inv.sem, c_inv.at(0, i + 1))
                pool.tensor_scalar(self.sc[:, i % 4, :], self.sc[:, i % 4, :], self.inv[:, i % 4:i % 4 + 1], None,
                                   ALU.mult).then_inc(c_div.sem, 1)
                pool.wait_ge(c_div.sem, c_div.at(0, i + 1))
            pool.wait_ge(x_done.sem, x_done.at(self.sub, 1))
            link(pool, pchain, pool.memset(qs[:, :].bitcast(F32), 0.0))
            link(pool, pchain, pool.memset(ks[:, :].bitcast(F32), 0.0))
            pool.memset(ks[MAXROW:MAXROW + 3, :], 1.0).then_inc(rows_again.sem, 1)
            pool.wait_ge(rows_again.sem, rows_again.at(0, 1))
    rows_again = counter("rows_again", [1])

    f_in = counter("f_in", [2], 16)
    f_abs = counter("f_abs", [2])
    f_tot = counter("f_tot", [2])
    f_wq = counter("f_wq", [2])
    f_q = counter("f_q", [NT])
    f_tp = counter("f_tp", [2])
    f_qT = counter("f_qT", [2])
    f_h = counter("f_h", [NT])
    f_z = counter("f_z", [NT])
    f_g = counter("f_g", [NT])
    f_hq = counter("f_hq", [NT])
    f_htp = counter("f_htp", [NT])
    f_hT = counter("f_hT", [NT])
    f_y = counter("f_y", [NT])
    f_done = counter("f_done", [NT])
    FH = 4 * D
    ROUND = 1.5 * 2.0 ** 23

    class Ternary:
        sub, norm, name = 11, 14, "L3_ffn"
        w1 = tmp[:, 0:FH]
        w2 = tmp[:, FH:2 * FH]
        wtmp = tmp[:, 1024:1536]
        wint = tmp[:, 1536:2048].bitcast(BF16).rearrange("p (w n) -> p w n", w=2)
        z = tmp[:, 2048:3072].rearrange("p (s n) -> p s n", s=2)
        zi = tmp[:, 3072:3584].bitcast(BF16).rearrange("p (s n) -> p s n", s=2)
        ziT = tmp[:, 3584:4096].bitcast(BF16).rearrange("p (s n) -> p s n", s=2)
        hi = tmp[:, 4096:4608].bitcast(BF16).rearrange("p (t n) -> p t n", t=NT)
        hiT = tmp[:, 4608:5120].bitcast(BF16)
        y = tmp[:, 5120:5376].rearrange("p (s n) -> p s n", s=2)
        c = r1[:, :, :].rearrange("p t e -> p (t e)")
        ones = tmp[:, 5376:5504]

        def sync(self, sp):
            sp.wait_ge(x_done.sem, x_done.at(self.sub - 1, 1))
            sp.dma_start(self.w1, a["L3_ffn_w1"]).then_inc(f_in.sem, 16)
            sp.dma_start(self.w2, a["L3_ffn_w2"]).then_inc(f_in.sem, 16)

        def gpsimd(self, pool):
            pass

        def col(self, i, n=1):
            return self.c[:, i:i + n]

        def tensor(self, pe):
            for k in range(2):
                pe.wait_ge(f_abs.sem, f_abs.at(0, k + 1))
                pe.matmul(bank(0, k, k + 1), self.ones, self.col(k), start=True, stop=True).then_inc(f_tot.sem, 1)
                pe.wait_ge(f_wq.sem, f_wq.at(0, k + 1))
            for t in range(NT):
                pe.wait_ge(f_q.sem, f_q.at(0, t + 1))
                ins = pe.transpose(bank(6).bitcast(BF16)[:, t * P:(t + 1) * P], self.hi[:, t, :], identb[:, :])
                if t % 4 == 3:
                    ins.then_inc(f_tp.sem, 1)
                    pe.wait_ge(f_qT.sem, f_qT.at(0, t // 4 + 1))
            for t in range(NT + 2):
                if t < NT:
                    if t >= 2:
                        pe.wait_ge(f_z.sem, f_z.at(0, t - 1))
                    pe.matmul(bank(t % 2), self.hiT[:, t * P:(t + 1) * P], self.wint[:, 0, :],
                              start=True, stop=True).then_inc(f_h.sem, 1)
                if 0 <= t - 1 < NT:
                    q = t - 1
                    pe.wait_ge(f_hq.sem, f_hq.at(0, q + 1))
                    if q >= 2:
                        pe.wait_ge(f_hT.sem, f_hT.at(0, q - 1))
                    for j in range(4):
                        ins = pe.transpose(bank(2 + q % 2).bitcast(BF16)[:, j * P:(j + 1) * P],
                                           self.zi[:, q % 2, j * P:(j + 1) * P], identb[:, :])
                    ins.then_inc(f_htp.sem, 1)
                if 0 <= t - 2:
                    q = t - 2
                    pe.wait_ge(f_hT.sem, f_hT.at(0, q + 1))
                    if q >= 2:
                        pe.wait_ge(f_done.sem, f_done.at(0, q - 1))
                    for j in range(4):
                        ins = pe.matmul(bank(4 + q % 2, 0, D), self.ziT[:, q % 2, j * P:(j + 1) * P],
                                        self.wint[:, 1, j * D:(j + 1) * D], start=(j == 0), stop=(j == 3))
                    ins.then_inc(f_y.sem, 1)

        def scalar(self, act):
            for c in range(2):
                act.wait_ge(f_tp.sem, f_tp.at(0, c + 1))
                act.copy(self.hiT[:, c * 512:c * 512 + 512],
                         bank(6).bitcast(BF16)[:, c * 512:c * 512 + 512]).then_inc(f_qT.sem, 1)
            for t in range(NT + 1):
                if t < NT:
                    act.wait_ge(f_z.sem, f_z.at(0, t + 1))
                    act.activation(self.z[:, t % 2, :], self.z[:, t % 2, :], ACT.Gelu).then_inc(f_g.sem, 1)
                if t:
                    q = t - 1
                    act.wait_ge(f_htp.sem, f_htp.at(0, q + 1))
                    if q >= 2:
                        act.wait_ge(f_y.sem, f_y.at(0, q - 1))
                    act.copy(self.ziT[:, q % 2, :], bank(2 + q % 2).bitcast(BF16)[:, 0:FH]).then_inc(f_hT.sem, 1)

        def quantize(self, do, dve, src, out, cols):
            big, inv, scale = cols
            do(dve.tensor_reduce(big, src, AX.X, ALU.max, apply_absolute_value=True))
            do(dve.tensor_scalar(big, big, EPS, None, ALU.max))
            do(dve.reciprocal(inv, big))
            do(dve.tensor_scalar(inv, inv, 127.0, None, ALU.mult))
            do(dve.tensor_scalar(scale, big, 1.0 / 127.0, None, ALU.mult))
            do(dve.tensor_scalar(src, src, inv, ROUND, ALU.mult, ALU.add))
            return dve.tensor_scalar(out, src, ROUND, None, ALU.subtract)

        def vector(self, dve):
            do = lambda ins: link(dve, dchain, ins)
            do(dve.memset(self.ones, 1.0))
            dve.wait_ge(f_in.sem, f_in.at(0, 2))
            for k, wgt in enumerate((self.w1, self.w2)):
                dve.tensor_reduce(self.col(k), wgt, AX.X, ALU.add, apply_absolute_value=True).then_inc(f_abs.sem, 1)
                dve.wait_ge(f_tot.sem, f_tot.at(0, k + 1))
                s, inv = self.col(2 + k), self.col(4)
                do(dve.tensor_scalar(s, bank(0, k, k + 1), 1.0 / (D * FH), EPS, ALU.mult, ALU.max))
                do(dve.reciprocal(inv, s))
                do(dve.tensor_scalar(self.wtmp, wgt, inv, ROUND, ALU.mult, ALU.add))
                do(dve.tensor_scalar(self.wtmp, self.wtmp, ROUND, 1.0, ALU.subtract, ALU.min))
                dve.tensor_scalar(self.wint[:, k, :], self.wtmp, -1.0, None, ALU.max).then_inc(f_wq.sem, 1)
                dve.wait_ge(f_wq.sem, f_wq.at(0, k + 1))
            for t in range(NT):
                self.quantize(do, dve, h[:, t, :], self.hi[:, t, :],
                              (self.col(5), self.col(6), self.col(16 + t))).then_inc(f_q.sem, 1)
                dve.wait_ge(f_q.sem, f_q.at(0, t + 1))
                do(dve.tensor_tensor(self.col(16 + t), self.col(16 + t), self.col(2), ALU.mult))
            for t in range(NT + 2):
                if t < NT:
                    dve.wait_ge(f_h.sem, f_h.at(0, t + 1))
                    dve.tensor_scalar(self.z[:, t % 2, :], bank(t % 2), self.col(16 + t), None,
                                      ALU.mult).then_inc(f_z.sem, 1)
                if 0 <= t - 1 < NT:
                    q = t - 1
                    dve.wait_ge(f_g.sem, f_g.at(0, q + 1))
                    if q >= 2:
                        dve.wait_ge(f_htp.sem, f_htp.at(0, q - 1))
                    self.quantize(do, dve, self.z[:, q % 2, :], self.zi[:, q % 2, :],
                                  (self.col(5), self.col(6), self.col(32 + q))).then_inc(f_hq.sem, 1)
                    dve.wait_ge(f_hq.sem, f_hq.at(0, q + 1))
                    do(dve.tensor_tensor(self.col(32 + q), self.col(32 + q), self.col(3), ALU.mult))
                if 0 <= t - 2:
                    q = t - 2
                    dve.wait_ge(f_y.sem, f_y.at(0, q + 1))
                    dve.scalar_tensor_tensor(out=x[:, q, :], in0=bank(4 + q % 2, 0, D), scalar=self.col(32 + q),
                                             in1=x[:, q, :], op0=ALU.mult, op1=ALU.add).then_inc(f_done.sem, 1)
            dve.wait_ge(f_done.sem, f_done.at(0, NT))

    clip_sb = wring[:, :, :].rearrange("p s n -> p (s n)")[:, 0:12 * P].rearrange("p (s n) -> p s n", s=4)
    tri = sb("tri", [P, P])
    lat = wring[0:64, 0, 0:T]
    y_out = counter("y_out", [B] * len(ATTN))

    attn = [Attention(0, 0), Attention(1, 1), Attention(2, 3), Attention(3, 12), Attention(4, 13)]
    subs = {t.sub: t for t in attn}
    mixtures = {t.sub: t for t in (Mixture(0, 2), Mixture(1, 5), Mixture(2, 11))}
    others = {t.sub: t for t in (Gathered(), Linear(), Latents(), Ternary())}
    norm_of = {s: (s if s < 8 else s + 3) for s in range(N_SUB)}
    n_loads = [0]

    block = ctx.enter_context(nc.Block())

    @block.sync
    def _(sp):
        for dst, src in ((x[:, :, :], a["x"].rearrange("(t p) d -> p t d", p=P)), (ident[:, :], a["ident"]),
                         (w[:, :], a["w"]), (bcol[:, :], a["bcol"]),
                         (brow[:, :, :], a["brow"].unsqueeze(0).to_broadcast([P, len(R_OF), D])),
                         (ctxT[:, :], a["ctxT"]), (sumsel[:, :], a["sumsel"]), (tri[:, :], a["tri"]),
                         (mrow_raw[:, :], a["mask_row"]), (gatew[:, :], a["gates"]), (b1c[:, :], a["b1"]),
                         (b2r[:, :], a["b2"]), (down[:, :], a["order"]), (bmask[:, :], a["bmask"]), (vmask[:, :], a["vmask"]),
                         (m3a_raw[:, :, :, :], a["mask_L3a"].rearrange("w (t p) k -> p w t k", p=P)),
                         (m3x_raw[:, 0:2 * S2].rearrange("p (t k) -> p t k", t=2), a["mask_L3x"].rearrange("(t p) k -> p t k", p=P)),
                         (m3x_raw[:, 2 * S2:].rearrange("p (t k) -> p t k", t=4), a["mask_L3xT"].rearrange("(t p) k -> p t k", p=P))):
            sp.dma_start(dst, src).then_inc(loaded, 16)
        for s in range(N_SUB_RUN):
            if s in subs:
                subs[s].stack_sync(sp)
                subs[s].maxima_sync(sp)
            elif s in mixtures:
                mixtures[s].sync(sp)
            elif s in others:
                others[s].sync(sp)
        sp.wait_ge(x_done.sem, x_done.at(N_SUB_RUN - 1, 1))
        sp.dma_start(a["out"].rearrange("(t p) d -> p t d", p=P), x[:, :, :]).then_inc(out_sem, 16)
        sp.wait_ge(out_sem, 16)

    LOADED = 16 * 18

    @block.gpsimd
    def _(pool):
        link(pool, pchain, pool.memset(mhalf[:, :], -0.5))
        link(pool, pchain, pool.memset(vaug[:, :, :, :, 8:32], 0.0))
        link(pool, pchain, pool.memset(vaug[:, :, :, :, 8:16], 1.0))
        link(pool, pchain, pool.memset(qs[32:64, :].bitcast(F32), 0.0))
        link(pool, pchain, pool.memset(qs[64:128, :].bitcast(F32), 0.0))
        link(pool, pchain, pool.memset(qs[MASKROW:MASKROW + 1, :], 1.0))
        for s in range(N_SUB_RUN):
            if s != 7:
                norm_gpsimd(pool, norm_of[s])
            if s in subs:
                t = subs[s]
                if t.bias:
                    bias_gpsimd(pool, s, norm_of[s], f"{t.name}_o")
                if t.n:
                    pool.wait_ge(b_mm.sem, b_mm.at(t.n - 1, G * units[t.n - 1]))
                if t.n == 2:
                    link(pool, pchain, pool.memset(qs[MASKROW:MASKROW + 1, :], 0.0))
                pool.memset(qs[MAXROW:MAXROW + 32, :].bitcast(F32), 0.0).then_inc(q_rows_clear.sem, 1)
                pool.wait_ge(q_rows_clear.sem, q_rows_clear.at(t.n, 1))
                t.gpsimd(pool)
            elif s in others:
                others[s].gpsimd(pool)

    @block.vector
    def _(dve):
        link(dve, dchain, dve.memset(ks[:, :].bitcast(F32), 0.0))
        dve.memset(ks[MAXROW:MAXROW + 3, :], 1.0).then_inc(consts, 1)
        dve.wait_ge(loaded, LOADED)
        dve.tensor_copy(identb[:, :], ident[:, :]).then_inc(consts, 1)
        dve.tensor_scalar(mrow[:, :], mrow_raw[:, :], -BIG, None, ALU.mult).then_inc(consts, 1)
        dve.tensor_scalar(m3a[:, :, :], m3a_raw[:, :, :, :].rearrange("p w t k -> p w (t k)"), 0.0, -BIG,
                          ALU.is_equal, ALU.mult).then_inc(consts, 1)
        dve.tensor_scalar(m3x[:, :, :], m3x_raw.rearrange("p (w k) -> p w k", w=2), 0.0, -BIG,
                          ALU.is_equal, ALU.mult).then_inc(consts, 1)
        dve.wait_ge(consts, CONSTS)
        for s in range(N_SUB_RUN):
            if s != 7:
                norm_vector(dve, norm_of[s])
            if s in subs:
                subs[s].project_vector(dve)
                subs[s].vector(dve)
                dve.wait_ge(y_out.sem, y_out.at(subs[s].n, B))
            elif s in mixtures:
                mixtures[s].vector(dve)
                dve.wait_ge(mixed.sem, mixed.at(mixtures[s].m, 2 * mixtures[s].runs))
            elif s in others:
                others[s].vector(dve)
            dve.engine_nop().then_inc(x_done.sem, 1)

    @block.scalar
    def _(act):
        for s in range(N_SUB_RUN):
            if s not in (7, 11):
                norm_scalar(act, norm_of[s])
            if s in subs:
                subs[s].project_scalar(act)
                subs[s].scalar(act)
            elif s in mixtures:
                mixtures[s].scalar(act)
            elif s in others:
                others[s].scalar(act)

    @block.tensor
    def _(pe):
        pe.wait_ge(consts, CONSTS)
        for s in range(N_SUB_RUN):
            if s not in (7, 11):
                norm_tensor(pe, norm_of[s])
            if s in subs:
                subs[s].project_tensor(pe)
                subs[s].tensor(pe)
            elif s in mixtures:
                mixtures[s].tensor(pe)
            elif s in others:
                others[s].tensor(pe)


CONSTS = 5
N_SUB_RUN = N_SUB


def layout(i):
    f = {}
    g = {k: np.asarray(v) for k, v in i.items()}
    f["x"] = g["x"].reshape(T, D)
    f["ident"] = np.eye(P, dtype=np.float32)
    wp = np.zeros((P, W_COLS * D), np.float32)

    def put(name, m, rows=slice(0, P)):
        wp[rows, W_OF[name] * D:W_OF[name] * D + m.shape[1]] = m

    def quads(m):
        o = np.zeros((4, 32, NQ, D), np.float32)
        o[:, :HD] = m.reshape(NQ, 4, HD, D).transpose(1, 2, 0, 3)
        return o.reshape(P, NQ * D)

    def tall(m):
        return m.reshape(m.shape[0], -1, P, D).transpose(0, 2, 1, 3).reshape(m.shape[0], P, -1)

    for k, nm in enumerate("qkv"):
        put(f"L0_attn_{nm}", g["L0_attn_W_qkv"][:, k * D:(k + 1) * D])
        put(f"L1_attn_{nm}", g["L1_attn_Wqkv"][k * D:(k + 1) * D].T)
        put(f"L3_xattn_{nm}", g[f"L3_xattn_W{nm}"].T)
        put(f"L1_xattn_{nm}", g[f"L1_xattn_W{nm}"].T)
        put(f"L2_attn_{nm}", g[f"L2_attn_W{nm}"])
    put("L0_attn_o", quads(g["L0_attn_W_proj"]))
    put("L0_xattn_q", g["L0_xattn_q_w"])
    put("L0_xattn_k", g["L0_xattn_kv_w"][:, :D])
    put("L0_xattn_v", g["L0_xattn_kv_w"][:, D:])
    put("L0_xattn_o", quads(g["L0_xattn_proj_w"]))
    put("L1_attn_o", quads(g["L1_attn_Wout"].T))
    put("L3_down", np.concatenate([g["L3_attn_Wq_down"].T, g["L3_attn_Wkv_down"].T], 1))
    put("L3_attn_q", g["L3_attn_Wq_up"].T, slice(0, 32))
    put("L3_attn_k", g["L3_attn_Wk_up"].T, slice(32, 64))
    put("L3_attn_v", g["L3_attn_Wv_up"].T, slice(32, 64))
    put("L3_attn_o", quads(g["L3_attn_Wout"].T))
    put("L3_xattn_o", quads(g["L3_xattn_Wo"].T))
    put("L1_xattn_o", g["L1_xattn_Wo"].T)
    put("L2_attn_o", g["L2_attn_Wo"])
    f["w"] = wp
    biases = dict(zip(("L0_attn_q", "L0_attn_k", "L0_attn_v"), g["L0_attn_b_qkv"].reshape(3, D)),
                  L0_attn_o=g["L0_attn_b_proj"], L0_xattn_q=g["L0_xattn_q_b"],
                  L0_xattn_k=g["L0_xattn_kv_b"][:D], L0_xattn_v=g["L0_xattn_kv_b"][D:],
                  L0_xattn_o=g["L0_xattn_proj_b"], zero=np.zeros(D, np.float32))
    for n in ("L1_xattn", "L2_attn", "L3_xattn"):
        for c in "qkvo":
            biases[f"{n}_{c}"] = g[f"{n}_b{c}"]
    for c in ("gm", "bm", "gl", "bl"):
        biases[f"L2_xattn_{c}"] = g[f"L2_xattn_{c}"]
    f["bcol"] = np.stack([biases[n] for n in C_OF], 1)
    f["brow"] = np.stack([biases[n] for n in R_OF])
    f["ctxT"] = g["ctx_1024"].reshape(TC, D).T
    sel = np.zeros((P, P), np.float32)
    for j in range(4):
        sel[32 * j + HD, 32 * j:32 * j + 32] = 1
    f["sumsel"] = sel
    f["tri"] = np.triu(np.ones((P, P), np.float32))
    f["mask_row"] = g["mask_BxS2_bk0"]
    m = g["L3_attn_mask"].reshape(S, S)
    f["mask_L3a"] = np.stack([m, m.T])
    m = g["mask_1x1xSxS2_if1"].reshape(S, S2)
    f["mask_L3x"], f["mask_L3xT"] = m, m.T
    f["ctxT_by_head"] = g["ctx_1024"].reshape(B, S2 // H, H, D).transpose(3, 0, 2, 1).reshape(D, TC)
    f["bmask"] = np.repeat(np.eye(H, dtype=np.float32), HD, 0)
    f["vmask"] = np.kron(np.eye(4, dtype=np.float32), np.ones((S2 // H, HD), np.float32))
    f["kv_mask"] = np.concatenate([np.repeat(f["bmask"], HD, 1), f["bmask"]], 1)
    angle = (np.float32(np.pi / 2) * np.arange(1, S + 1, dtype=np.float32) / np.float32(S)).astype(np.float64)
    sc = np.stack([np.sin(angle), np.cos(angle), -np.sin(angle), -np.cos(angle)], 1).astype(np.float32)
    f["trig"] = sc.reshape(2, P, 4).transpose(1, 0, 2).reshape(P, 8)
    f["ctx"] = g["ctx_1024"].reshape(TC, D)
    f["mask_L2x"] = g["mask_BxS2_bf1"].reshape(TC)
    for n in "qk":
        f[f"L2_xattn_{n}T"] = g[f"L2_xattn_W{n}"].reshape(D, H, 64).transpose(2, 1, 0).reshape(64, H * D)
    f["L2_xattn_v"] = g["L2_xattn_Wv"]
    f["L2_xattn_o"] = tall(g["L2_xattn_Wo"][None])[0]
    f["L3_ffn_w1"] = g["L3_ffn_w1"].T
    f["L3_ffn_w2"] = tall(g["L3_ffn_w2"].T[None])[0]
    f["gates"] = np.concatenate([g["L0_ffn_gate_w"], g["L1_ffn_gate_w"].T, g["L2_ffn_gate_w"].T], 1)
    f["order"] = np.tile(np.arange(32, 0, -1, dtype=np.float32), (P, 1))
    f["b1"] = g["L2_ffn_b1"].reshape(8, 4, P).transpose(2, 0, 1).reshape(P, 32)
    f["b2"] = g["L2_ffn_b2"]

    f["L0_ffn_up"] = np.concatenate(
        [np.concatenate([g[f"L0_ffn_shared_{n}_w"][None], g[f"L0_ffn_routed_{n}_w"]]) for n in ("gate", "up")], 2)
    f["L0_ffn_down"] = tall(np.concatenate([g["L0_ffn_shared_down_w"][None], g["L0_ffn_routed_down_w"]]))
    f["L1_ffn_up"] = np.concatenate([g["L1_ffn_w1"].transpose(0, 2, 1), g["L1_ffn_w3"].transpose(0, 2, 1)], 2)
    f["L1_ffn_down"] = tall(g["L1_ffn_w2"].transpose(0, 2, 1))
    f["L2_ffn_up"] = g["L2_ffn_w1"]
    f["L2_ffn_down"] = tall(g["L2_ffn_w2"])
    return {k: np.ascontiguousarray(v) for k, v in f.items()}


def kernel(**inputs):
    import concourse.bacc as bacc
    from concourse.bass_utils import run_bass_kernel_spmd

    nc = bacc.Bacc("TRN2", target_bir_lowering=False, num_devices=1)
    arrays = layout(inputs)
    a = {n: nc.dram_tensor(f"in_{n}", v.shape, mybir.dt.from_np(v.dtype), kind="ExternalInput").ap()
         for n, v in arrays.items()}
    a["out"] = nc.dram_tensor("out", (T, D), F32, kind="ExternalOutput").ap()
    with ExitStack() as ctx:
        program(nc, a, ctx)
    r = run_bass_kernel_spmd(nc, [{f"in_{n}": v for n, v in arrays.items()}], core_ids=[0])
    return r.results[0]["out"].reshape(B, S, D)
```

```python
from contextlib import ExitStack

import numpy as np

import concourse.bass as bass
from concourse import mybir

P = 128
B, S, D = 4, 256, 128
T = B * S
NT = T // P
S2 = 512
TC = B * S2
H, HD = 16, 8
NQ = H // 4
G = B * NQ
SCALE = float(HD) ** -0.5
BIG = float(2.0 ** 100)
EPS = 1e-5
TWO_ONES = float(np.array([0x3F803F80], np.uint32).view(np.float32)[0])

F32 = mybir.dt.float32
BF16 = mybir.dt.bfloat16
ALU = mybir.AluOpType
ACT = mybir.ActivationFunctionType
AX = mybir.AxisListType

TERMS = 6
Q_PART = [0, 0, 0, 1, 1, 2]
K_PART = [0, 1, 2, 0, 1, 0]
STACK = HD * TERMS
MAXROW = 64
MASKROW = 96

N_SUB = 12

ATTN = [
    dict(name="L0_attn", sub=0, cross=False, maximum=True, mask=None),
    dict(name="L0_xattn", sub=1, cross=True, maximum=True, mask="row"),
    dict(name="L1_attn", sub=3, cross=False, maximum=False, mask="causal"),
    dict(name="L3_attn", sub=9, cross=False, maximum=True, mask="full"),
    dict(name="L3_xattn", sub=10, cross=True, maximum=True, mask="full"),
]


W_OF = {}
W_COLS = 0
for _name, _n in ([(f"{a}_{w}", n) for a in ("L0_attn", "L0_xattn", "L1_attn", "L3_attn", "L3_xattn")
                   for w, n in (("q", 1), ("k", 1), ("v", 1), ("o", NQ))]
                  + [("L3_down", 1)]
                  + [(f"{a}_{w}", 1) for a in ("L1_xattn", "L2_attn") for w in "qkvo"]):
    W_OF[_name] = W_COLS
    W_COLS += _n
C_OF = {n: i for i, n in enumerate([
    "L0_attn_q", "L0_attn_k", "L0_xattn_q", "L0_xattn_k", "L3_xattn_q", "L3_xattn_k",
    "L1_xattn_q", "L1_xattn_k", "zero"])}
R_OF = {n: i for i, n in enumerate([
    "L0_attn_v", "L0_attn_o", "L0_xattn_v", "L0_xattn_o", "L3_xattn_v", "L3_xattn_o",
    "L1_xattn_v", "L1_xattn_o", "L2_attn_q", "L2_attn_k", "L2_attn_v", "L2_attn_o",
    "L2_xattn_gm", "L2_xattn_bm", "L2_xattn_gl", "L2_xattn_bl"])}


class Count:

    def __init__(self, sem, totals, step=1):
        self.sem, self.totals, self.step = sem, list(totals), step

    def at(self, use, n):
        return self.step * (sum(self.totals[:use]) + n)


def program(nc, a, ctx):
    sb = lambda name, shape, dt=F32: ctx.enter_context(nc.sbuf_tensor(name, shape, dt))
    new = lambda name: ctx.enter_context(nc.semaphore(name))
    counter = lambda name, totals, step=1: Count(new(name), totals, step)

    x = sb("x", [P, NT, D])
    h = sb("h", [P, NT, D])
    hT = sb("hT", [P, T])
    ctxT = sb("ctxT", [P, TC])
    w = sb("w", [P, W_COLS * D])
    bcol = sb("bcol", [P, len(C_OF)])
    brow = sb("brow", [P, len(R_OF), D])
    ident = sb("ident", [P, P])
    identb = sb("identb", [P, P], BF16)
    qs = sb("qs", [P, G * 4 * S], BF16)
    ks = sb("ks", [P, G * 4 * S], BF16)
    probs = sb("probs", [P, 2, 4, 2 * S2])
    v = sb("v", [P, TC // P, D])
    vaug = sb("vaug", [P, 2, 4, 4, 32])
    osb = sb("osb", [P, 2, S])
    rsum = sb("rsum", [P, 2 * 4])
    o = sb("o", [P, 2, D])
    oT = sb("oT", [P, S])
    mx = sb("mx", [P, 2, 8])
    mres = sb("mres", [P, 2, 8])
    mpart = sb("mpart", [P, 2, 2, 3, 4], BF16)
    mT = sb("mT", [P, 2, S], BF16)
    stats = sb("stats", [P, NT, 6])
    mv = sb("mv", [P, NT, 2])
    rstd = sb("rstd", [P, NT])
    veps = sb("veps", [P, NT])
    mhalf = sb("mhalf", [P, NT])
    tmp = probs[:, :, :, :].rearrange("p s j n -> p (s j n)")
    parts_at = tmp[:, 6 * 512:].bitcast(BF16)
    qpart = parts_at[:, 0:3 * T].rearrange("p (k n) -> p k n", k=3)
    kpart = parts_at[:, 3 * T:3 * (T + TC)].rearrange("p (k n) -> p k n", k=3)
    ps = ctx.enter_context(nc.psum_tensor("ps", [P, 8, 512], F32))
    scr_q = nc.dram_tensor("scr_q", [TERMS, D, T], BF16, kind="Internal").ap()
    scr_k = nc.dram_tensor("scr_k", [3, D, TC], BF16, kind="Internal").ap()
    mrow_raw = sb("mrow_raw", [B, S2], mybir.dt.uint8)
    mrow = sb("mrow", [B, S2], BF16)
    m3a_raw = sb("m3a_raw", [P, 2, 2, S], mybir.dt.uint8)
    m3a = sb("m3a", [P, 2, 2 * S], BF16)
    wring2 = sb("wring2", [P, 2, 1536])
    m3x_raw = wring2[:, :, :].rearrange("p s n -> p (s n)")[:, 0:4 * S2].bitcast(mybir.dt.int32)
    m3x = sb("m3x", [P, 2, 2 * S2], BF16)

    def wt(name, n=1):
        c = W_OF[name] * D
        return w[:, c:c + n * D]

    def bank(i, lo=0, hi=512):
        return ps[:, i, lo:hi]

    A = range(len(ATTN))
    kt_n = [4 if c["cross"] else 2 for c in ATTN]
    units = [8 if c["cross"] else 4 for c in ATTN]
    chunks = [6 if c["cross"] else 4 for c in ATTN]
    vgroups = [4 if c["cross"] else 2 for c in ATTN]
    maxed = [int(c["maximum"]) for c in ATTN]
    first_in = new("first_in")
    loaded = new("loaded")
    consts = new("consts")
    dchain, achain, pchain = new("dve_chain"), new("act_chain"), new("pool_chain")
    norms = 15
    ln_var = counter("ln_var", [1] * norms)
    ln_rstd = counter("ln_rstd", [1] * norms)
    ln_h = counter("ln_h", [1] * norms)
    ln_tp = counter("ln_tp", [0 if n in (9, 14) else 2 for n in range(norms)])
    ln_hT = counter("ln_hT", [0 if n in (7, 8, 9, 10, 14) else 2 for n in range(norms)])
    x_done = counter("x_done", [1] * N_SUB)
    biased = [0, 1, 4, 6, 10]
    x_biased = counter("x_biased", [1] * len(biased))
    lat_mm = counter("lat_mm", [2])
    lat_sb = counter("lat_sb", [2])
    proj_mm = counter("proj_mm", chunks)
    proj_f = counter("proj_f", chunks)
    proj_p1 = counter("proj_p1", chunks)
    proj_r = counter("proj_r", chunks)
    proj_p2 = counter("proj_p2", chunks)
    proj_p3 = counter("proj_p3", chunks)
    v_mm = counter("v_mm", vgroups)
    v_sb = counter("v_sb", vgroups)
    spilled = [counter(f"spilled{i}", [int(i < chunks[n]) for n in A], 48) for i in range(6)]
    stacked = [counter(f"stacked{b}", [1 for n in A], 64) for b in range(B)]
    mask_in = [counter(f"mask_in{b}", [2], 16) for b in range(2)]
    q_rows_clear = counter("q_rows_clear", [0, 1, 1, 1, 1])
    a_mm = counter("a_mm", [G * u * m for u, m in zip(units, maxed)])
    a_max = counter("a_max", [G * u * m for u, m in zip(units, maxed)])
    m_split = counter("m_split", [G * m for m in maxed])
    m_tp = counter("m_tp", [G * m for m in maxed])
    m_sb = counter("m_sb", [G * m for m in maxed])
    m_in = [counter(f"m_in{i}", [G // 4 * m for m in maxed], 48) for i in range(4)]
    b_mm = counter("b_mm", [G * u for u in units])
    clipped = counter("clipped", [G * u * (1 - m) for u, m in zip(units, maxed)])
    p_exp = counter("p_exp", [G * u for u in units])
    p_cut = counter("p_cut", [G * 4 * (1 - m) for u, m in zip(units, maxed)])
    va_set = counter("va_set", [G] * len(ATTN))
    av_mm = counter("av_mm", [G] * len(ATTN))
    o_sb = counter("o_sb", [G] * len(ATTN))
    o_tp = counter("o_tp", [G] * len(ATTN))
    oT_tp = counter("oT_tp", [B] * len(ATTN))
    oT_sb = counter("oT_sb", [B] * len(ATTN))
    o_div = counter("o_div", [G] * len(ATTN))
    y_mm = counter("y_mm", [B] * len(ATTN))
    written = new("written")

    chained = {}

    def link(eng, sem, ins):
        ins.then_inc(sem, 1)
        chained[sem.name] = chained.get(sem.name, 0) + 1
        eng.wait_ge(sem, chained[sem.name])

    def made(n):
        return {6: 8, 7: 6, 8: 7}.get(n, n)

    def norm_vector(dve, n, src=x, dst=h, affine=None):
        for j in range(NT):
            dve.bn_stats(stats[:, j, :], src[:, j, :]).then_inc(dchain, 1)
            chained[dchain.name] = chained.get(dchain.name, 0) + 1
        dve.wait_ge(dchain, chained[dchain.name])
        for j in range(NT):
            ins = dve.bn_aggr(mv[:, j, :], stats[:, j, :])
        link(dve, dchain, ins)
        dve.tensor_scalar(veps[:, :], mv[:, :, 1], EPS, None, ALU.add).then_inc(ln_var.sem, 1)
        dve.wait_ge(ln_rstd.sem, ln_rstd.at(made(n), 1))
        for j in range(NT):
            ins = dve.tensor_scalar(dst[:, j, :], src[:, j, :], mv[:, j, 0:1], rstd[:, j:j + 1],
                                    ALU.subtract, ALU.mult)
        if affine:
            for name, op in zip(affine, (ALU.mult, ALU.add)):
                link(dve, dchain, ins)
                ins = dve.tensor_tensor(dst[:, :, :], dst[:, :, :], brow[:, R_OF[name], :].unsqueeze(1).to_broadcast([P, NT, D]), op)
        ins.then_inc(ln_h.sem, 1)

    def norm_gpsimd(pool, n):
        pool.wait_ge(ln_var.sem, ln_var.at(made(n), 1))
        pool.tensor_tensor(rstd[:, :], veps[:, :], mhalf[:, :], ALU.pow).then_inc(ln_rstd.sem, 1)
        pool.wait_ge(ln_rstd.sem, ln_rstd.at(made(n), 1))

    def norm_tensor(pe, n, src=h, after=None):
        pe.wait_ge(ln_h.sem, ln_h.at(made(n), 1))
        if after:
            pe.wait_ge(*after)
        for j in range(NT):
            ins = pe.transpose(bank(6 + j // 4, j % 4 * P, j % 4 * P + P), src[:, j, :], ident[:, :])
            if j % 4 == 3:
                ins.then_inc(ln_tp.sem, 1)

    def norm_scalar(act, n):
        for c in range(2):
            act.wait_ge(ln_tp.sem, ln_tp.at(n, c + 1))
            act.copy(hT[:, c * 512:c * 512 + 512], bank(6 + c)).then_inc(ln_hT.sem, 1)

    def bias_gpsimd(pool, sub, n, name):
        pool.wait_ge(ln_h.sem, ln_h.at(made(n), 1))
        pool.tensor_tensor(x[:, :, :], x[:, :, :],
                           brow[:, R_OF[name], :].unsqueeze(1).to_broadcast([P, NT, D]),
                           ALU.add).then_inc(x_biased.sem, 1)
        pool.wait_ge(x_biased.sem, x_biased.at(biased.index(sub), 1))

    class Attention:
        def __init__(self, n, norm):
            c = ATTN[n]
            self.n, self.norm, self.name, self.sub = n, norm, c["name"], c["sub"]
            self.cross, self.maximum, self.mask = c["cross"], c["maximum"], c["mask"]
            self.kt, self.u, self.nch, self.nv = kt_n[n], units[n], chunks[n], vgroups[n]
            self.keys = self.kt * P
            self.low_rank = self.name == "L3_attn"
            self.kin = ctxT if self.cross else hT
            self.lag = 3 if self.maximum else 0
            self.bias = f"{self.name}_q" in C_OF
            self.chunk_order = [0, 2, 3, 1, 4, 5] if self.cross else [0, 2, 1, 3]

        def qv(self, g, j):
            return qs[:, (4 * g + j) * S:(4 * g + j + 1) * S]

        def kv(self, g, j, lo=0, hi=None):
            at = (4 * g + j) % (G * 4 * S // self.keys) * self.keys
            return ks[:, at + lo:at + (hi or self.keys)]

        def chunk(self, i):
            return (True, i) if i < 2 else (False, i - 2)

        def project_tensor(self, pe):
            n = self.n
            if self.low_rank:
                for c in range(2):
                    pe.wait_ge(ln_hT.sem, ln_hT.at(self.norm, c + 1))
                    pe.matmul(bank(c)[0:64, :], wt("L3_down")[:, 0:64], hT[:, c * 512:c * 512 + 512],
                              start=True, stop=True).then_inc(lat_mm.sem, 1)
                for c in range(2):
                    pe.wait_ge(lat_sb.sem, lat_sb.at(0, c + 1))
            for i in self.chunk_order:
                query, c = self.chunk(i)
                if query or not self.cross:
                    pe.wait_ge(ln_hT.sem, ln_hT.at(self.norm, c + 1))
                cols = slice(c * 512, c * 512 + 512)
                if self.low_rank:
                    r = slice(0, 32) if query else slice(32, 64)
                    lhs, rhs = wt(f"{self.name}_{'q' if query else 'k'}")[r, :], lat[r, cols]
                else:
                    lhs = wt(f"{self.name}_{'q' if query else 'k'}")
                    rhs = (hT if query else self.kin)[:, cols]
                pe.matmul(bank(i), lhs, rhs, start=True, stop=True).then_inc(proj_mm.sem, 1)
            for c in range(self.nv):
                if c >= 2:
                    pe.wait_ge(v_sb.sem, v_sb.at(n, c - 1))
                else:
                    pe.wait_ge(ln_hT.sem, ln_hT.at(self.norm, 2))
                for t in range(4):
                    cols = slice((4 * c + t) * P, (4 * c + t + 1) * P)
                    if self.low_rank:
                        lhs, rhs = lat[32:64, cols], wt(f"{self.name}_v")[32:64, :]
                    else:
                        lhs, rhs = self.kin[:, cols], wt(f"{self.name}_v")
                    ins = pe.matmul(bank(6 + c % 2, t * P, t * P + P), lhs, rhs, start=True, stop=True)
                ins.then_inc(v_mm.sem, 1)

        def project_vector(self, dve):
            n = self.n
            if self.low_rank:
                for c in range(2):
                    dve.wait_ge(lat_mm.sem, lat_mm.at(0, c + 1))
                    dve.tensor_copy(lat[0:64, c * 512:c * 512 + 512], bank(c)[0:64, :]).then_inc(lat_sb.sem, 1)
            for at in range(self.nch + 2):
                if at < self.nch:
                    i = self.chunk_order[at]
                    query, c = self.chunk(i)
                    f = tmp[:, i * 512:i * 512 + 512]
                    col = C_OF[f"{self.name}_{'q' if query else 'k'}" if self.bias else "zero"]
                    dve.wait_ge(proj_mm.sem, proj_mm.at(n, at + 1))
                    dve.tensor_scalar(f, bank(i), bcol[:, col:col + 1], SCALE if query else 1.0,
                                      ALU.add, ALU.mult).then_inc(proj_f.sem, 1)
                if 0 <= at - 1 < self.nch:
                    i = self.chunk_order[at - 1]
                    f, (p1, _, _) = tmp[:, i * 512:i * 512 + 512], self.parts(i)
                    dve.wait_ge(proj_f.sem, proj_f.at(n, at))
                    dve.wait_ge(proj_p1.sem, proj_p1.at(n, at))
                    dve.tensor_tensor(f, f, p1, ALU.subtract).then_inc(proj_r.sem, 1)
                if 0 <= at - 2:
                    i = self.chunk_order[at - 2]
                    f, (_, p2, p3) = tmp[:, i * 512:i * 512 + 512], self.parts(i)
                    dve.wait_ge(proj_r.sem, proj_r.at(n, at - 1))
                    dve.wait_ge(proj_p2.sem, proj_p2.at(n, at - 1))
                    dve.tensor_tensor(p3, f, p2, ALU.subtract).then_inc(proj_p3.sem, 1)
            for c in range(self.nv):
                out = v[:, 4 * c:4 * c + 4, :]
                src = bank(6 + c % 2).rearrange("p (t d) -> p t d", d=D)
                dve.wait_ge(v_mm.sem, v_mm.at(n, c + 1))
                if self.bias:
                    b_v = brow[:, R_OF[f"{self.name}_v"], :].unsqueeze(1).to_broadcast([P, 4, D])
                    dve.tensor_tensor(out, src, b_v, ALU.add).then_inc(v_sb.sem, 1)
                else:
                    dve.tensor_copy(out, src).then_inc(v_sb.sem, 1)

        def parts(self, i):
            query, c = self.chunk(i)
            return [(qpart if query else kpart)[:, k, c * 512:c * 512 + 512] for k in range(3)]

        def project_scalar(self, act):
            n = self.n
            for at in range(self.nch + 1):
                if at < self.nch:
                    i = self.chunk_order[at]
                    act.wait_ge(proj_f.sem, proj_f.at(n, at + 1))
                    act.copy(self.parts(i)[0], tmp[:, i * 512:i * 512 + 512]).then_inc(proj_p1.sem, 1)
                if at >= 1:
                    i = self.chunk_order[at - 1]
                    act.wait_ge(proj_r.sem, proj_r.at(n, at))
                    act.copy(self.parts(i)[1], tmp[:, i * 512:i * 512 + 512]).then_inc(proj_p2.sem, 1)

        def stack_sync(self, sp):
            n = self.n
            for at, i in enumerate(self.chunk_order):
                query, c = self.chunk(i)
                sp.wait_ge(proj_p3.sem, proj_p3.at(n, at + 1))
                sp.wait_ge(proj_p2.sem, proj_p2.at(n, at + 1))
                cols = slice(c * 512, c * 512 + 512)
                for k, part in enumerate(self.parts(i)):
                    if query:
                        terms = [t for t in range(TERMS) if Q_PART[t] == k]
                        sp.dma_start(scr_q[terms[0]:terms[-1] + 1, :, cols].rearrange("t r n -> r t n"),
                                     part.unsqueeze(1).to_broadcast([P, len(terms), 512])).then_inc(spilled[i].sem, 16)
                    else:
                        sp.dma_start(scr_k[k, :, cols], part).then_inc(spilled[i].sem, 16)
                if at == 1:
                    self.load_sync(sp, 0)
            if not self.maximum:
                for b in range(1, B):
                    self.load_sync(sp, b)

        def load_sync(self, sp, b):
            n = self.n
            if n == 0 and b == 0:
                sp.wait_ge(consts, CONSTS)
            if n == 3 and b == 0:
                sp.wait_ge(rows_again.sem, rows_again.at(0, 1))
            if self.cross and b >= 2:
                sp.wait_ge(b_mm.sem, b_mm.at(n, (b - 1) * NQ * self.u))
            for query in (True, False):
                cols = S if query else self.keys
                i = b * cols // 512 + (0 if query else 2)
                sp.wait_ge(spilled[i].sem, spilled[i].at(n, 1))
                scr = (scr_q if query else scr_k)[:, :, b * cols:(b + 1) * cols]
                slot = b if query or not self.cross else b % 2
                at = slice(slot * H * cols, (slot + 1) * H * cols)
                for first, terms in (((0, TERMS),) if query else ((0, 3), (3, 2), (5, 1))):
                    dst = (qs if query else ks)[first * HD:(first + terms) * HD, at]
                    sp.dma_start(dst.rearrange("p (h k) -> p h k", h=H),
                                 scr[0:terms].rearrange("k (d h) n -> (k d) h n", h=H)).then_inc(stacked[b].sem, 16)
            if self.mask == "row":
                sp.dma_start(ks[MASKROW:MASKROW + 1, at].rearrange("p (h k) -> p h k", h=H),
                             mrow[b:b + 1, :].unsqueeze(1).to_broadcast([1, H, S2])).then_inc(mask_in[b % 2].sem, 16)

        def maxima_sync(self, sp):
            if not self.maximum:
                return
            for g in range(G):
                sp.wait_ge(m_sb.sem, m_sb.at(self.n, g + 1))
                for k in range(3):
                    sp.dma_start(qs[MAXROW + k:MAXROW + k + 1, 4 * g * S:4 * (g + 1) * S],
                                 mT[4 * k:4 * k + 4, g % 2, :]).then_inc(m_in[g % 4].sem, 16)
                if g in ((0, 5, 9) if self.cross else (0, 4, 8)):
                    self.load_sync(sp, (g + 7) // 4 if not self.cross or g == 0 else (g + 3) // 4)

        def a_tensor(self, pe, s, u):
            n, k = self.n, s * self.u + u
            if u == 0 and s % NQ == 0:
                pe.wait_ge(stacked[s // NQ].sem, stacked[s // NQ].at(n, 1))
                if self.mask == "row":
                    mask = mask_in[s // NQ % 2]
                    pe.wait_ge(mask.sem, mask.at(0, s // NQ // 2 + 1))
            if k == 0 and n:
                pe.wait_ge(q_rows_clear.sem, q_rows_clear.at(n, 1))
            if k >= 2:
                pe.wait_ge(a_max.sem, a_max.at(n, k - 1))
            full = self.mask == "full"
            if self.cross:
                j, qt = u // 2, u % 2
                if full:
                    pe.matmul(bank(k % 2), identb[:, :], m3x[:, 0, qt * S2:(qt + 1) * S2], start=True, stop=False)
                ins = pe.matmul(bank(k % 2), self.qv(s, j)[:, qt * P:(qt + 1) * P], self.kv(s, j),
                                start=not full, stop=True)
            else:
                for qt in range(2):
                    if full:
                        pe.matmul(bank(k % 2, qt * S, (qt + 1) * S), identb[:, :], m3a[:, 0, qt * S:(qt + 1) * S],
                                  start=True, stop=False)
                    ins = pe.matmul(bank(k % 2, qt * S, (qt + 1) * S), self.qv(s, u)[:, qt * P:(qt + 1) * P],
                                    self.kv(s, u), start=not full, stop=True)
            ins.then_inc(a_mm.sem, 1)

        def a_vector(self, dve, s, u):
            n, k = self.n, s * self.u + u
            if u == 0 and s >= 2:
                dve.wait_ge(m_split.sem, m_split.at(n, s - 1))
            dve.wait_ge(a_mm.sem, a_mm.at(n, k + 1))
            if self.cross:
                j, qt = u // 2, u % 2
                out, src = mx[:, s % 2, 4 * qt + j:4 * qt + j + 1], bank(k % 2)
            else:
                out = mx[:, s % 2, :].rearrange("p (t j) -> p j t", t=2)[:, u, :]
                src = bank(k % 2).rearrange("p (t k) -> p t k", t=2)
            dve.tensor_reduce(out, src, AX.X, ALU.max).then_inc(a_max.sem, 1)

        def split_gpsimd(self, pool, s):
            n = self.n
            m, r = (t[:, s % 2, :].rearrange("p (t j) -> p t j", t=2) for t in (mx, mres))
            part = lambda k: mpart[:, s % 2, :, k, :]
            do = lambda ins: link(pool, pchain, ins)
            if s >= 2:
                pool.wait_ge(m_tp.sem, m_tp.at(n, s - 1))
            pool.wait_ge(a_max.sem, a_max.at(n, (s + 1) * self.u))
            do(pool.tensor_scalar(r, m, -1.0, None, ALU.mult))
            do(pool.tensor_copy(part(0), r))
            do(pool.tensor_tensor(r, r, part(0), ALU.subtract))
            do(pool.tensor_copy(part(1), r))
            pool.tensor_tensor(part(2), r, part(1), ALU.subtract).then_inc(m_split.sem, 1)
            pool.wait_ge(m_split.sem, m_split.at(n, s + 1))

        def turn_tensor(self, pe, s):
            n = self.n
            pe.wait_ge(m_split.sem, m_split.at(n, s + 1))
            if s >= 1:
                pe.wait_ge(m_sb.sem, m_sb.at(n, s))
            for qt in range(2):
                ins = pe.transpose(bank(7).bitcast(BF16)[0:12, qt * P:(qt + 1) * P],
                                   mpart[:, s % 2, qt, :, :].rearrange("p k j -> p (k j)"), identb[:, :])
            ins.then_inc(m_tp.sem, 1)

        def turn_scalar(self, act, s):
            n = self.n
            act.wait_ge(m_tp.sem, m_tp.at(n, s + 1))
            if s >= 2:
                act.wait_ge(m_in[s % 4 - 2].sem, m_in[s % 4 - 2].at(n, (s - 2) // 4 + 1))
            act.copy(mT[0:12, s % 2, :], bank(7).bitcast(BF16)[0:12, 0:S]).then_inc(m_sb.sem, 1)

        def unit(self, u):
            return (u // 2, 2 * (u % 2)) if self.cross else (u, 0)

        def b_tensor(self, pe, s, u):
            n, k = self.n, s * self.u + u
            j, kt0 = self.unit(u)
            if u == 0:
                if self.maximum:
                    pe.wait_ge(m_in[s % 4].sem, m_in[s % 4].at(n, s // 4 + 1))
                elif s % NQ == 0:
                    pe.wait_ge(stacked[s // NQ].sem, stacked[s // NQ].at(n, 1))
            if k == 0 and not self.maximum:
                pe.wait_ge(q_rows_clear.sem, q_rows_clear.at(n, 1))
            if k >= 2:
                done = p_exp if self.maximum else clipped
                pe.wait_ge(done.sem, done.at(n, k - 1))
            full = self.mask == "full"
            mask = m3x[:, 1, kt0 * S:(kt0 + 2) * S] if self.cross else m3a[:, 1, :]
            for t in range(2):
                q0 = P if self.mask == "causal" and t else 0
                out = bank(2 + k % 2, t * S, (t + 1) * S - q0)
                if full:
                    pe.matmul(out, identb[:, :], mask[:, t * S:(t + 1) * S], start=True, stop=False)
                ins = pe.matmul(out, self.kv(s, j, (kt0 + t) * P, (kt0 + t + 1) * P), self.qv(s, j)[:, q0:S],
                                start=not full, stop=True)
            ins.then_inc(b_mm.sem, 1)

        def clip_vector(self, dve, s, u):
            n, k = self.n, s * self.u + u
            dve.wait_ge(b_mm.sem, b_mm.at(n, k + 1))
            if k >= 4:
                dve.wait_ge(p_exp.sem, p_exp.at(n, k - 3))
            dve.tensor_scalar(clip_sb[:, k % 4, :], bank(2 + k % 2, 0, 3 * P), 10.0, -10.0,
                              ALU.min, ALU.max).then_inc(clipped.sem, 1)

        def b_scalar(self, act, s, u):
            n, k = self.n, s * self.u + u
            j, kt0 = self.unit(u)
            if k == 0:
                for i in range(self.nch):
                    act.wait_ge(spilled[i].sem, spilled[i].at(n, 1))
            if u == 0 and s >= 2:
                act.wait_ge(av_mm.sem, av_mm.at(n, s - 1))
            if self.maximum:
                act.wait_ge(b_mm.sem, b_mm.at(n, k + 1))
                act.activation(probs[:, s % 2, j, kt0 * S:(kt0 + 2) * S], bank(2 + k % 2),
                               ACT.Exp).then_inc(p_exp.sem, 1)
            else:
                act.wait_ge(clipped.sem, clipped.at(n, k + 1))
                act.activation(probs[:, s % 2, j, 0:3 * P], clip_sb[:, k % 4, :], ACT.Exp).then_inc(p_exp.sem, 1)

        def cut_gpsimd(self, pool, s):
            n = self.n
            for j in range(4):
                pool.wait_ge(p_exp.sem, p_exp.at(n, s * self.u + j + 1))
                part = probs[:, s % 2, j, 0:4 * P].rearrange("p (t q) -> p t q", t=2)[:, :, 0:P]
                pool.tensor_tensor(part, part, tri[:, :].unsqueeze(1).to_broadcast([P, 2, P]),
                                   ALU.mult).then_inc(p_cut.sem, 1)
                pool.wait_ge(p_cut.sem, p_cut.at(n, 4 * s + j + 1))

        def values_gpsimd(self, pool, s):
            n, b, quad = self.n, s // NQ, s % NQ
            if s == 0:
                pool.wait_ge(v_sb.sem, v_sb.at(n, self.nv))
            if s >= 2:
                pool.wait_ge(av_mm.sem, av_mm.at(n, s - 1))
            src = v[:, b * self.kt:(b + 1) * self.kt, quad * 4 * HD:(quad + 1) * 4 * HD]
            pool.tensor_copy(vaug[:, s % 2, 0:self.kt, :, 0:HD],
                             src.rearrange("p t (j d) -> p t j d", j=4)).then_inc(va_set.sem, 1)
            pool.wait_ge(va_set.sem, va_set.at(n, s + 1))

        def av_tensor(self, pe, s, kt):
            n = self.n
            if kt == 0:
                pe.wait_ge(va_set.sem, va_set.at(n, s + 1))
                if s >= 2:
                    pe.wait_ge(o_sb.sem, o_sb.at(n, s - 1))
                done = p_exp if self.maximum else p_cut
                pe.wait_ge(done.sem, done.at(n, (s + 1) * (self.u if self.maximum else 4)))
            q0 = P if self.mask == "causal" and kt else 0
            for j in range(4):
                ins = pe.matmul(ps[32 * j:32 * j + 32, 4 + s % 2, q0:S], vaug[:, s % 2, kt, j, :],
                                probs[:, s % 2, j, kt * S:(kt + 1) * S - q0],
                                start=(kt == 0), stop=(kt == self.kt - 1), skip_group_check=True)
            if kt == self.kt - 1:
                ins.then_inc(av_mm.sem, 1)

        def o_scalar(self, act, s):
            n = self.n
            act.wait_ge(av_mm.sem, av_mm.at(n, s + 1))
            if s >= 2:
                act.wait_ge(o_tp.sem, o_tp.at(n, s - 1))
            act.copy(osb[:, s % 2, :], bank(4 + s % 2, 0, S)).then_inc(o_sb.sem, 1)

        def o_tensor(self, pe, s):
            n = self.n
            pe.wait_ge(o_sb.sem, o_sb.at(n, s + 1))
            if s >= 1:
                pe.wait_ge(o_div.sem, o_div.at(n, s))
            if s and s % NQ == 0:
                pe.wait_ge(y_out.sem, y_out.at(n, s // NQ))
            for t in range(2):
                ins = pe.transpose(bank(6, t * P, t * P + P), osb[:, s % 2, t * P:(t + 1) * P], ident[:, :])
            ins.then_inc(o_tp.sem, 1)

        def div_vector(self, dve, s):
            n, quad = self.n, s % NQ
            dve.wait_ge(o_tp.sem, o_tp.at(n, s + 1))
            if quad == 0 and s:
                dve.wait_ge(oT_tp.sem, oT_tp.at(n, s // NQ))
            src = bank(6, 0, S).rearrange("p (t j c) -> p t j c", t=2, j=4)
            link(dve, dchain, dve.reciprocal(rsum[:, :].rearrange("p (t j) -> p t j", t=2), src[:, :, :, HD]))
            for t in range(2):
                ins = dve.tensor_tensor(o[:, t, quad * 4 * HD:(quad + 1) * 4 * HD].rearrange("p (j d) -> p j d", j=4),
                                        src[:, t, :, 0:HD], rsum[:, 4 * t:4 * t + 4].unsqueeze(2).to_broadcast([P, 4, HD]),
                                        ALU.mult)
            ins.then_inc(o_div.sem, 1)

        def oT_tensor(self, pe, b):
            n = self.n
            pe.wait_ge(o_div.sem, o_div.at(n, NQ * (b + 1)))
            for t in range(2):
                ins = pe.transpose(bank(6, S + t * P, S + t * P + P), o[:, t, :], ident[:, :])
            ins.then_inc(oT_tp.sem, 1)

        def oT_scalar(self, act, b):
            n = self.n
            act.wait_ge(oT_tp.sem, oT_tp.at(n, b + 1))
            if b:
                act.wait_ge(y_mm.sem, y_mm.at(n, b))
            act.copy(oT[:, :], bank(6, S, 2 * S)).then_inc(oT_sb.sem, 1)

        def y_tensor(self, pe, b):
            n = self.n
            pe.wait_ge(oT_sb.sem, oT_sb.at(n, b + 1))
            for t in range(2):
                ins = pe.matmul(bank(6, S + t * P, S + (t + 1) * P), oT[:, t * P:(t + 1) * P], wt(f"{self.name}_o"),
                                start=True, stop=True)
            ins.then_inc(y_mm.sem, 1)

        def y_vector(self, dve, b):
            n = self.n
            dve.wait_ge(y_mm.sem, y_mm.at(n, b + 1))
            if b == 0 and self.bias:
                dve.wait_ge(x_biased.sem, x_biased.at(biased.index(self.sub), 1))
            xb = x[:, 2 * b:2 * b + 2, :]
            dve.tensor_tensor(xb, xb, bank(6, S, 2 * S).rearrange("p (t d) -> p t d", d=D),
                              ALU.add).then_inc(y_out.sem, 1)

        def order(self):
            for s in range(G + self.lag + 5):
                e, o, d = s - self.lag, s - self.lag - 1, s - self.lag - 2
                for u in range(self.u):
                    if self.maximum and s < G:
                        yield "a", s, u
                    if 0 <= e < G:
                        yield "b", e, u
                    if 0 <= o < G and u % 2:
                        yield "av", o, u // 2
                    if u == 0 and 0 <= d < G:
                        yield "div", d, 0
                    if u == 1 and 0 <= d < G and d % NQ == NQ - 1:
                        yield "oT", d // NQ, 0
                    if u == 3 and 0 <= d < G and d % NQ == NQ - 1:
                        yield "y", d // NQ, 0
                    if u == self.u // 2 and self.maximum and 0 <= s - 1 < G:
                        yield "turn", s - 1, 0
                if self.maximum and s < G:
                    yield "split", s, 0
                if 0 <= o < G:
                    yield "o", o, 0

        def tensor(self, pe):
            for what, s, u in self.order():
                if what == "a":
                    self.a_tensor(pe, s, u)
                elif what == "b":
                    self.b_tensor(pe, s, u)
                elif what == "av":
                    self.av_tensor(pe, s, u)
                elif what == "div":
                    self.o_tensor(pe, s)
                elif what == "oT":
                    self.oT_tensor(pe, s)
                elif what == "turn":
                    self.turn_tensor(pe, s)
                elif what == "y":
                    self.y_tensor(pe, s)

        def vector(self, dve):
            for what, s, u in self.order():
                if what == "a":
                    self.a_vector(dve, s, u)
                elif what == "b" and not self.maximum:
                    self.clip_vector(dve, s, u)
                elif what == "div":
                    self.div_vector(dve, s)
                elif what == "y":
                    self.y_vector(dve, s)

        def scalar(self, act):
            for what, s, u in self.order():
                if what == "b":
                    self.b_scalar(act, s, u)
                elif what == "o":
                    self.o_scalar(act, s)
                elif what == "oT":
                    self.oT_scalar(act, s)
                elif what == "turn":
                    self.turn_scalar(act, s)

        def gpsimd(self, pool):
            for what, s, u in self.order():
                if what == "b" and u == 0:
                    self.values_gpsimd(pool, s)
                if what == "split":
                    self.split_gpsimd(pool, s)
                elif what == "b" and u == self.u - 1 and self.mask == "causal":
                    self.cut_gpsimd(pool, s)

    MOES = [dict(name="L0_ffn", sub=2, experts=32, chunks=2, shared=1, choices=1, gate_at=0),
            dict(name="L1_ffn", sub=5, experts=8, chunks=4, shared=0, choices=2, gate_at=32),
            dict(name="L2_ffn", sub=8, experts=8, chunks=4, shared=0, choices=2, gate_at=40)]
    blocks = [m["choices"] * NT + m["experts"] - 1 for m in MOES]
    GB = 4
    groups = [-(-n // GB) for n in blocks]
    SLOTS = max(blocks) * P
    WS = 5
    ROUND = 1.5 * 2.0 ** 23
    wring = sb("wring", [P, 2, 1536])
    gatew = sb("gatew", [P, 48])
    down = sb("expert_order", [P, 33])
    b2r = sb("b2r", [8, D])
    trib = sb("trib", [P, P], BF16)
    onesb = sb("onesb", [P, P], BF16)
    gated = sb("gated", [P, 2, 512])
    comb = sb("comb", [P, NT, 32])
    lg = sb("lg", [P, NT, 32])
    r1 = sb("r1", [P, NT, 32])
    r2 = sb("r2", [P, NT, 32])
    rcol = sb("rcol", [P, 8, NT])
    place = sb("place", [P, 2, NT], mybir.dt.int32)
    expert_of = sb("expert_of", [P, 1], mybir.dt.int32)
    wslot = [wring[:, 0, :], wring[:, 1, :], wring2[:, 0, :], wring2[:, 1, :], tmp[:, 0:1536]]
    xin = tmp[:, 1536:2560].rearrange("p (s k d) -> p s k d", s=2, k=GB)
    xbT = tmp[:, 2560:3584].rearrange("p (s k n) -> p s k n", s=2, k=GB)
    yblk = tmp[:, 3584:4608].rearrange("p (s k d) -> p s k d", s=2, k=GB)
    hid = tmp[:, 4608:5632].rearrange("p (s n) -> p s n", s=2)
    shid = tmp[:, 5632:5632 + 2 * T].rearrange("p (c n) -> p c n", c=2)
    back = tmp[:, 5632:5632 + 2 * T].rearrange("p (k t d) -> p k t d", k=2, t=NT)
    combT = tmp[0:8, 1536:1536 + T]
    chosen_b = tmp[:, 7680:7808].bitcast(BF16).rearrange("p (t e) -> p t e", e=32)
    small = lambda i: tmp[:, 7808 + 32 * i:7840 + 32 * i]
    soft = tmp[:, 8000:8064].rearrange("p (t e) -> p t e", e=8)
    scr_x = nc.dram_tensor("scr_x", [SLOTS, D], F32, kind="Internal").ap()
    scr_y = nc.dram_tensor("scr_y", [SLOTS, D], F32, kind="Internal").ap()
    m3 = range(3)
    sh = [4 * m["shared"] for m in MOES]
    routed_mm = counter("routed_mm", [1] * 3)
    chosen = counter("chosen", [1] * 3)
    ranked_mm = counter("ranked_mm", [1] * 3)
    placed = counter("placed", [2] * 3)
    r_exp = counter("r_exp", [1] * 3)
    sorted_out = counter("sorted_out", [m["choices"] * NT for m in MOES], 16)
    x_in = [counter(f"x_in{i}", [(g + 1 - i) // 2 for g in groups], 16) for i in range(2)]
    x_tp = counter("x_tp", groups)
    x_T = counter("x_T", groups)
    w_in = [counter(f"w_in{i}", [(n + m["shared"] + WS - 1 - i) // WS for n, m in zip(blocks, MOES)], 16) for i in range(WS)]
    up_mm = counter("up_mm", [s + n for s, n in zip(sh, blocks)])
    act_sb = counter("act_sb", [s + n for s, n in zip(sh, blocks)])
    hid_sb = counter("hid_sb", [s + n for s, n in zip(sh, blocks)])
    down_mm = counter("down_mm", [s // 2 + n for s, n in zip(sh, blocks)])
    y_sb = counter("y_sb", blocks)
    y_spill = [counter(f"y_spill{i}", [(g + 1 - i) // 2 for g in groups], 16) for i in range(2)]
    gathered = counter("gathered", [m["choices"] * NT for m in MOES], 16)
    mixed = counter("mixed", [m["shared"] + 1 for m in MOES])
    bias_mm = counter("bias_mm", [0, 0, 2])
    combT_sb = counter("combT_sb", [0, 0, 1])

    class Mixture:
        def __init__(self, m, norm):
            c = MOES[m]
            self.m, self.norm, self.name, self.sub = m, norm, c["name"], c["sub"]
            self.e, self.c, self.shared, self.gate_at = c["experts"], c["chunks"], c["shared"], c["gate_at"]
            self.choices, self.nb, self.ng, self.sh = c["choices"], blocks[m], groups[m], sh[m]
            self.relu = self.name == "L2_ffn"
            self.width = self.c * P
            self.packed = a[f"{self.name}_w"]

        def weights(self, r):
            w, n = wslot[r % WS], self.width
            if self.relu:
                return w[:, 0:n], None, w[:, n:2 * n], w[:, 2 * n:2 * n + self.c]
            return w[:, 0:n], w[:, n:2 * n], w[:, 2 * n:3 * n], None

        def group(self, g):
            n = min(GB, self.nb - g * GB)
            return n, slice(g * GB * P, (g * GB + n) * P)

        def x_sync(self, sp, g):
            m = self.m
            n, rows = self.group(g)
            if g >= 2:
                sp.wait_ge(x_tp.sem, x_tp.at(m, g - 1))
            sp.dma_start(xin[:, g % 2, 0:n, :], scr_x[rows, :].rearrange("(k p) d -> p k d", p=P)
                         ).then_inc(x_in[g % 2].sem, 16)

        def sync(self, sp):
            m, n = self.m, self.packed.shape[2]
            sp.wait_ge(x_done.sem, x_done.at(self.sub - 1, 1))
            if self.shared:
                sp.dma_start(wslot[0][:, 0:n], self.packed[0]).then_inc(w_in[0].sem, 16)
            sp.wait_ge(placed.sem, placed.at(m, 2))
            for b in range(self.nb):
                r = b + self.shared
                if r >= WS:
                    sp.wait_ge(down_mm.sem, down_mm.at(m, self.sh // 2 + b - WS + 1))
                expert = sp.value_load(expert_of[b:b + 1, 0:1], min_val=0, max_val=self.e - 1 + self.shared)
                sp.dma_start(wslot[r % WS][:, 0:n], self.packed[bass.ds(expert, 1), :, :].rearrange("o p n -> p (o n)")
                             ).then_inc(w_in[r % WS].sem, 16)
                if b == 0:
                    sp.wait_ge(sorted_out.sem, sorted_out.at(m, self.choices * NT))
                    self.x_sync(sp, 0)
                if b % GB == 0 and b // GB + 1 < self.ng:
                    self.x_sync(sp, b // GB + 1)

        def tensor(self, pe):
            m, e = self.m, self.e
            pe.wait_ge(ln_hT.sem, ln_hT.at(self.norm, 2))
            for t in range(NT):
                ins = pe.matmul(bank(7, t * 32, t * 32 + e), hT[:, t * P:(t + 1) * P],
                                gatew[:, self.gate_at:self.gate_at + e], start=True, stop=True)
            ins.then_inc(routed_mm.sem, 1)
            if self.shared:
                pe.wait_ge(w_in[0].sem, w_in[0].at(m, 1))
                self.shared_up_tensor(pe, 0)
                self.shared_up_tensor(pe, 1)
            pe.wait_ge(chosen.sem, chosen.at(m, 1))
            for t in range(NT + 1):
                for before in range(min(t + 1, NT)):
                    ins = pe.matmul(bank(6, t * 32, t * 32 + e), trib[:, :] if before == t else onesb[:, :],
                                    chosen_b[:, before, 0:e], start=(before == 0), stop=(before == min(t, NT - 1)))
            ins.then_inc(ranked_mm.sem, 1)
            if self.shared:
                self.shared_up_tensor(pe, 2)
                self.shared_up_tensor(pe, 3)
                self.shared_down_tensor(pe)
            for b in range(self.nb):
                g = b // GB
                if b == 0:
                    self.turn_tensor(pe, 0)
                if b % GB == GB // 2 and g + 1 < self.ng:
                    self.turn_tensor(pe, g + 1)
                self.up_tensor(pe, b)
                if b:
                    self.down_tensor(pe, b - 1)
            self.down_tensor(pe, self.nb - 1)
            if self.relu:
                pe.wait_ge(y_sb.sem, y_sb.at(m, self.nb))
                for t in range(NT):
                    ins = pe.transpose(bank(0 + t // 4, t % 4 * P, t % 4 * P + P)[0:8, :], comb[:, t, 0:8], ident[:, :])
                ins.then_inc(bias_mm.sem, 1)
                pe.wait_ge(combT_sb.sem, combT_sb.at(m, 1))
                for t in range(NT):
                    ins = pe.matmul(bank(2 + t // 4, t % 4 * P, t % 4 * P + P), combT[:, t * P:(t + 1) * P],
                                    b2r[:, :], start=True, stop=True)
                ins.then_inc(bias_mm.sem, 1)

        def shared_up_tensor(self, pe, k):
            m = self.m
            gate, up, _, _ = self.weights(0)
            c, cols = k // 2, hT[:, k % 2 * 512:k % 2 * 512 + 512]
            if k >= 2:
                pe.wait_ge(hid_sb.sem, hid_sb.at(m, k - 1))
            pe.matmul(bank(k % 2), gate[:, c * P:(c + 1) * P], cols, start=True, stop=True)
            pe.matmul(bank(2 + k % 2), up[:, c * P:(c + 1) * P], cols, start=True, stop=True).then_inc(up_mm.sem, 1)

        def shared_down_tensor(self, pe):
            m = self.m
            last = self.weights(0)[2]
            pe.wait_ge(hid_sb.sem, hid_sb.at(m, self.sh))
            for half in range(2):
                for q in range(4):
                    t = half * 4 + q
                    for c in range(self.c):
                        ins = pe.matmul(bank(4 + half, q * P, q * P + P), shid[:, c, t * P:(t + 1) * P],
                                        last[:, c * D:(c + 1) * D], start=(c == 0), stop=(c == self.c - 1))
                ins.then_inc(down_mm.sem, 1)

        def turn_tensor(self, pe, g):
            m = self.m
            pe.wait_ge(x_in[g % 2].sem, x_in[g % 2].at(m, g // 2 + 1))
            if g == 0:
                pe.wait_ge(placed.sem, placed.at(m, 1))
            else:
                pe.wait_ge(x_T.sem, x_T.at(m, g))
            for k in range(self.group(g)[0]):
                ins = pe.transpose(bank(6 + g % 2, k * P, k * P + P), xin[:, g % 2, k, :], ident[:, :])
            ins.then_inc(x_tp.sem, 1)

        def up_tensor(self, pe, b):
            m, k = self.m, self.sh + b
            r = b + self.shared
            gate, up, _, _ = self.weights(r)
            pe.wait_ge(w_in[r % WS].sem, w_in[r % WS].at(m, r // WS + 1))
            pe.wait_ge(x_T.sem, x_T.at(m, b // GB + 1))
            if k >= 2:
                pe.wait_ge(hid_sb.sem, hid_sb.at(m, k - 1))
            cols = xbT[:, b // GB % 2, b % GB, :]
            for c in range(self.c):
                at = slice(c * P, (c + 1) * P)
                ins = pe.matmul(bank(k % 2)[:, at], gate[:, at], cols, start=True, stop=True)
                if up is not None:
                    ins = pe.matmul(bank(2 + k % 2)[:, at], up[:, at], cols, start=True, stop=True)
            ins.then_inc(up_mm.sem, 1)

        def down_tensor(self, pe, b):
            m, last = self.m, self.weights(b + self.shared)[2]
            pe.wait_ge(hid_sb.sem, hid_sb.at(m, self.sh + b + 1))
            if b >= 2:
                pe.wait_ge(y_sb.sem, y_sb.at(m, b - 1))
            elif self.shared:
                pe.wait_ge(mixed.sem, mixed.at(m, 1))
            for c in range(self.c):
                ins = pe.matmul(bank(4 + b % 2, 0, P), hid[:, b % 2, c * P:(c + 1) * P], last[:, c * D:(c + 1) * D],
                                start=(c == 0), stop=(c == self.c - 1))
            ins.then_inc(down_mm.sem, 1)

        def turn_scalar(self, act, g):
            m = self.m
            n = self.group(g)[0]
            act.wait_ge(x_tp.sem, x_tp.at(m, g + 1))
            if g >= 2:
                act.wait_ge(up_mm.sem, up_mm.at(m, self.sh + (g - 1) * GB))
            act.copy(xbT[:, g % 2, 0:n, :].rearrange("p k n -> p (k n)"),
                     bank(6 + g % 2, 0, n * P)).then_inc(x_T.sem, 1)

        def scalar(self, act):
            m = self.m
            act.wait_ge(chosen.sem, chosen.at(m, 1))
            if self.shared:
                act.activation(rcol[:, 1, :], rcol[:, 0, :], ACT.Exp, scale=-1.0).then_inc(r_exp.sem, 1)
            else:
                if self.relu:
                    act.activation(soft, soft, ACT.Exp)
                act.activation(rcol[:, 3, :], rcol[:, 2, :], ACT.Exp).then_inc(r_exp.sem, 1)
            for k in range(self.sh):
                act.wait_ge(up_mm.sem, up_mm.at(m, k + 1))
                if k >= 2:
                    act.wait_ge(hid_sb.sem, hid_sb.at(m, k - 1))
                act.activation(gated[:, k % 2, :], bank(k % 2), ACT.Silu).then_inc(act_sb.sem, 1)
            for b in range(self.nb):
                k, g = self.sh + b, b // GB
                if b == 0:
                    self.turn_scalar(act, 0)
                if b % GB == GB // 2 and g + 1 < self.ng:
                    self.turn_scalar(act, g + 1)
                act.wait_ge(up_mm.sem, up_mm.at(m, k + 1))
                if self.relu:
                    if b >= 2:
                        act.wait_ge(down_mm.sem, down_mm.at(m, self.sh // 2 + b - 1))
                    bias = self.weights(b + self.shared)[3]
                    for c in range(self.c):
                        ins = act.activation(hid[:, b % 2, c * P:(c + 1) * P], bank(k % 2, c * P, (c + 1) * P), ACT.Relu,
                                             bias=bias[:, c:c + 1])
                    ins.then_inc(hid_sb.sem, 1)
                else:
                    if k >= 2:
                        act.wait_ge(hid_sb.sem, hid_sb.at(m, k - 1))
                    act.activation(gated[:, k % 2, 0:self.width], bank(k % 2, 0, self.width),
                                   ACT.Silu).then_inc(act_sb.sem, 1)
            if self.relu:
                act.wait_ge(bias_mm.sem, bias_mm.at(m, 1))
                act.copy(combT.rearrange("p (b n) -> p b n", b=2), ps[0:8, 0:2, :]).then_inc(combT_sb.sem, 1)

        def choose_vector(self, dve):
            m, e = self.m, self.e
            L, R1, R2, C = lg[:, :, 0:e], r1[:, :, 0:e], r2[:, :, 0:e], comb[:, :, 0:e]
            col = lambda i: rcol[:, i, :]
            wide = lambda ap: ap.unsqueeze(2).to_broadcast([P, NT, e])
            do = lambda ins: link(dve, dchain, ins)
            order = down[:, 32 - e:32].unsqueeze(1).to_broadcast([P, NT, e])

            def first_of(out, src, top, scratch, topcol):
                do(dve.tensor_tensor(out, src, wide(top), ALU.is_equal))
                do(dve.tensor_tensor(scratch, out, order, ALU.mult))
                do(dve.tensor_reduce(topcol, scratch, AX.X, ALU.max))
                do(dve.tensor_tensor(out, scratch, wide(topcol), ALU.is_equal))

            dve.wait_ge(routed_mm.sem, routed_mm.at(m, 1))
            do(dve.tensor_copy(L, bank(7, 0, NT * 32).rearrange("p (t e) -> p t e", e=32)[:, :, 0:e]))
            do(dve.tensor_reduce(col(0), L, AX.X, ALU.max))
            first_of(C, L, col(0), R2, col(4))
            if self.choices == 1:
                dve.tensor_copy(chosen_b[:, :, 0:e], C).then_inc(chosen.sem, 1)
                return
            do(dve.scalar_tensor_tensor(out=R1, in0=C, scalar=-BIG, in1=L, op0=ALU.mult, op1=ALU.add))
            do(dve.tensor_reduce(col(1), R1, AX.X, ALU.max))
            first_of(R2, R1, col(1), R1, col(4))
            do(dve.tensor_tensor(col(2), col(1), col(0), ALU.subtract))
            if self.relu:
                do(dve.tensor_tensor(soft, L, wide(col(0)), ALU.subtract))
            dve.tensor_tensor(chosen_b[:, :, 0:e], C, R2, ALU.add).then_inc(chosen.sem, 1)

        def place_vector(self, dve):
            m, e = self.m, self.e
            do = lambda ins: link(dve, dchain, ins)
            need, end, off, ones = (small(i)[:, 0:e] for i in range(4))
            before = small(4)[:, 0:2]
            L = lg[:, :, 0:e]
            if self.choices == 1:
                dve.wait_ge(r_exp.sem, r_exp.at(m, 1))
                do(dve.tensor_scalar(rcol[:, 2, :], rcol[:, 1, :], 1.0, None, ALU.add))
                do(dve.reciprocal(rcol[:, 3, :], rcol[:, 2, :]))
                do(dve.tensor_tensor(h[:, :, :], h[:, :, :], rcol[:, 3, :].unsqueeze(2).to_broadcast([P, NT, D]), ALU.mult))
            dve.wait_ge(ranked_mm.sem, ranked_mm.at(m, 1))
            do(dve.tensor_scalar(need, bank(6, NT * 32, NT * 32 + e), 1.0 / P, 0.5 - 0.5 / P, ALU.mult, ALU.add))
            do(dve.tensor_scalar(need, need, ROUND, ROUND, ALU.add, ALU.subtract))
            do(dve.memset(ones, 1.0))
            do(dve.tensor_tensor_scan(end, ones, need, 0.0, ALU.mult, ALU.add))
            do(dve.tensor_tensor(off, end, need, ALU.subtract))
            do(dve.scalar_tensor_tensor(out=L, in0=off.unsqueeze(1).to_broadcast([P, NT, e]), scalar=float(P),
                                        in1=bank(6, 0, NT * 32).rearrange("p (t e) -> p t e", e=32)[:, :, 0:e],
                                        op0=ALU.mult, op1=ALU.add))
            for k, choice in enumerate((comb, r2)[:self.choices]):
                do(dve.tensor_tensor(r1[:, :, 0:e], L, choice[:, :, 0:e], ALU.mult))
                do(dve.tensor_reduce(rcol[:, 4, :], r1[:, :, 0:e], AX.X, ALU.add))
                ins = dve.tensor_scalar(place[:, k, :], rcol[:, 4, :], -1.0, None, ALU.add)
                if k + 1 < self.choices:
                    do(ins)
            ins.then_inc(placed.sem, 1)
            do(dve.tensor_scalar(off, end, down[:, 32:33], None, ALU.is_le, ALU.add, accum_out=before[:, 0:1]))
            dve.tensor_scalar(expert_of[:, :], before[:, 0:1], self.e - 1.0, float(self.shared),
                              ALU.min, ALU.add).then_inc(placed.sem, 1)
            if self.choices == 2:
                first, second, total = rcol[:, 5, :], rcol[:, 6, :], rcol[:, 7, :]
                dve.wait_ge(r_exp.sem, r_exp.at(m, 1))
                dve.wait_ge(placed.sem, placed.at(m, 1))
                if self.relu:
                    do(dve.tensor_reduce(total, soft, AX.X, ALU.add))
                else:
                    do(dve.tensor_scalar(total, rcol[:, 3, :], 1.0, None, ALU.add))
                do(dve.reciprocal(first, total))
                do(dve.tensor_tensor(second, first, rcol[:, 3, :], ALU.mult))
                if self.relu:
                    wide = lambda ap: ap.unsqueeze(2).to_broadcast([P, NT, e])
                    C, R2 = comb[:, :, 0:e], r2[:, :, 0:e]
                    do(dve.tensor_tensor(C, C, wide(first), ALU.mult))
                    do(dve.tensor_tensor(R2, R2, wide(second), ALU.mult))
                    do(dve.tensor_tensor(C, C, R2, ALU.add))

        def shared_vector(self, dve, k):
            m = self.m
            dve.wait_ge(act_sb.sem, act_sb.at(m, k + 1))
            dve.tensor_tensor(shid[:, k // 2, k % 2 * 512:k % 2 * 512 + 512], gated[:, k % 2, :], bank(2 + k % 2),
                              ALU.mult).then_inc(hid_sb.sem, 1)

        def vector(self, dve):
            m = self.m
            self.choose_vector(dve)
            if self.shared:
                self.shared_vector(dve, 0)
                self.shared_vector(dve, 1)
            self.place_vector(dve)
            if m == 1:
                others[7].context_vector(dve)
            xf = x[:, :, :].rearrange("p t d -> p (t d)")
            if self.shared:
                self.shared_vector(dve, 2)
                self.shared_vector(dve, 3)
                dve.wait_ge(down_mm.sem, down_mm.at(m, 2))
                dve.tensor_tensor(xf, xf, ps[:, 4:6, :].rearrange("p b n -> p (b n)"), ALU.add).then_inc(mixed.sem, 1)
            for b in range(self.nb + 1):
                k = self.sh + b
                if b < self.nb and not self.relu:
                    if b >= 2:
                        dve.wait_ge(down_mm.sem, down_mm.at(m, self.sh // 2 + b - 1))
                    dve.wait_ge(act_sb.sem, act_sb.at(m, k + 1))
                    dve.tensor_tensor(hid[:, b % 2, 0:self.width], gated[:, k % 2, 0:self.width],
                                      bank(2 + k % 2, 0, self.width), ALU.mult).then_inc(hid_sb.sem, 1)
                if b:
                    y, g = b - 1, (b - 1) // GB
                    dve.wait_ge(down_mm.sem, down_mm.at(m, self.sh // 2 + y + 1))
                    if y % GB == 0 and g >= 2:
                        dve.wait_ge(y_spill[g % 2].sem, y_spill[g % 2].at(m, g // 2))
                    dve.tensor_copy(yblk[:, g % 2, y % GB, :], bank(4 + y % 2, 0, P)).then_inc(y_sb.sem, 1)
            if self.relu:
                dve.wait_ge(bias_mm.sem, bias_mm.at(m, 2))
                link(dve, dchain, dve.tensor_tensor(xf, xf, ps[:, 2:4, :].rearrange("p b n -> p (b n)"), ALU.add))
            dve.wait_ge(gathered.sem, gathered.at(m, self.choices * NT))
            for k in range(self.choices):
                if self.shared:
                    dve.wait_ge(mixed.sem, mixed.at(m, 1))
                    ins = dve.tensor_tensor(x[:, :, :], x[:, :, :], back[:, 0, :, :], ALU.add)
                else:
                    for t in range(NT):
                        ins = dve.scalar_tensor_tensor(out=x[:, t, :], in0=back[:, k, t, :],
                                                       scalar=rcol[:, 5 + k, t:t + 1], in1=x[:, t, :],
                                                       op0=ALU.mult, op1=ALU.add)
                if k + 1 < self.choices:
                    link(dve, dchain, ins)
            ins.then_inc(mixed.sem, 1)
            dve.wait_ge(mixed.sem, mixed.at(m, self.shared + 1))

        def gpsimd(self, pool):
            m = self.m
            pool.wait_ge(placed.sem, placed.at(m, 1))
            if m == 0:
                pool.wait_ge(written, 16)
            for k in range(self.choices):
                for t in range(NT):
                    pool.indirect_dma_start(scr_x, bass.IndirectOffsetOnAxis(ap=place[:, k, t:t + 1], axis=0),
                                            h[:, t, :], None).then_inc(sorted_out.sem, 16)
            if m == 1:
                others[7].context_gpsimd(pool)
            if self.relu:
                link(pool, pchain, pool.memset(qs[:, :].bitcast(F32), 0.0))
                link(pool, pchain, pool.memset(ks[:, :].bitcast(F32), 0.0))
                pool.memset(ks[MAXROW:MAXROW + 3, :].bitcast(F32), TWO_ONES).then_inc(rows_again.sem, 1)
                pool.wait_ge(rows_again.sem, rows_again.at(0, 1))
            for g in range(self.ng):
                n, rows = self.group(g)
                pool.wait_ge(y_sb.sem, y_sb.at(m, g * GB + n))
                if g >= 2:
                    pool.wait_ge(y_spill[g % 2].sem, y_spill[g % 2].at(m, g // 2))
                pool.dma_start(scr_y[rows, :].rearrange("(k p) d -> p k d", p=P),
                               yblk[:, g % 2, 0:n, :]).then_inc(y_spill[g % 2].sem, 16)
            for i in range(2):
                pool.wait_ge(y_spill[i].sem, y_spill[i].at(m, (self.ng + 1 - i) // 2))
            for k in range(self.choices):
                for t in range(NT):
                    pool.indirect_dma_start(back[:, k, t, :], None, scr_y,
                                            bass.IndirectOffsetOnAxis(ap=place[:, k, t:t + 1], axis=0)
                                            ).then_inc(gathered.sem, 16)

    bmask = sb("bmask", [P, H])
    vmask = sb("vmask", [P, 32])
    NK = S2 // H
    g_ctx = counter("g_ctx", [1], 16)
    g_k_mm = counter("g_k_mm", [B])
    g_k_sb = counter("g_k_sb", [B])
    g_v_mm = counter("g_v_mm", [1])
    g_v_sb = counter("g_v_sb", [1])
    g_q_mm = counter("g_q_mm", [2])
    g_q_sb = counter("g_q_sb", [2])
    g_s_mm = counter("g_s_mm", [NT])
    g_s_sub = counter("g_s_sub", [NT])
    g_exp = counter("g_exp", [NT])
    g_p = counter("g_p", [NT])
    g_tp = counter("g_tp", [NT])
    g_pT = counter("g_pT", [NT])
    g_av = counter("g_av", [B])
    g_oT = counter("g_oT", [B])
    g_y = counter("g_y", [2])

    class Gathered:
        sub, norm, name = 4, 4, "L1_xattn"
        ctxg = tmp[:, 0:TC]
        kbd = tmp[:, TC:2 * TC]
        vbd = tmp[:, 2 * TC:2 * TC + 512].rearrange("p (t n) -> p t n", n=32)
        qT = tmp[:, 2 * TC + 512:2 * TC + 512 + T]
        pr = tmp[:, 2 * TC + 512 + T:2 * TC + 512 + 2 * T].rearrange("p (s n) -> p s n", s=2)
        pT = tmp[:, 2 * TC + 512 + 2 * T:2 * TC + 512 + 3 * T].rearrange("p (c n) -> p c n", c=NQ)
        oT = hT

        def sync(self, sp):
            sp.wait_ge(x_done.sem, x_done.at(self.sub - 1, 1))
            sp.dma_start(self.ctxg, a["ctxT_by_head"]).then_inc(g_ctx.sem, 16)

        def order(self):
            for t in range(NT + 2):
                if t < NT:
                    yield "score", t
                if 0 <= t - 1 < NT:
                    yield "turn", t - 1
                    if (t - 1) % 2:
                        yield "sum", (t - 1) // 2

        def tensor(self, pe):
            pe.wait_ge(g_ctx.sem, 16)
            for b in range(B):
                pe.matmul(bank(b), wt("L1_xattn_k"), self.ctxg[:, b * S2:(b + 1) * S2],
                          start=True, stop=True).then_inc(g_k_mm.sem, 1)
            for t in range(B * NQ):
                c = t % NQ
                ins = pe.matmul(bank(4, t * 32, t * 32 + 32), self.ctxg[:, t * P:(t + 1) * P],
                                wt("L1_xattn_v")[:, c * 32:c * 32 + 32], start=True, stop=True)
            ins.then_inc(g_v_mm.sem, 1)
            for c in range(2):
                pe.wait_ge(ln_hT.sem, ln_hT.at(self.norm, c + 1))
                pe.matmul(bank(5 + c), wt("L1_xattn_q"), hT[:, c * 512:c * 512 + 512],
                          start=True, stop=True).then_inc(g_q_mm.sem, 1)
            pe.wait_ge(g_k_sb.sem, g_k_sb.at(0, B))
            pe.wait_ge(g_q_sb.sem, g_q_sb.at(0, 2))
            pe.wait_ge(g_v_sb.sem, g_v_sb.at(0, 1))
            for what, t in self.order():
                if what == "score":
                    if t >= 2:
                        pe.wait_ge(g_s_sub.sem, g_s_sub.at(0, t - 1))
                    pe.matmul(bank(t % 2), self.qT[:, t * P:(t + 1) * P], self.kbd[:, t // 2 * S2:(t // 2 + 1) * S2],
                              start=True, stop=True).then_inc(g_s_mm.sem, 1)
                elif what == "turn":
                    pe.wait_ge(g_p.sem, g_p.at(0, t + 1))
                    if t >= 2:
                        pe.wait_ge(g_pT.sem, g_pT.at(0, t - 1))
                    for c in range(NQ):
                        ins = pe.transpose(bank(2 + t % 2, c * P, c * P + P), self.pr[:, t % 2, c * P:(c + 1) * P],
                                           ident[:, :])
                    ins.then_inc(g_tp.sem, 1)
                else:
                    b = t
                    pe.wait_ge(g_pT.sem, g_pT.at(0, 2 * b + 2))
                    if b >= 2:
                        pe.wait_ge(g_oT.sem, g_oT.at(0, b - 1))
                    for c in range(NQ):
                        ins = pe.matmul(ps[32 * c:32 * c + 32, 4 + b % 2, 0:S], self.vbd[:, b * NQ + c, :],
                                        self.pT[:, c, :], start=True, stop=True)
                    ins.then_inc(g_av.sem, 1)
            pe.wait_ge(g_oT.sem, g_oT.at(0, B))
            for t in range(NT):
                ins = pe.matmul(bank(6 + t // 4, t % 4 * P, t % 4 * P + P), self.oT[:, t * P:(t + 1) * P],
                                wt("L1_xattn_o"), start=True, stop=True)
                if t % 4 == 3:
                    ins.then_inc(g_y.sem, 1)

        def scalar(self, act):
            for what, t in self.order():
                if what == "score":
                    act.wait_ge(g_s_sub.sem, g_s_sub.at(0, t + 1))
                    act.activation(self.pr[:, t % 2, :], self.pr[:, t % 2, :], ACT.Exp).then_inc(g_exp.sem, 1)
                elif what == "turn":
                    act.wait_ge(g_tp.sem, g_tp.at(0, t + 1))
                    if t >= 2 and t % 2 == 0:
                        act.wait_ge(g_av.sem, g_av.at(0, t // 2))
                    act.copy(self.pT[:, :, t % 2 * P:t % 2 * P + P],
                             bank(2 + t % 2).rearrange("p (c n) -> p c n", c=NQ)).then_inc(g_pT.sem, 1)
                else:
                    act.wait_ge(g_av.sem, g_av.at(0, t + 1))
                    act.wait_ge(g_q_mm.sem, g_q_mm.at(0, 2))
                    act.copy(self.oT[:, t * S:(t + 1) * S], bank(4 + t % 2, 0, S)).then_inc(g_oT.sem, 1)

        def vector(self, dve):
            do = lambda ins: link(dve, dchain, ins)
            for b in range(B):
                dve.wait_ge(g_k_mm.sem, g_k_mm.at(0, b + 1))
                dve.scalar_tensor_tensor(
                    out=self.kbd[:, b * S2:(b + 1) * S2].rearrange("p (h k) -> p h k", h=H),
                    in0=bank(b).rearrange("p (h k) -> p h k", h=H), scalar=bcol[:, C_OF["L1_xattn_k"]:C_OF["L1_xattn_k"] + 1],
                    in1=bmask[:, :].unsqueeze(2).to_broadcast([P, H, NK]), op0=ALU.add, op1=ALU.mult).then_inc(g_k_sb.sem, 1)
            dve.wait_ge(g_v_mm.sem, g_v_mm.at(0, 1))
            b_v = brow[:, R_OF["L1_xattn_v"], :].unsqueeze(1).to_broadcast([P, B, D])
            do(dve.tensor_tensor(self.vbd[:, :, :].rearrange("p (b c) n -> p b (c n)", b=B),
                                 bank(4).rearrange("p (b n) -> p b n", b=B), b_v, ALU.add))
            dve.tensor_tensor(self.vbd[:, :, :], self.vbd[:, :, :],
                              vmask[:, :].unsqueeze(1).to_broadcast([P, B * NQ, 32]), ALU.mult).then_inc(g_v_sb.sem, 1)
            for c in range(2):
                dve.wait_ge(g_q_mm.sem, g_q_mm.at(0, c + 1))
                dve.tensor_scalar(self.qT[:, c * 512:c * 512 + 512], bank(5 + c),
                                  bcol[:, C_OF["L1_xattn_q"]:C_OF["L1_xattn_q"] + 1], SCALE,
                                  ALU.add, ALU.mult).then_inc(g_q_sb.sem, 1)
            for what, t in self.order():
                top, tot = r1[:, t % 2, 0:H], r1[:, 2 + t % 2, 0:H]
                pr = self.pr[:, t % 2, :].rearrange("p (h k) -> p h k", h=H)
                wide = lambda ap: ap.unsqueeze(2).to_broadcast([P, H, NK])
                if what == "score":
                    src = bank(t % 2).rearrange("p (h k) -> p h k", h=H)
                    dve.wait_ge(g_s_mm.sem, g_s_mm.at(0, t + 1))
                    do(dve.tensor_reduce(top, src, AX.X, ALU.max))
                    if t >= 2:
                        dve.wait_ge(g_tp.sem, g_tp.at(0, t - 1))
                    dve.tensor_tensor(pr, src, wide(top), ALU.subtract).then_inc(g_s_sub.sem, 1)
                elif what == "turn":
                    dve.wait_ge(g_exp.sem, g_exp.at(0, t + 1))
                    do(dve.tensor_reduce(tot, pr, AX.X, ALU.add))
                    do(dve.reciprocal(tot, tot))
                    dve.tensor_tensor(pr, pr, wide(tot), ALU.mult).then_inc(g_p.sem, 1)
            for c in range(2):
                dve.wait_ge(g_y.sem, g_y.at(0, c + 1))
                dve.wait_ge(x_biased.sem, x_biased.at(biased.index(self.sub), 1))
                xc = x[:, 4 * c:4 * c + 4, :]
                do(dve.tensor_tensor(xc, xc, bank(6 + c).rearrange("p (t d) -> p t d", d=D), ALU.add))

        def gpsimd(self, pool):
            bias_gpsimd(pool, self.sub, self.norm, "L1_xattn_o")

    l_in = counter("l_in", [2], 16)
    l_ones = counter("l_ones", [1])
    l_qkv = counter("l_qkv", [NT])
    l_sub = counter("l_sub", [NT])
    l_exp = counter("l_exp", [NT])
    l_z = counter("l_z", [NT])
    l_sm = counter("l_sm", [NT])
    l_kf = counter("l_kf", [NT])
    l_v = counter("l_v", [NT])
    l_tp = counter("l_tp", [NT])
    l_qTb = counter("l_qTb", [B])
    l_cT = counter("l_cT", [B])
    l_kv = counter("l_kv", [B])
    l_kvm = counter("l_kvm", [B])
    l_num = counter("l_num", [NT])
    l_read = counter("l_read", [NT])
    l_o = counter("l_o", [NT])
    l_otp = counter("l_otp", [NT])
    l_oT = counter("l_oT", [NT])
    l_y = counter("l_y", [2])

    class Linear:
        sub, norm, name = 6, 6, "L2_attn"
        AW = D + H
        at = np.cumsum([0, 768, 4 * 4 * D, NT * (D + H), 2 * 4 * (D + H), T, T, D + H, 8, 4 * (D + H), 2 * D])
        part = lambda at, i: tmp[:, int(at[i]):int(at[i + 1])]
        z = part(at, 0).rearrange("p (s n) -> p s n", s=2)
        kf = part(at, 1).rearrange("p (t f n) -> p t f n", t=4, f=4)
        vx = part(at, 2).rearrange("p (t n) -> p t n", t=NT)
        kvm = part(at, 3).rearrange("p (s f n) -> p s f n", s=2, f=4)
        qT, cT = part(at, 4), part(at, 5)
        kvmask = part(at, 6)
        trig = part(at, 7).rearrange("p (t k) -> p t k", t=2)
        nd = part(at, 8).rearrange("p (f n) -> p f n", f=4)
        o = part(at, 9).rearrange("p (s n) -> p s n", s=2)
        oT = hT

        def sync(self, sp):
            sp.wait_ge(x_done.sem, x_done.at(self.sub - 1, 1))
            sp.dma_start(self.kvmask, a["kv_mask"]).then_inc(l_in.sem, 16)
            sp.dma_start(self.trig, a["trig"]).then_inc(l_in.sem, 16)

        def order(self):
            for t in range(NT + 1):
                if t < NT:
                    yield "qkv", t
                if t:
                    yield "turn", t - 1
                    if (t - 1) % 2:
                        yield "kv", (t - 1) // 2
                        for q in (t - 2, t - 1):
                            yield "num", q
            for t in range(NT):
                yield "out", t

        def tensor(self, pe):
            for what, t in self.order():
                if what == "qkv":
                    pe.wait_ge(ln_hT.sem, ln_hT.at(self.norm, t // 4 + 1))
                    if t >= 2:
                        pe.wait_ge(l_z.sem, l_z.at(0, t - 1))
                    pe.matmul(bank(t % 2, 0, 3 * D), hT[:, t * P:(t + 1) * P], wt("L2_attn_q", 3),
                              start=True, stop=True).then_inc(l_qkv.sem, 1)
                elif what == "turn":
                    pe.wait_ge(l_sm.sem, l_sm.at(0, t + 1))
                    if t >= 2 and t % 2 == 0:
                        pe.wait_ge(l_cT.sem, l_cT.at(0, t // 2))
                    pe.transpose(bank(4, t % 2 * P, t % 2 * P + P), self.z[:, t % 2, 0:D],
                                 ident[:, :]).then_inc(l_tp.sem, 1)
                elif what == "kv":
                    b = t
                    pe.wait_ge(l_v.sem, l_v.at(0, 2 * b + 2))
                    pe.wait_ge(l_kf.sem, l_kf.at(0, 2 * b + 2))
                    if b:
                        pe.wait_ge(l_kvm.sem, l_kvm.at(0, b))
                    for f in range(4):
                        for k in range(2):
                            ins = pe.matmul(bank(2 + f // 2, f % 2 * self.AW, (f % 2 + 1) * self.AW),
                                            self.kf[:, (2 * b + k) % 4, f, :], self.vx[:, 2 * b + k, :],
                                            start=(k == 0), stop=(k == 1))
                    ins.then_inc(l_kv.sem, 1)
                elif what == "num":
                    b = t // 2
                    pe.wait_ge(l_kvm.sem, l_kvm.at(0, b + 1))
                    pe.wait_ge(l_cT.sem, l_cT.at(0, b + 1))
                    if t:
                        pe.wait_ge(l_read.sem, l_read.at(0, t))
                    for f in range(4):
                        lhs = (self.qT if f < 2 else self.cT)[:, t * P:(t + 1) * P]
                        ins = pe.matmul(bank(6 + f // 2, f % 2 * self.AW, (f % 2 + 1) * self.AW), lhs,
                                        self.kvm[:, b % 2, f, :], start=True, stop=True)
                    ins.then_inc(l_num.sem, 1)
                else:
                    pe.wait_ge(l_o.sem, l_o.at(0, t + 1))
                    pe.transpose(bank(5, t % 4 * P, t % 4 * P + P), self.o8(t), ident[:, :]).then_inc(l_otp.sem, 1)
                    pe.wait_ge(l_oT.sem, l_oT.at(0, t + 1))
            for t in range(NT):
                ins = pe.matmul(bank(2 + t // 4, t % 4 * P, t % 4 * P + P), self.oT[:, t * P:(t + 1) * P],
                                wt("L2_attn_o"), start=True, stop=True)
                if t % 4 == 3:
                    ins.then_inc(l_y.sem, 1)

        def o8(self, t):
            return h[:, t, :]

        def scalar(self, act):
            for what, t in self.order():
                if what == "qkv":
                    act.wait_ge(l_sub.sem, l_sub.at(0, t + 1))
                    act.activation(self.z[:, t % 2, 0:2 * D], self.z[:, t % 2, 0:2 * D], ACT.Exp).then_inc(l_exp.sem, 1)
                elif what == "turn" and t % 2:
                    b = t // 2
                    act.wait_ge(l_tp.sem, l_tp.at(0, t + 1))
                    act.copy(self.qT[:, b * S:(b + 1) * S], bank(4, 0, S)).then_inc(l_qTb.sem, 1)
                elif what == "out":
                    act.wait_ge(l_otp.sem, l_otp.at(0, t + 1))
                    b, k = t // 2, t % 2
                    act.copy(self.oT[:, :].rearrange("p (l b) -> p b l", b=B)[:, b, k * P:(k + 1) * P],
                             bank(5, t % 4 * P, t % 4 * P + P)).then_inc(l_oT.sem, 1)

        def vector(self, dve):
            do = lambda ins: link(dve, dchain, ins)
            dve.wait_ge(l_in.sem, l_in.at(0, 2))
            dve.memset(self.vx[:, :, D:], 1.0).then_inc(l_ones.sem, 1)
            for what, t in self.order():
                z = self.z[:, t % 2, :]
                if what == "qkv":
                    top = r1[:, 0, 0:32]
                    qk = z[:, 0:2 * D].rearrange("p (h d) -> p h d", d=HD)
                    dve.wait_ge(l_qkv.sem, l_qkv.at(0, t + 1))
                    if t >= 2:
                        dve.wait_ge(l_tp.sem, l_tp.at(0, t - 1))
                        dve.wait_ge(l_v.sem, l_v.at(0, t - 1))
                        dve.wait_ge(l_kf.sem, l_kf.at(0, t - 1))
                    dve.tensor_tensor(z, bank(t % 2, 0, 3 * D), brow[:, R_OF["L2_attn_q"]:R_OF["L2_attn_q"] + 3, :]
                                      .rearrange("p r d -> p (r d)"), ALU.add).then_inc(l_z.sem, 1)
                    dve.wait_ge(l_z.sem, l_z.at(0, t + 1))
                    do(dve.tensor_reduce(top, qk, AX.X, ALU.max))
                    dve.tensor_tensor(qk, qk, top.unsqueeze(2).to_broadcast([P, 32, HD]),
                                      ALU.subtract).then_inc(l_sub.sem, 1)
                elif what == "turn":
                    qk = z[:, 0:2 * D].rearrange("p (h d) -> p h d", d=HD)
                    tot, inv = r1[:, 1, 0:32], r1[:, 2, 0:32]
                    dve.wait_ge(l_exp.sem, l_exp.at(0, t + 1))
                    do(dve.tensor_reduce(tot, qk, AX.X, ALU.add))
                    do(dve.reciprocal(inv, tot))
                    dve.tensor_tensor(qk, qk, inv.unsqueeze(2).to_broadcast([P, 32, HD]),
                                      ALU.mult).then_inc(l_sm.sem, 1)
                    dve.wait_ge(l_sm.sem, l_sm.at(0, t + 1))
                    if t >= 4 and t % 2 == 0:
                        dve.wait_ge(l_kv.sem, l_kv.at(0, t // 2 - 1))
                    for f in range(4):
                        tr = self.trig[:, t % 2, :]
                        out = self.kf[:, t % 4, f, :]
                        if f < 2:
                            ins = dve.tensor_scalar(out, z[:, D:2 * D], tr[:, f:f + 1], None, ALU.mult)
                        else:
                            ins = dve.tensor_scalar(out, z[:, D:2 * D], 1.0, tr[:, f:f + 1], ALU.subtract, ALU.mult)
                    ins.then_inc(l_kf.sem, 1)
                    if t % 2:
                        b = t // 2
                        dve.wait_ge(l_qTb.sem, l_qTb.at(0, b + 1))
                        dve.tensor_scalar(self.cT[:, b * S:(b + 1) * S], self.qT[:, b * S:(b + 1) * S], -1.0, 1.0,
                                          ALU.mult, ALU.add).then_inc(l_cT.sem, 1)
                elif what == "kv":
                    b = t
                    dve.wait_ge(l_kv.sem, l_kv.at(0, b + 1))
                    if b >= 2:
                        dve.wait_ge(l_num.sem, l_num.at(0, 2 * b - 2))
                    for k in range(2):
                        ins = dve.tensor_tensor(self.kvm[:, b % 2, 2 * k:2 * k + 2, :],
                                                bank(2 + k, 0, 2 * self.AW).rearrange("p (f n) -> p f n", f=2),
                                                self.kvmask.unsqueeze(1).to_broadcast([P, 2, self.AW]), ALU.mult)
                    ins.then_inc(l_kvm.sem, 1)
                elif what == "num":
                    tr = self.trig[:, t % 2, :]
                    nd, both = self.nd, ps[:, 6:8, :]
                    even = both[:, :, 0:self.AW]
                    odd = both[:, :, self.AW:2 * self.AW]
                    dve.wait_ge(l_num.sem, l_num.at(0, t + 1))
                    do(dve.tensor_scalar(nd[:, 0:2, :], even, tr[:, 0:1], None, ALU.mult))
                    dve.scalar_tensor_tensor(out=nd[:, 2:4, :], in0=odd, scalar=tr[:, 1:2], in1=nd[:, 0:2, :],
                                             op0=ALU.mult, op1=ALU.add).then_inc(l_read.sem, 1)
                    dve.wait_ge(l_read.sem, l_read.at(0, t + 1))
                    den = r1[:, 3, 0:32].rearrange("p (f h) -> p f h", f=2)
                    inv = r1[:, 4, 0:32].rearrange("p (f h) -> p f h", f=2)
                    do(dve.tensor_scalar(den, nd[:, 2:4, D:], 1e-6, None, ALU.max))
                    do(dve.reciprocal(inv, den))
                    for k in range(2):
                        ins = dve.tensor_tensor(nd[:, k, 0:D].rearrange("p (h d) -> p h d", d=HD),
                                                nd[:, 2 + k, 0:D].rearrange("p (h d) -> p h d", d=HD),
                                                inv[:, k, :].unsqueeze(2).to_broadcast([P, H, HD]), ALU.mult)
                    do(ins)
                    dve.tensor_tensor(self.o8(t), nd[:, 0, 0:D], nd[:, 1, 0:D], ALU.add).then_inc(l_o.sem, 1)
                    dve.wait_ge(l_o.sem, l_o.at(0, t + 1))
            for c in range(2):
                dve.wait_ge(l_y.sem, l_y.at(0, c + 1))
                dve.wait_ge(x_biased.sem, x_biased.at(biased.index(self.sub), 1))
                xc = x[:, 4 * c:4 * c + 4, :]
                do(dve.tensor_tensor(xc, xc, bank(2 + c).rearrange("p (t d) -> p t d", d=D), ALU.add))

        def gpsimd(self, pool):
            bias_gpsimd(pool, self.sub, self.norm, "L2_attn_o")
            pool.wait_ge(l_ones.sem, l_ones.at(0, 1))
            for t in range(NT):
                pool.wait_ge(l_z.sem, l_z.at(0, t + 1))
                pool.tensor_copy(self.vx[:, t, 0:D], self.z[:, t % 2, 2 * D:3 * D]).then_inc(l_v.sem, 1)
                pool.wait_ge(l_v.sem, l_v.at(0, t + 1))

    HW = 64
    PR = H // 2
    KV = S2 + S
    KT = KV // P
    UN = B * H * 2
    c_in = counter("c_in", [6], 16)
    c_mask = counter("c_mask", [1])
    c_m_mm = counter("c_m_mm", [4])
    c_m_sb = counter("c_m_sb", [4])
    c_kvT = counter("c_kvT", [6])
    c_q_mm = counter("c_q_mm", [B * PR])
    c_q_sb = counter("c_q_sb", [B * PR])
    c_v_mm = counter("c_v_mm", [B * KT * 2])
    c_v_sb = counter("c_v_sb", [B * KT * 2])
    c_s_mm = counter("c_s_mm", [UN])
    c_max = counter("c_max", [UN])
    c_neg = counter("c_neg", [UN])
    c_exp = counter("c_exp", [UN])
    c_div = counter("c_div", [UN])
    c_tp = counter("c_tp", [UN])
    c_pT = counter("c_pT", [UN])
    c_av = counter("c_av", [B * PR])
    c_o = counter("c_o", [B * PR])
    c_y = counter("c_y", [B])
    c_y_out = counter("c_y_out", [B])

    class Latents:
        sub, name = 7, "L2_xattn"
        LAG = 3
        ksf, qsf = ks[:, :].bitcast(F32), qs[:, :].bitcast(F32)
        kvT = tmp[:, 0:B * KV].rearrange("p (b n) -> p b n", b=B)
        mqk = tmp[:, 3072:3072 + H * D].rearrange("p (h n) -> p h n", h=H)
        qT = tmp[:, 5120:6144].rearrange("p (s j q) -> p s j q", s=2, j=2)
        maskb = tmp[:, 6144:6144 + B * KV // 2].bitcast(BF16).rearrange("p (b n) -> p b n", b=B)
        v = ksf[:, 0:KT * H * HW].rearrange("p (t n) -> p t n", t=KT)
        oT = ksf[:, 6144:8192].rearrange("p (r q) -> p r q", r=PR)
        mask_raw = ksf[:, 0:TC // 4].bitcast(mybir.dt.uint8)
        pT = qsf[:, 0:6144].rearrange("p (s j t q) -> p s j t q", s=2, j=2, t=KT)
        wo = qsf[:, 6144:7168]
        wv = qsf[:, 7168:8192]
        ctx_tm = qsf[:, 0:TC].rearrange("p (t d) -> p t d", d=D)
        wqT = qsf[0:HW, 2048:4096]
        wkT = qsf[0:HW, 4096:6144]
        sc = wring[:, :, :].rearrange("p s n -> p (s n)").rearrange("p (s n) -> p s n", s=4)
        cols = r1[:, :, :].rearrange("p t e -> p (t e)")
        top, neg, tot, inv = cols[:, 0:4], cols[:, 4:8], cols[:, 8:12], cols[:, 12:16]

        def sync(self, sp):
            sp.wait_ge(x_done.sem, x_done.at(3, 1))
            for dst, src in ((self.ctx_tm, a["ctx"].rearrange("(t p) d -> p t d", p=P)), (self.wqT, a["L2_xattn_qT"]),
                             (self.wkT, a["L2_xattn_kT"]), (self.wo, a["L2_xattn_o"]), (self.wv, a["L2_xattn_v"]),
                             (self.mask_raw, a["mask_L2x"].unsqueeze(0).to_broadcast([P, TC]))):
                sp.dma_start(dst, src).then_inc(c_in.sem, 16)

        def order(self, late=False):
            for i in range(KT * 2):
                yield "v", i
            yield "q", 0
            for u in range(UN + self.LAG + 5):
                if u < UN:
                    if u % 4 == 2 and u // 4 + 1 < B * PR:
                        yield "q", u // 4 + 1
                    if not late:
                        yield "score", u
                t = u - self.LAG
                if 0 <= t < UN:
                    yield "turn", t
                if late and u < UN:
                    yield "score", u
                if t % 4 == 0 and 4 <= t <= UN:
                    g = t // 4 - 1
                    yield "sum", g
                    if g % PR == PR - 1:
                        if g // PR + 1 < B:
                            for i in range(KT * 2):
                                yield "v", (g // PR + 1) * KT * 2 + i
                        yield "y", g // PR

        def tensor(self, pe):
            pe.wait_ge(x_done.sem, x_done.at(self.sub - 1, 1))
            for half in range(2):
                norm_tensor(pe, 7 + half, src=self.ctx_tm[:, 8 * half:8 * half + 8, :],
                            after=(c_kvT.sem, c_kvT.at(0, 2)) if half else None)
            pe.wait_ge(c_in.sem, c_in.at(0, 6))
            for i in range(4):
                for j in range(4):
                    cols = slice((4 * i + j) * D, (4 * i + j + 1) * D)
                    ins = pe.matmul(bank(i, j * D, j * D + D), self.wqT[:, cols], self.wkT[:, cols], start=True, stop=True)
                ins.then_inc(c_m_mm.sem, 1)
            norm_tensor(pe, 10, after=(c_kvT.sem, c_kvT.at(0, 4)))
            pe.wait_ge(c_kvT.sem, c_kvT.at(0, 6))
            pe.wait_ge(c_m_sb.sem, c_m_sb.at(0, 4))
            for what, i in self.order():
                if what == "v":
                    b, kt, half = i // (2 * KT), i // 2 % KT, i % 2
                    if i % (2 * KT) < 2 and b:
                        pe.wait_ge(c_pT.sem, c_pT.at(0, 4 * PR * b + 1))
                    if i % (2 * KT) >= 2:
                        pe.wait_ge(c_v_sb.sem, c_v_sb.at(0, i - 1))
                    pe.matmul(bank(4 + i % 2), self.kvT[:, b, kt * P:(kt + 1) * P],
                              self.wv[:, half * 512:half * 512 + 512], start=True, stop=True).then_inc(c_v_mm.sem, 1)
                elif what == "q":
                    b = i // PR
                    if i >= 1:
                        pe.wait_ge(c_q_sb.sem, c_q_sb.at(0, i))
                    for j in range(2):
                        ins = pe.matmul(bank(7, j * S, j * S + S), self.mqk[:, 2 * (i % PR) + j, :],
                                        self.kvT[:, b, S2:KV], start=True, stop=True)
                    ins.then_inc(c_q_mm.sem, 1)
                elif what == "score":
                    g, b, j, k = i // 4, i // (4 * PR), i // 2 % 2, i % 2
                    pe.wait_ge(c_q_sb.sem, c_q_sb.at(0, g + 1))
                    if i >= 2:
                        pe.wait_ge(c_max.sem, c_max.at(0, i - 1))
                    lhs = self.qT[:, g % 2, j, k * P:(k + 1) * P]
                    at = i % 2 * 2
                    pe.matmul(bank(at), lhs, self.kvT[:, b, 0:512], start=True, stop=True)
                    pe.matmul(bank(at + 1, 0, S), lhs, self.kvT[:, b, 512:KV],
                              start=True, stop=True).then_inc(c_s_mm.sem, 1)
                elif what == "turn":
                    pe.wait_ge(c_div.sem, c_div.at(0, i + 1))
                    if i:
                        pe.wait_ge(c_pT.sem, c_pT.at(0, i))
                    if i == 0 or i % (4 * PR) == 1 and i > 1:
                        pe.wait_ge(c_v_sb.sem, c_v_sb.at(0, (i // (4 * PR) + 1) * 2 * KT))
                    for t in range(KT):
                        ins = pe.transpose(bank(4 + t // 4, t % 4 * P, t % 4 * P + P), self.sc[:, i % 4, t * P:(t + 1) * P],
                                           ident[:, :])
                    ins.then_inc(c_tp.sem, 1)
                elif what == "sum":
                    pe.wait_ge(c_pT.sem, c_pT.at(0, 4 * i + 4))
                    if i:
                        pe.wait_ge(c_o.sem, c_o.at(0, i))
                    r = i % PR
                    for t in range(KT):
                        for j in range(2):
                            ins = pe.matmul(ps[HW * j:HW * j + HW, 6, 0:S], self.v[:, t, (2 * r + j) * HW:(2 * r + j + 1) * HW],
                                            self.pT[:, i % 2, j, t, :], start=(t == 0), stop=(t == KT - 1),
                                            skip_group_check=True)
                    ins.then_inc(c_av.sem, 1)
                else:
                    b = i
                    pe.wait_ge(c_o.sem, c_o.at(0, PR * (b + 1)))
                    for k in range(2):
                        for r in range(PR):
                            ins = pe.matmul(bank(6, k * D, k * D + D), self.oT[:, r, k * P:(k + 1) * P],
                                            self.wo[:, r * D:(r + 1) * D], start=(r == 0), stop=(r == PR - 1))
                    ins.then_inc(c_y.sem, 1)
                    pe.wait_ge(c_y_out.sem, c_y_out.at(0, b + 1))

        def scalar(self, act):
            for half in range(2):
                for c in range(2):
                    act.wait_ge(ln_tp.sem, ln_tp.at(7 + half, c + 1))
                    act.copy(self.kvT[:, 2 * half + c, 0:S2], bank(6 + c)).then_inc(c_kvT.sem, 1)
            for i in range(4):
                act.wait_ge(c_m_mm.sem, c_m_mm.at(0, i + 1))
                act.mul(self.mqk[:, 4 * i:4 * i + 4, :].rearrange("p h n -> p (h n)"), bank(i),
                        float(HW) ** -0.5).then_inc(c_m_sb.sem, 1)
            for c in range(2):
                act.wait_ge(ln_tp.sem, ln_tp.at(10, c + 1))
                act.copy(self.kvT[:, 2 * c:2 * c + 2, S2:KV],
                         bank(6 + c).rearrange("p (b n) -> p b n", b=2)).then_inc(c_kvT.sem, 1)
            for what, i in self.order(late=True):
                if what == "v":
                    b, kt, half = i // (2 * KT), i // 2 % KT, i % 2
                    act.wait_ge(c_v_mm.sem, c_v_mm.at(0, i + 1))
                    if i % (2 * KT) == 0 and b:
                        act.wait_ge(c_av.sem, c_av.at(0, PR * b))
                    act.copy(self.v[:, kt, half * 512:half * 512 + 512], bank(4 + i % 2)).then_inc(c_v_sb.sem, 1)
                elif what == "q":
                    act.wait_ge(c_q_mm.sem, c_q_mm.at(0, i + 1))
                    if i >= 2:
                        act.wait_ge(c_s_mm.sem, c_s_mm.at(0, 4 * (i - 1)))
                    act.copy(self.qT[:, i % 2, :, :], bank(7).rearrange("p (j q) -> p j q", j=2)).then_inc(c_q_sb.sem, 1)
                elif what == "score":
                    act.wait_ge(c_neg.sem, c_neg.at(0, i + 1))
                    act.activation(self.sc[:, i % 4, :], self.sc[:, i % 4, :], ACT.Exp, bias=self.neg[:, i % 4:i % 4 + 1],
                                   accum_out=self.tot[:, i % 4:i % 4 + 1]).then_inc(c_exp.sem, 1)
                elif what == "turn":
                    g, j, k = i // 4, i // 2 % 2, i % 2
                    act.wait_ge(c_tp.sem, c_tp.at(0, i + 1))
                    if i % 4 == 0 and g >= 2:
                        act.wait_ge(c_av.sem, c_av.at(0, g - 1))
                    act.copy(self.pT[:, g % 2, j, :, k * P:(k + 1) * P],
                             ps[:, 4:6, :].rearrange("p b n -> p (b n)")[:, 0:KV].rearrange("p (t n) -> p t n", n=P)
                             ).then_inc(c_pT.sem, 1)
                elif what == "sum":
                    act.wait_ge(c_av.sem, c_av.at(0, i + 1))
                    if i % PR == 0 and i:
                        act.wait_ge(c_y.sem, c_y.at(0, i // PR))
                    act.copy(self.oT[:, i % PR, :], bank(6, 0, S)).then_inc(c_o.sem, 1)

        def context_vector(self, dve):
            dve.wait_ge(c_in.sem, c_in.at(0, 6))
            for half in range(2):
                c = self.ctx_tm[:, 8 * half:8 * half + 8, :]
                norm_vector(dve, 7 + half, src=c, dst=c, affine=("L2_xattn_gm", "L2_xattn_bm"))

        def context_gpsimd(self, pool):
            for n in (7, 8):
                norm_gpsimd(pool, n)

        def vector(self, dve):
            do = lambda ins: link(dve, dchain, ins)
            do(dve.memset(self.maskb[:, :, S2:KV], 0.0))
            dve.tensor_scalar(self.maskb[:, :, 0:S2], self.mask_raw.rearrange("p (b n) -> p b n", b=B), 0.0, -BIG,
                              ALU.is_equal, ALU.mult).then_inc(c_mask.sem, 1)
            norm_vector(dve, 9)
            dve.wait_ge(ln_h.sem, ln_h.at(9, 1))
            norm_vector(dve, 10, src=h, affine=("L2_xattn_gl", "L2_xattn_bl"))
            dve.wait_ge(c_mask.sem, c_mask.at(0, 1))
            for what, i in self.order():
                if what == "score":
                    b, s = i // (4 * PR), i % 4
                    dve.wait_ge(c_s_mm.sem, c_s_mm.at(0, i + 1))
                    if i >= 4:
                        dve.wait_ge(c_tp.sem, c_tp.at(0, i - 3))
                        dve.wait_ge(c_neg.sem, c_neg.at(0, i - 3))
                    src = ps[:, i % 2 * 2:i % 2 * 2 + 2, :].rearrange("p b n -> p (b n)")[:, 0:KV]
                    dve.tensor_tensor_reduce(self.sc[:, s, :], src, self.maskb[:, b, :], 1.0, -3.0e38,
                                             ALU.add, ALU.max, self.top[:, s:s + 1]).then_inc(c_max.sem, 1)
                    dve.wait_ge(c_max.sem, c_max.at(0, i + 1))
                    dve.tensor_scalar(self.neg[:, s:s + 1], self.top[:, s:s + 1], -1.0, None,
                                      ALU.mult).then_inc(c_neg.sem, 1)
                    if i:
                        self.div_vector(dve, i - 1)
                    if i == UN - 1:
                        self.div_vector(dve, i)
                elif what == "y":
                    b = i
                    dve.wait_ge(c_y.sem, c_y.at(0, b + 1))
                    xb = x[:, 2 * b:2 * b + 2, :]
                    dve.tensor_tensor(xb, xb, bank(6, 0, S).rearrange("p (t d) -> p t d", d=D),
                                      ALU.add).then_inc(c_y_out.sem, 1)
            dve.wait_ge(c_y_out.sem, c_y_out.at(0, B))

        def div_vector(self, dve, i):
            dve.wait_ge(c_exp.sem, c_exp.at(0, i + 1))
            if i >= 4:
                dve.wait_ge(c_div.sem, c_div.at(0, i - 3))
            link(dve, dchain, dve.reciprocal(self.inv[:, i % 4:i % 4 + 1], self.tot[:, i % 4:i % 4 + 1]))
            dve.tensor_scalar(self.sc[:, i % 4, :], self.sc[:, i % 4, :], self.inv[:, i % 4:i % 4 + 1], None,
                              ALU.mult).then_inc(c_div.sem, 1)

        def gpsimd(self, pool):
            for n in (9, 10):
                norm_gpsimd(pool, n)
    rows_again = counter("rows_again", [1])

    f_in = counter("f_in", [2], 16)
    f_abs = counter("f_abs", [2])
    f_tot = counter("f_tot", [2])
    f_wq = counter("f_wq", [2])
    f_q = counter("f_q", [NT])
    f_tp = counter("f_tp", [2])
    f_qT = counter("f_qT", [2])
    f_h = counter("f_h", [NT])
    f_z = counter("f_z", [NT])
    f_g = counter("f_g", [NT])
    f_hq = counter("f_hq", [NT])
    f_htp = counter("f_htp", [NT])
    f_hT = counter("f_hT", [NT])
    f_y = counter("f_y", [NT])
    f_done = counter("f_done", [NT])
    FH = 4 * D
    ROUND = 1.5 * 2.0 ** 23

    class Ternary:
        sub, norm, name = 11, 14, "L3_ffn"
        w1 = tmp[:, 0:FH]
        w2 = tmp[:, FH:2 * FH]
        wtmp = tmp[:, 1024:1536]
        wint = tmp[:, 1536:2048].bitcast(BF16).rearrange("p (w n) -> p w n", w=2)
        z = tmp[:, 2048:3072].rearrange("p (s n) -> p s n", s=2)
        zi = tmp[:, 3072:3584].bitcast(BF16).rearrange("p (s n) -> p s n", s=2)
        ziT = tmp[:, 3584:4096].bitcast(BF16).rearrange("p (s n) -> p s n", s=2)
        hi = tmp[:, 4096:4608].bitcast(BF16).rearrange("p (t n) -> p t n", t=NT)
        hiT = tmp[:, 4608:5120].bitcast(BF16)
        y = tmp[:, 5120:5376].rearrange("p (s n) -> p s n", s=2)
        c = r1[:, :, :].rearrange("p t e -> p (t e)")
        ones = tmp[:, 5376:5504]

        def sync(self, sp):
            sp.wait_ge(x_done.sem, x_done.at(self.sub - 1, 1))
            sp.dma_start(self.w1, a["L3_ffn_w1"]).then_inc(f_in.sem, 16)
            sp.dma_start(self.w2, a["L3_ffn_w2"]).then_inc(f_in.sem, 16)

        def gpsimd(self, pool):
            pass

        def col(self, i, n=1):
            return self.c[:, i:i + n]

        def tensor(self, pe):
            for k in range(2):
                pe.wait_ge(f_abs.sem, f_abs.at(0, k + 1))
                pe.matmul(bank(0, k, k + 1), self.ones, self.col(k), start=True, stop=True).then_inc(f_tot.sem, 1)
                pe.wait_ge(f_wq.sem, f_wq.at(0, k + 1))
            for t in range(NT):
                pe.wait_ge(f_q.sem, f_q.at(0, t + 1))
                ins = pe.transpose(bank(6).bitcast(BF16)[:, t * P:(t + 1) * P], self.hi[:, t, :], identb[:, :])
                if t % 4 == 3:
                    ins.then_inc(f_tp.sem, 1)
                    pe.wait_ge(f_qT.sem, f_qT.at(0, t // 4 + 1))
            for t in range(NT + 2):
                if t < NT:
                    if t >= 2:
                        pe.wait_ge(f_z.sem, f_z.at(0, t - 1))
                    pe.matmul(bank(t % 2), self.hiT[:, t * P:(t + 1) * P], self.wint[:, 0, :],
                              start=True, stop=True).then_inc(f_h.sem, 1)
                if 0 <= t - 1 < NT:
                    q = t - 1
                    pe.wait_ge(f_hq.sem, f_hq.at(0, q + 1))
                    if q >= 2:
                        pe.wait_ge(f_hT.sem, f_hT.at(0, q - 1))
                    for j in range(4):
                        ins = pe.transpose(bank(2 + q % 2).bitcast(BF16)[:, j * P:(j + 1) * P],
                                           self.zi[:, q % 2, j * P:(j + 1) * P], identb[:, :])
                    ins.then_inc(f_htp.sem, 1)
                if 0 <= t - 2:
                    q = t - 2
                    pe.wait_ge(f_hT.sem, f_hT.at(0, q + 1))
                    if q >= 2:
                        pe.wait_ge(f_done.sem, f_done.at(0, q - 1))
                    for j in range(4):
                        ins = pe.matmul(bank(4 + q % 2, 0, D), self.ziT[:, q % 2, j * P:(j + 1) * P],
                                        self.wint[:, 1, j * D:(j + 1) * D], start=(j == 0), stop=(j == 3))
                    ins.then_inc(f_y.sem, 1)

        def scalar(self, act):
            for c in range(2):
                act.wait_ge(f_tp.sem, f_tp.at(0, c + 1))
                act.copy(self.hiT[:, c * 512:c * 512 + 512],
                         bank(6).bitcast(BF16)[:, c * 512:c * 512 + 512]).then_inc(f_qT.sem, 1)
            for t in range(NT + 1):
                if t < NT:
                    act.wait_ge(f_z.sem, f_z.at(0, t + 1))
                    act.activation(self.z[:, t % 2, :], self.z[:, t % 2, :], ACT.Gelu).then_inc(f_g.sem, 1)
                if t:
                    q = t - 1
                    act.wait_ge(f_htp.sem, f_htp.at(0, q + 1))
                    if q >= 2:
                        act.wait_ge(f_y.sem, f_y.at(0, q - 1))
                    act.copy(self.ziT[:, q % 2, :], bank(2 + q % 2).bitcast(BF16)[:, 0:FH]).then_inc(f_hT.sem, 1)

        def quantize(self, do, dve, src, out, cols):
            big, inv, scale = cols
            do(dve.tensor_reduce(big, src, AX.X, ALU.max, apply_absolute_value=True))
            do(dve.tensor_scalar(big, big, EPS, None, ALU.max))
            do(dve.reciprocal(inv, big))
            do(dve.tensor_scalar(inv, inv, 127.0, None, ALU.mult))
            do(dve.tensor_scalar(scale, big, 1.0 / 127.0, None, ALU.mult))
            do(dve.tensor_scalar(src, src, inv, ROUND, ALU.mult, ALU.add))
            return dve.tensor_scalar(out, src, ROUND, None, ALU.subtract)

        def vector(self, dve):
            do = lambda ins: link(dve, dchain, ins)
            do(dve.memset(self.ones, 1.0))
            dve.wait_ge(f_in.sem, f_in.at(0, 2))
            for k, wgt in enumerate((self.w1, self.w2)):
                dve.tensor_reduce(self.col(k), wgt, AX.X, ALU.add, apply_absolute_value=True).then_inc(f_abs.sem, 1)
                dve.wait_ge(f_tot.sem, f_tot.at(0, k + 1))
                s, inv = self.col(2 + k), self.col(4)
                do(dve.tensor_scalar(s, bank(0, k, k + 1), 1.0 / (D * FH), EPS, ALU.mult, ALU.max))
                do(dve.reciprocal(inv, s))
                do(dve.tensor_scalar(self.wtmp, wgt, inv, ROUND, ALU.mult, ALU.add))
                do(dve.tensor_scalar(self.wtmp, self.wtmp, ROUND, 1.0, ALU.subtract, ALU.min))
                dve.tensor_scalar(self.wint[:, k, :], self.wtmp, -1.0, None, ALU.max).then_inc(f_wq.sem, 1)
                dve.wait_ge(f_wq.sem, f_wq.at(0, k + 1))
            for t in range(NT):
                self.quantize(do, dve, h[:, t, :], self.hi[:, t, :],
                              (self.col(5), self.col(6), self.col(16 + t))).then_inc(f_q.sem, 1)
                dve.wait_ge(f_q.sem, f_q.at(0, t + 1))
                do(dve.tensor_tensor(self.col(16 + t), self.col(16 + t), self.col(2), ALU.mult))
            for t in range(NT + 2):
                if t < NT:
                    dve.wait_ge(f_h.sem, f_h.at(0, t + 1))
                    dve.tensor_scalar(self.z[:, t % 2, :], bank(t % 2), self.col(16 + t), None,
                                      ALU.mult).then_inc(f_z.sem, 1)
                if 0 <= t - 1 < NT:
                    q = t - 1
                    dve.wait_ge(f_g.sem, f_g.at(0, q + 1))
                    if q >= 2:
                        dve.wait_ge(f_htp.sem, f_htp.at(0, q - 1))
                    self.quantize(do, dve, self.z[:, q % 2, :], self.zi[:, q % 2, :],
                                  (self.col(5), self.col(6), self.col(32 + q))).then_inc(f_hq.sem, 1)
                    dve.wait_ge(f_hq.sem, f_hq.at(0, q + 1))
                    do(dve.tensor_tensor(self.col(32 + q), self.col(32 + q), self.col(3), ALU.mult))
                if 0 <= t - 2:
                    q = t - 2
                    dve.wait_ge(f_y.sem, f_y.at(0, q + 1))
                    dve.scalar_tensor_tensor(out=x[:, q, :], in0=bank(4 + q % 2, 0, D), scalar=self.col(32 + q),
                                             in1=x[:, q, :], op0=ALU.mult, op1=ALU.add).then_inc(f_done.sem, 1)
            dve.wait_ge(f_done.sem, f_done.at(0, NT))

    clip_sb = wring[:, :, :].rearrange("p s n -> p (s n)")[:, 0:12 * P].rearrange("p (s n) -> p s n", s=4)
    tri = sb("tri", [P, P])
    lat = wring[0:64, 0, 0:T]
    y_out = counter("y_out", [B] * len(ATTN))

    attn = [Attention(0, 0), Attention(1, 1), Attention(2, 3), Attention(3, 12), Attention(4, 13)]
    subs = {t.sub: t for t in attn}
    mixtures = {t.sub: t for t in (Mixture(0, 2), Mixture(1, 5), Mixture(2, 11))}
    others = {t.sub: t for t in (Gathered(), Linear(), Latents(), Ternary())}
    norm_of = {s: (s if s < 8 else s + 3) for s in range(N_SUB)}
    n_loads = [0]

    block = ctx.enter_context(nc.Block())

    @block.sync
    def _(sp):
        first = W_OF["L0_attn_o"] * D + D
        rows = a["brow"].unsqueeze(0).to_broadcast([P, len(R_OF), D])
        for dst, src in ((x[:, :, :], a["x"].rearrange("(t p) d -> p t d", p=P)), (ident[:, :], a["ident"]),
                         (w[:, 0:first], a["w"][:, 0:first]), (bcol[:, :], a["bcol"]), (brow[:, 0:2, :], rows[:, 0:2, :])):
            sp.dma_start(dst, src).then_inc(first_in, 16)
        for dst, src in ((w[:, first:], a["w"][:, first:]), (brow[:, 2:, :], rows[:, 2:, :]),
                         (ctxT[:, :], a["ctxT"]), (tri[:, :], a["tri"]),
                         (mrow_raw[:, :], a["mask_row"]), (gatew[:, :], a["gates"]),
                         (b2r[:, :], a["b2"]), (down[:, :], a["order"]), (bmask[:, :], a["bmask"]), (vmask[:, :], a["vmask"]),
                         (m3a_raw[:, :, :, :], a["mask_L3a"].rearrange("w (t p) k -> p w t k", p=P)),
                         (m3x_raw[:, 0:2 * S2].rearrange("p (t k) -> p t k", t=2), a["mask_L3x"].rearrange("(t p) k -> p t k", p=P)),
                         (m3x_raw[:, 2 * S2:].rearrange("p (t k) -> p t k", t=4), a["mask_L3xT"].rearrange("(t p) k -> p t k", p=P))):
            sp.dma_start(dst, src).then_inc(loaded, 16)
        for s in range(N_SUB_RUN):
            if s == 1:
                sp.wait_ge(x_done.sem, x_done.at(0, 1))
                sp.dma_start(scr_x.rearrange("(p k) d -> p (k d)", p=P),
                             ks[:, :].bitcast(F32)[:, 0:SLOTS]).then_inc(written, 16)
                sp.wait_ge(written, 16)
            if s in subs:
                subs[s].stack_sync(sp)
                subs[s].maxima_sync(sp)
            elif s in mixtures:
                mixtures[s].sync(sp)
            elif s in others and s != 7:
                others[s].sync(sp)
                if s == 4:
                    others[7].sync(sp)
        sp.wait_ge(x_done.sem, x_done.at(N_SUB_RUN - 1, 1))
        sp.dma_start(a["out"].rearrange("(t p) d -> p t d", p=P), x[:, :, :]).then_inc(written, 16)
        sp.wait_ge(written, 32)

    LOADED = 16 * 13

    @block.gpsimd
    def _(pool):
        link(pool, pchain, pool.memset(mhalf[:, :], -0.5))
        link(pool, pchain, pool.memset(vaug[:, :, :, :, 8:32], 0.0))
        link(pool, pchain, pool.memset(vaug[:, :, :, :, 8:16], 1.0))
        for s in range(N_SUB_RUN):
            if s != 7:
                norm_gpsimd(pool, norm_of[s])
            if s == 0:
                link(pool, pchain, pool.memset(ks[MAXROW:MAXROW + 3, :].bitcast(F32), TWO_ONES))
                pool.engine_nop().then_inc(consts, 1)
                pool.wait_ge(first_in, 16 * 5)
            if s == 1:
                pool.wait_ge(loaded, LOADED)
            if s in subs:
                t = subs[s]
                if t.bias:
                    bias_gpsimd(pool, s, norm_of[s], f"{t.name}_o")
                if t.n:
                    pool.wait_ge(b_mm.sem, b_mm.at(t.n - 1, G * units[t.n - 1]))
                    if t.n in (1, 2):
                        link(pool, pchain, pool.memset(qs[MASKROW:MASKROW + 1, :].bitcast(F32),
                                                       TWO_ONES if t.n == 1 else 0.0))
                    pool.memset(qs[MAXROW:MAXROW + 32, :].bitcast(F32), 0.0).then_inc(q_rows_clear.sem, 1)
                    pool.wait_ge(q_rows_clear.sem, q_rows_clear.at(t.n, 1))
                t.gpsimd(pool)
            elif s in mixtures:
                mixtures[s].gpsimd(pool)
            elif s in others:
                others[s].gpsimd(pool)

    def masks_vector(dve):
        dve.wait_ge(loaded, LOADED)
        dve.tensor_scalar(mrow[:, :], mrow_raw[:, :], -BIG, None, ALU.mult)
        dve.tensor_scalar(m3a[:, :, :], m3a_raw[:, :, :, :].rearrange("p w t k -> p w (t k)"), 0.0, -BIG,
                          ALU.is_equal, ALU.mult)
        dve.tensor_scalar(m3x[:, :, :], m3x_raw.rearrange("p (w k) -> p w k", w=2), 0.0, -BIG,
                          ALU.is_equal, ALU.mult)
        dve.tensor_copy(trib[:, :], tri[:, :])
        link(dve, dchain, dve.memset(onesb[:, :], 1.0))

    @block.vector
    def _(dve):
        link(dve, dchain, dve.memset(ks[:, :].bitcast(F32), 0.0))
        dve.wait_ge(first_in, 16 * 5)
        dve.tensor_copy(identb[:, :], ident[:, :]).then_inc(consts, 1)
        for s in range(N_SUB_RUN):
            if s != 7:
                norm_vector(dve, norm_of[s])
            if s in subs:
                subs[s].project_vector(dve)
                if s == 0:
                    masks_vector(dve)
                subs[s].vector(dve)
                dve.wait_ge(y_out.sem, y_out.at(subs[s].n, B))
            elif s in mixtures:
                mixtures[s].vector(dve)
            elif s in others:
                others[s].vector(dve)
            dve.engine_nop().then_inc(x_done.sem, 1)

    @block.scalar
    def _(act):
        act.wait_ge(first_in, 16 * 5)
        act.mul(qs[:, :].bitcast(F32).rearrange("p (k n) -> p k n", n=P),
                ident[:, :].unsqueeze(1).to_broadcast([P, G * 4 * S // 2 // P, P]), 0.0).then_inc(consts, 1)
        for s in range(N_SUB_RUN):
            if s not in (7, 11):
                norm_scalar(act, norm_of[s])
            if s in subs:
                subs[s].project_scalar(act)
                subs[s].scalar(act)
            elif s in mixtures:
                mixtures[s].scalar(act)
            elif s in others:
                others[s].scalar(act)

    @block.tensor
    def _(pe):
        pe.wait_ge(first_in, 16 * 5)
        for s in range(N_SUB_RUN):
            if s not in (7, 11):
                norm_tensor(pe, norm_of[s])
            if s in subs:
                subs[s].project_tensor(pe)
                if s == 0:
                    pe.wait_ge(consts, CONSTS)
                subs[s].tensor(pe)
            elif s in mixtures:
                mixtures[s].tensor(pe)
            elif s in others:
                others[s].tensor(pe)


CONSTS = 3
N_SUB_RUN = N_SUB


def layout(i):
    f = {}
    g = {k: np.asarray(v) for k, v in i.items()}
    f["x"] = g["x"].reshape(T, D)
    f["ident"] = np.eye(P, dtype=np.float32)
    wp = np.zeros((P, W_COLS * D), np.float32)

    narrow = {f"{c['name']}_{n}" for c in ATTN for n in "qk"}

    def turned(name, m):
        return m.reshape(*m.shape[:-1], H, HD).swapaxes(-1, -2).reshape(m.shape) if name in narrow else m

    def put(name, m, rows=slice(0, P)):
        m = turned(name, m)
        wp[rows, W_OF[name] * D:W_OF[name] * D + m.shape[1]] = m

    def tall(m):
        return m.reshape(m.shape[0], -1, P, D).transpose(0, 2, 1, 3).reshape(m.shape[0], P, -1)

    for k, nm in enumerate("qkv"):
        put(f"L0_attn_{nm}", g["L0_attn_W_qkv"][:, k * D:(k + 1) * D])
        put(f"L1_attn_{nm}", g["L1_attn_Wqkv"][k * D:(k + 1) * D].T)
        put(f"L3_xattn_{nm}", g[f"L3_xattn_W{nm}"].T)
        put(f"L1_xattn_{nm}", g[f"L1_xattn_W{nm}"].T)
        put(f"L2_attn_{nm}", g[f"L2_attn_W{nm}"])
    put("L0_attn_o", g["L0_attn_W_proj"])
    put("L0_xattn_q", g["L0_xattn_q_w"])
    put("L0_xattn_k", g["L0_xattn_kv_w"][:, :D])
    put("L0_xattn_v", g["L0_xattn_kv_w"][:, D:])
    put("L0_xattn_o", g["L0_xattn_proj_w"])
    put("L1_attn_o", g["L1_attn_Wout"].T)
    put("L3_down", np.concatenate([g["L3_attn_Wq_down"].T, g["L3_attn_Wkv_down"].T], 1))
    put("L3_attn_q", g["L3_attn_Wq_up"].T, slice(0, 32))
    put("L3_attn_k", g["L3_attn_Wk_up"].T, slice(32, 64))
    put("L3_attn_v", g["L3_attn_Wv_up"].T, slice(32, 64))
    put("L3_attn_o", g["L3_attn_Wout"].T)
    put("L3_xattn_o", g["L3_xattn_Wo"].T)
    put("L1_xattn_o", g["L1_xattn_Wo"].T)
    put("L2_attn_o", g["L2_attn_Wo"])
    f["w"] = wp
    biases = dict(zip(("L0_attn_q", "L0_attn_k", "L0_attn_v"), g["L0_attn_b_qkv"].reshape(3, D)),
                  L0_attn_o=g["L0_attn_b_proj"], L0_xattn_q=g["L0_xattn_q_b"],
                  L0_xattn_k=g["L0_xattn_kv_b"][:D], L0_xattn_v=g["L0_xattn_kv_b"][D:],
                  L0_xattn_o=g["L0_xattn_proj_b"], zero=np.zeros(D, np.float32))
    for n in ("L1_xattn", "L2_attn", "L3_xattn"):
        for c in "qkvo":
            biases[f"{n}_{c}"] = g[f"{n}_b{c}"]
    for c in ("gm", "bm", "gl", "bl"):
        biases[f"L2_xattn_{c}"] = g[f"L2_xattn_{c}"]
    f["bcol"] = np.stack([turned(n, biases[n]) for n in C_OF], 1)
    f["brow"] = np.stack([biases[n] for n in R_OF])
    f["ctxT"] = g["ctx_1024"].reshape(TC, D).T
    f["tri"] = np.triu(np.ones((P, P), np.float32))
    f["mask_row"] = g["mask_BxS2_bk0"]
    m = g["L3_attn_mask"].reshape(S, S)
    f["mask_L3a"] = np.stack([m, m.T])
    m = g["mask_1x1xSxS2_if1"].reshape(S, S2)
    f["mask_L3x"], f["mask_L3xT"] = m, m.T
    f["ctxT_by_head"] = g["ctx_1024"].reshape(B, S2 // H, H, D).transpose(3, 0, 2, 1).reshape(D, TC)
    f["bmask"] = np.repeat(np.eye(H, dtype=np.float32), HD, 0)
    f["vmask"] = np.kron(np.eye(4, dtype=np.float32), np.ones((S2 // H, HD), np.float32))
    f["kv_mask"] = np.concatenate([np.repeat(f["bmask"], HD, 1), f["bmask"]], 1)
    angle = (np.float32(np.pi / 2) * np.arange(1, S + 1, dtype=np.float32) / np.float32(S)).astype(np.float64)
    sc = np.stack([np.sin(angle), np.cos(angle), -np.sin(angle), -np.cos(angle)], 1).astype(np.float32)
    f["trig"] = sc.reshape(2, P, 4).transpose(1, 0, 2).reshape(P, 8)
    f["ctx"] = g["ctx_1024"].reshape(TC, D)
    f["mask_L2x"] = g["mask_BxS2_bf1"].reshape(TC)
    for n in "qk":
        f[f"L2_xattn_{n}T"] = g[f"L2_xattn_W{n}"].reshape(D, H, 64).transpose(2, 1, 0).reshape(64, H * D)
    f["L2_xattn_v"] = g["L2_xattn_Wv"]
    f["L2_xattn_o"] = tall(g["L2_xattn_Wo"][None])[0]
    f["L3_ffn_w1"] = g["L3_ffn_w1"].T
    f["L3_ffn_w2"] = tall(g["L3_ffn_w2"].T[None])[0]
    f["gates"] = np.concatenate([g["L0_ffn_gate_w"], g["L1_ffn_gate_w"].T, g["L2_ffn_gate_w"].T], 1)
    f["order"] = np.concatenate([np.tile(np.arange(32, 0, -1), (P, 1)), np.arange(P)[:, None]], 1).astype(np.float32)
    f["b2"] = g["L2_ffn_b2"]
    routed = [g[f"L0_ffn_routed_{n}_w"] for n in ("gate", "up", "down")]
    shared = [g[f"L0_ffn_shared_{n}_w"][None] for n in ("gate", "up", "down")]
    gate, up, last = (np.concatenate(pair) for pair in zip(shared, routed))
    f["L0_ffn_w"] = np.concatenate([gate, up, tall(last)], 2)
    f["L1_ffn_w"] = np.concatenate([g["L1_ffn_w1"].transpose(0, 2, 1), g["L1_ffn_w3"].transpose(0, 2, 1),
                                    tall(g["L1_ffn_w2"].transpose(0, 2, 1))], 2)
    f["L2_ffn_w"] = np.concatenate([g["L2_ffn_w1"], tall(g["L2_ffn_w2"]),
                                    g["L2_ffn_b1"].reshape(8, 4, P).transpose(0, 2, 1)], 2)
    return {k: np.ascontiguousarray(v) for k, v in f.items()}


def kernel(**inputs):
    import concourse.bacc as bacc
    from concourse.bass_utils import run_bass_kernel_spmd

    nc = bacc.Bacc("TRN2", target_bir_lowering=False, num_devices=1)
    arrays = layout(inputs)
    a = {n: nc.dram_tensor(f"in_{n}", v.shape, mybir.dt.from_np(v.dtype), kind="ExternalInput").ap()
         for n, v in arrays.items()}
    a["out"] = nc.dram_tensor("out", (T, D), F32, kind="ExternalOutput").ap()
    with ExitStack() as ctx:
        program(nc, a, ctx)
    r = run_bass_kernel_spmd(nc, [{f"in_{n}": v for n, v in arrays.items()}], core_ids=[0])
    return r.results[0]["out"].reshape(B, S, D)
```
